# Optimizing a Trainium2 kernel written in Bass

```python
import numpy as np
import jax
import jax.numpy as jnp

def _softmax(x, axis=-1):
    return jax.nn.softmax(x, axis=axis)

def _gelu(x):
    return jax.nn.gelu(x, approximate=True)

def _silu(x):
    return jax.nn.silu(x)

def _sigmoid(x):
    return jax.nn.sigmoid(x)

def _layernorm(x, axis=-1, eps=1e-05):
    m = jnp.mean(x, axis=axis, keepdims=True)
    v = jnp.var(x, axis=axis, keepdims=True)
    return (x - m) / jnp.sqrt(v + eps)

def _scatter_add(tgt, idx, src, axis=0):
    return tgt.at[idx].add(src)

def _segment_sum(src, seg, n):
    return jax.ops.segment_sum(src, seg, n)
kernel_name = 'mk_perceiver_d4_seqx_r4_5cd8f8'

def setup_inputs(seed: int=0):
    np.random.seed(seed)
    _w = jnp.asarray

    def _rec_inputs():
        import jax
        import jax.numpy as jnp
        _rk = jax.random.key(seed)
        x = -0.0002928 + 1 * jax.random.normal(jax.random.fold_in(_rk, 1), (8, 64, 256), jnp.float32)
        _lenS = 64 - jax.random.randint(jax.random.fold_in(_rk, 7), (8,), 0, max(1, 64 // 4) + 1, jnp.int32)
        _lenS2 = 1024 - jax.random.randint(jax.random.fold_in(_rk, 8), (8,), 0, max(1, 1024 // 4) + 1, jnp.int32)
        _ctx_1024P = jax.random.normal(jax.random.fold_in(_rk, 11), (8, 16, 256), jnp.float32)
        _ctx_1024c = jax.random.dirichlet(jax.random.fold_in(_rk, 511), 0.3 * jnp.ones((16,), jnp.float32), (8, 1024))
        _ctx_1024t = jnp.einsum('bsk,bkd->bsd', _ctx_1024c, _ctx_1024P)
        _ctx_1024t = _ctx_1024t * jax.lax.rsqrt(jnp.mean(jnp.square(_ctx_1024t)) + 1e-12) * 0.953939
        ctx_1024 = -1.39393e-06 + 0.999914 * (_ctx_1024t + 0.3 * jax.random.normal(jax.random.fold_in(_rk, 611), (8, 1024, 256), jnp.float32))
        _validS = jnp.arange(64)[None, :] < _lenS[:, None]
        _validS2 = jnp.arange(1024)[None, :] < _lenS2[:, None]
        _causal = jnp.tril(jnp.ones((64, 64), dtype=bool))
        mask_BxS2_bf1 = jnp.ones((8, 1024), dtype=bool)
        mask_1x1xSxS2_ff0 = jnp.where(jnp.ones((1, 1, 64, 1024), dtype=bool), 0.0, -1000000000.0).astype(jnp.float32)
        return (x, ctx_1024, mask_BxS2_bf1, mask_1x1xSxS2_ff0)
    x, ctx_1024, mask_BxS2_bf1, mask_1x1xSxS2_ff0 = _rec_inputs()

    def _L0_xattn_setup():
        import jax, jax.numpy as jnp
        import numpy as np
        EMBED_DIM = 256
        NUM_HEADS = 16
        HEAD_DIM = EMBED_DIM // NUM_HEADS
        key = jax.random.key(seed)
        ks = jax.random.split(key, 7)
        B, S, E = (2, 512, EMBED_DIM)
        bound = float(np.sqrt(6.0 / (E + E)))
        mkw = lambda k: jax.random.uniform(k, (E, E), jnp.float32, -bound, bound)
        return {'query': jax.random.normal(ks[0], (B, S, E), jnp.float32), 'key': jax.random.normal(ks[1], (B, S, E), jnp.float32), 'value': jax.random.normal(ks[2], (B, S, E), jnp.float32), 'Wq': mkw(ks[3]), 'Wk': mkw(ks[4]), 'Wv': mkw(ks[5]), 'Wo': mkw(ks[6])}
    _L0_xattn_all = _L0_xattn_setup()
    _L0_xattn_in = {k: v for k, v in _L0_xattn_all.items() if k in ('Wq', 'Wk', 'Wv', 'Wo')}
    del _L0_xattn_all

    def _L0_attn_setup():
        import jax, jax.numpy as jnp
        import numpy as np
        D_MODEL = 256
        D_STATE = 16
        EXPAND = 2
        D_INNER = D_MODEL * EXPAND
        DT_RANK = D_MODEL // 16

        def _ssm_forward(u, W_in, b_in, W_x, b_x, W_dt, b_dt, A_log, D, W_out, b_out):
            B, T, _ = u.shape
            u_inner = u @ W_in.T + b_in
            x, z = jnp.split(u_inner, 2, axis=-1)
            dbc = x @ W_x.T + b_x
            delta_raw = dbc[..., :DT_RANK]
            B_ssm = dbc[..., DT_RANK:DT_RANK + D_STATE]
            C_ssm = dbc[..., DT_RANK + D_STATE:]
            delta = jax.nn.softplus(delta_raw @ W_dt.T + b_dt)
            A = -jnp.exp(A_log)

            def step(h, xs):
                dt_t, x_t, Bt, Ct = xs
                dA = jnp.exp(dt_t[..., None] * A)
                dB = dt_t[..., None] * Bt[:, None, :]
                h = h * dA + x_t[..., None] * dB
                y_t = jnp.einsum('bdn,bn->bd', h, Ct)
                return (h, y_t)
            h0 = jnp.zeros((B, D_INNER, D_STATE), u.dtype)
            xs = (jnp.swapaxes(delta, 0, 1), jnp.swapaxes(x, 0, 1), jnp.swapaxes(B_ssm, 0, 1), jnp.swapaxes(C_ssm, 0, 1))
            _, y = jax.lax.scan(step, h0, xs)
            y = jnp.swapaxes(y, 0, 1)
            y = y + x * D
            y = y * (z * jax.nn.sigmoid(z))
            return y @ W_out.T + b_out
        key = jax.random.key(seed)
        ks = jax.random.split(key, 12)
        B, T = (2, 512)
        s_in = 1.0 / np.sqrt(D_MODEL)
        s_x = 1.0 / np.sqrt(D_INNER)
        s_dt = 1.0 / np.sqrt(DT_RANK)
        inp = {'u': jax.random.normal(ks[0], (B, T, D_MODEL), jnp.float32), 'W_in': jax.random.uniform(ks[1], (2 * D_INNER, D_MODEL), jnp.float32, -s_in, s_in), 'b_in': jax.random.uniform(ks[2], (2 * D_INNER,), jnp.float32, -s_in, s_in), 'W_x': jax.random.uniform(ks[3], (DT_RANK + 2 * D_STATE, D_INNER), jnp.float32, -s_x, s_x), 'b_x': jax.random.uniform(ks[4], (DT_RANK + 2 * D_STATE,), jnp.float32, -s_x, s_x), 'W_dt': jax.random.uniform(ks[5], (D_INNER, DT_RANK), jnp.float32, -s_dt, s_dt), 'b_dt': jax.random.uniform(ks[6], (D_INNER,), jnp.float32, -s_dt, s_dt), 'A_log': jnp.log(jnp.abs(jax.random.normal(ks[7], (D_INNER, D_STATE), jnp.float32)) + 1e-06), 'D': jnp.ones((D_INNER,), jnp.float32), 'W_out': jax.random.uniform(ks[8], (D_MODEL, D_INNER), jnp.float32, -s_x, s_x), 'b_out': jax.random.uniform(ks[9], (D_MODEL,), jnp.float32, -s_x, s_x)}
        return inp
    _L0_attn_all = _L0_attn_setup()
    _L0_attn_in = {k: v for k, v in _L0_attn_all.items() if k in ('W_in', 'b_in', 'W_x', 'b_x', 'W_dt', 'b_dt', 'A_log', 'D', 'W_out', 'b_out')}
    del _L0_attn_all

    def _L0_ffn_setup():
        import jax, jax.numpy as jnp
        import numpy as np
        B, S, D, E, H, DO = (4, 512, 256, 8, 1024, 256)
        TOP_K = 2
        LN_EPS = 1e-05
        key = jax.random.key(seed)
        ks = jax.random.split(key, 9)
        s = 0.02
        return {'x': jax.random.normal(ks[0], (B, S, D), dtype=jnp.float32), 'W1': jax.random.normal(ks[1], (E, D, H), dtype=jnp.float32) * s, 'b1': jnp.zeros((E, H), dtype=jnp.float32), 'W2': jax.random.normal(ks[2], (E, H, DO), dtype=jnp.float32) * s, 'b2': jnp.zeros((E, DO), dtype=jnp.float32), 'gate_W': jax.random.normal(ks[3], (D, E), dtype=jnp.float32) * s, 'shared_W': jax.random.normal(ks[4], (D, DO), dtype=jnp.float32) * s, 'shared_b': jnp.zeros((DO,), dtype=jnp.float32), 'gamma': jnp.ones((DO,), dtype=jnp.float32), 'beta': jnp.zeros((DO,), dtype=jnp.float32)}
    _L0_ffn_all = _L0_ffn_setup()
    _L0_ffn_in = {k: v for k, v in _L0_ffn_all.items() if k in ('W1', 'b1', 'W2', 'b2', 'gate_W', 'shared_W', 'shared_b', 'gamma', 'beta')}
    del _L0_ffn_all

    def _L1_xattn_setup():
        import jax, jax.numpy as jnp
        import numpy as np
        DIM = 256
        DIM_LATENT = 256
        DIM_HEAD = 64
        HEADS = 16
        INNER = HEADS * DIM_HEAD

        def layernorm(x, g, b, eps=1e-05):
            m = jnp.mean(x, axis=-1, keepdims=True)
            v = jnp.mean((x - m) ** 2, axis=-1, keepdims=True)
            return (x - m) / jnp.sqrt(v + eps) * g + b

        def rmsnorm(x, gamma, eps=1e-08):
            n = jnp.linalg.norm(x, axis=-1, keepdims=True) * x.shape[-1] ** (-0.5)
            return x / jnp.maximum(n, eps) * gamma
        key = jax.random.key(seed)
        ks = jax.random.split(key, 8)
        b, n, m = (4, 1024, 128)
        x = jax.random.normal(ks[0], (b, n, DIM), dtype=jnp.float32)
        latents = jax.random.normal(ks[1], (b, m, DIM_LATENT), dtype=jnp.float32)
        mask = jnp.ones((b, n), dtype=bool)
        s = 0.02
        return {'x': x, 'latents': latents, 'mask': mask, 'ln_x_g': jnp.ones((DIM,), jnp.float32), 'ln_x_b': jnp.zeros((DIM,), jnp.float32), 'ln_l_g': jnp.ones((DIM_LATENT,), jnp.float32), 'ln_l_b': jnp.zeros((DIM_LATENT,), jnp.float32), 'qn_g': jnp.ones((DIM_HEAD,), jnp.float32), 'kn_g': jnp.ones((DIM_HEAD,), jnp.float32), 'Wq': jax.random.normal(ks[2], (DIM_LATENT, INNER), jnp.float32) * s, 'Wkv': jax.random.normal(ks[3], (DIM, 2 * INNER), jnp.float32) * s, 'Wout': jax.random.normal(ks[4], (INNER, DIM_LATENT), jnp.float32) * s, 'bout': jnp.zeros((DIM_LATENT,), jnp.float32)}
    _L1_xattn_all = _L1_xattn_setup()
    _L1_xattn_in = {k: v for k, v in _L1_xattn_all.items() if k in ('ln_x_g', 'ln_x_b', 'ln_l_g', 'ln_l_b', 'qn_g', 'kn_g', 'Wq', 'Wkv', 'Wout', 'bout')}
    del _L1_xattn_all

    def _L1_attn_setup():
        import jax, jax.numpy as jnp
        import numpy as np
        import math
        EMBED_DIM = 256
        NUM_HEADS = 16
        HEAD_DIM = EMBED_DIM // NUM_HEADS
        MAX_LEN = 1250
        LN_EPS = 1e-05

        def _positional_encoding(max_len, embed_dim):
            pos = np.arange(max_len, dtype=np.float32)[:, None]
            div = np.exp(np.arange(0, embed_dim, 2, dtype=np.float32) * (-math.log(10000.0) / embed_dim))
            pe = np.zeros((max_len, embed_dim), dtype=np.float32)
            pe[:, 0::2] = np.sin(pos * div)
            pe[:, 1::2] = np.cos(pos * div)
            return jnp.asarray(pe)[None]
        key = jax.random.key(seed)
        ks = jax.random.split(key, 12)
        s = 1.0 / math.sqrt(EMBED_DIM)
        D = EMBED_DIM
        return {'x': jax.random.normal(ks[0], (4, 512, D), dtype=jnp.float32), 'wq': jax.random.uniform(ks[1], (D, D), jnp.float32, -s, s), 'bq': jax.random.uniform(ks[2], (D,), jnp.float32, -s, s), 'wk': jax.random.uniform(ks[3], (D, D), jnp.float32, -s, s), 'bk': jax.random.uniform(ks[4], (D,), jnp.float32, -s, s), 'wv': jax.random.uniform(ks[5], (D, D), jnp.float32, -s, s), 'bv': jax.random.uniform(ks[6], (D,), jnp.float32, -s, s), 'wo': jax.random.uniform(ks[7], (D, D), jnp.float32, -s, s), 'bo': jax.random.uniform(ks[8], (D,), jnp.float32, -s, s), 'gamma': jnp.ones((D,), jnp.float32), 'beta': jnp.zeros((D,), jnp.float32), 'pe': _positional_encoding(MAX_LEN, D)}
    _L1_attn_all = _L1_attn_setup()
    _L1_attn_in = {k: v for k, v in _L1_attn_all.items() if k in ('wq', 'bq', 'wk', 'bk', 'wv', 'bv', 'wo', 'bo', 'gamma', 'beta', 'pe')}
    del _L1_attn_all

    def _L1_ffn_setup():
        import jax, jax.numpy as jnp
        import numpy as np
        D_IN, D_HID = (256, 1024)

        def _ternary(key, shape):
            return jax.random.randint(key, shape, -1, 2).astype(jnp.float32)

        def _tlin(x, w, s):
            return jnp.einsum('bsi,oi->bso', x, w) * s
        key = jax.random.key(seed)
        ks = jax.random.split(key, 12)
        inv = lambda fan: 1.0 / np.sqrt(fan).astype(np.float32)
        return {'x': jax.random.normal(ks[0], (4, 512, D_IN), dtype=jnp.float32), 'w1_w': _ternary(ks[1], (D_HID, D_IN)), 'w1_s': jax.random.uniform(ks[2], (D_HID,), dtype=jnp.float32) * inv(D_IN), 'w2_w': _ternary(ks[3], (D_HID, D_IN)), 'w2_s': jax.random.uniform(ks[4], (D_HID,), dtype=jnp.float32) * inv(D_IN), 'h1_w': _ternary(ks[5], (D_HID, D_HID)), 'h1_s': jax.random.uniform(ks[6], (D_HID,), dtype=jnp.float32) * inv(D_HID), 'h2_w': _ternary(ks[7], (D_HID, D_HID)), 'h2_s': jax.random.uniform(ks[8], (D_HID,), dtype=jnp.float32) * inv(D_HID), 'w3_w': _ternary(ks[9], (D_IN, D_HID)), 'w3_s': jax.random.uniform(ks[10], (D_IN,), dtype=jnp.float32) * inv(D_HID)}
    _L1_ffn_all = _L1_ffn_setup()
    _L1_ffn_in = {k: v for k, v in _L1_ffn_all.items() if k in ('w1_w', 'w1_s', 'w2_w', 'w2_s', 'h1_w', 'h1_s', 'h2_w', 'h2_s', 'w3_w', 'w3_s')}
    del _L1_ffn_all

    def _L2_xattn_setup():
        import jax, jax.numpy as jnp
        import numpy as np
        B, L_ENC, L_DEC, D = (16, 128, 128, 256)
        key = jax.random.key(seed)
        k1, k2, k3, k4, k5, k6 = jax.random.split(key, 6)
        encoder_hc = jax.random.normal(k1, (B, L_ENC, D), dtype=jnp.float32)
        decoder_hq = jax.random.normal(k2, (B, L_DEC, D), dtype=jnp.float32)
        w_sim = jax.random.normal(k3, (3 * D,), dtype=jnp.float32) * 0.02
        b_sim = jax.random.normal(k4, (1,), dtype=jnp.float32) * 0.02
        W_qv = jax.random.normal(k5, (4 * D, D), dtype=jnp.float32) * 0.02
        b_qv = jax.random.normal(k6, (D,), dtype=jnp.float32) * 0.02
        return {'encoder_hc': encoder_hc, 'decoder_hq': decoder_hq, 'w_sim': w_sim, 'b_sim': b_sim, 'W_qv': W_qv, 'b_qv': b_qv}
    _L2_xattn_all = _L2_xattn_setup()
    _L2_xattn_in = {k: v for k, v in _L2_xattn_all.items() if k in ('w_sim', 'b_sim', 'W_qv', 'b_qv')}
    del _L2_xattn_all

    def _L2_attn_setup():
        import jax, jax.numpy as jnp
        import numpy as np
        B, M, D = (8, 512, 256)

        def _rope_tables(m, d):
            i = jnp.arange(d // 2, dtype=jnp.float32)
            theta = jnp.power(jnp.float32(10000.0), -2.0 * (i - 1.0) / d)
            ang = jnp.arange(m, dtype=jnp.float32)[:, None] * theta[None, :]
            return (jnp.cos(ang), jnp.sin(ang))

        def _rotate(t, cos, sin):
            te, to = (t[..., 0::2], t[..., 1::2])
            re = te * cos + to * sin
            ro = -te * sin + to * cos
            return jnp.stack([re, ro], axis=-1).reshape(t.shape)
        key = jax.random.key(seed)
        kx, kq, kk, kv = jax.random.split(key, 4)
        x = jax.random.normal(kx, (B, M, D), dtype=jnp.float32)
        wq = jax.random.normal(kq, (D, D), dtype=jnp.float32) * 0.02
        wk = jax.random.normal(kk, (D, D), dtype=jnp.float32) * 0.02
        wv = jax.random.normal(kv, (D, D), dtype=jnp.float32) * 0.02
        return {'x': x, 'wq': wq, 'wk': wk, 'wv': wv}
    _L2_attn_all = _L2_attn_setup()
    _L2_attn_in = {k: v for k, v in _L2_attn_all.items() if k in ('wq', 'wk', 'wv')}
    del _L2_attn_all

    def _L2_ffn_setup():
        import jax, jax.numpy as jnp
        import numpy as np

        def _binarize(w):
            alpha = jax.lax.stop_gradient(jnp.mean(jnp.abs(w), axis=1, keepdims=True))
            bw = alpha * jnp.sign(w)
            return w + jax.lax.stop_gradient(bw - w)
        key = jax.random.key(seed)
        k1, k2, k3, k4, k5 = jax.random.split(key, 5)
        D, H = (256, 1024)
        x = jax.random.normal(k1, (64, 196, D), dtype=jnp.float32)
        w1 = jax.random.normal(k2, (H, D), dtype=jnp.float32) * 0.02
        b1 = jax.random.normal(k3, (H,), dtype=jnp.float32) * 0.02
        w2 = jax.random.normal(k4, (D, H), dtype=jnp.float32) * 0.02
        b2 = jax.random.normal(k5, (D,), dtype=jnp.float32) * 0.02
        return {'x': x, 'w1': w1, 'b1': b1, 'w2': w2, 'b2': b2}
    _L2_ffn_all = _L2_ffn_setup()
    _L2_ffn_in = {k: v for k, v in _L2_ffn_all.items() if k in ('w1', 'b1', 'w2', 'b2')}
    del _L2_ffn_all

    def _L3_xattn_setup():
        import jax, jax.numpy as jnp
        import numpy as np
        import math
        B, S, D, H = (4, 512, 256, 16)
        HD = D // H
        key = jax.random.key(seed)
        ks = jax.random.split(key, 7)
        scale = 1.0 / math.sqrt(D)
        return {'q': jax.random.normal(ks[0], (B, S, D), jnp.float32), 'k': jax.random.normal(ks[1], (B, S, D), jnp.float32), 'v': jax.random.normal(ks[2], (B, S, D), jnp.float32), 'mask': jnp.zeros((1, 1, S, S), jnp.float32), 'wq': jax.random.normal(ks[3], (D, D), jnp.float32) * scale, 'wk': jax.random.normal(ks[4], (D, D), jnp.float32) * scale, 'wv': jax.random.normal(ks[5], (D, D), jnp.float32) * scale, 'wo': jax.random.normal(ks[6], (D, D), jnp.float32) * scale}
    _L3_xattn_all = _L3_xattn_setup()
    _L3_xattn_in = {k: v for k, v in _L3_xattn_all.items() if k in ('wq', 'wk', 'wv', 'wo')}
    del _L3_xattn_all

    def _L3_attn_setup():
        import jax, jax.numpy as jnp
        import numpy as np
        import math
        N_HEAD = 16
        V_HEAD = 32
        NOPE = 32
        ROPE_D = 64
        KEEP = 64
        EPS = 1e-06

        def _freqs(T, dim=ROPE_D, theta=10000.0):
            f = 1.0 / theta ** (jnp.arange(0, dim, 2, dtype=jnp.float32) / dim)
            t = jnp.arange(T, dtype=jnp.float32)
            a = jnp.outer(t, f)
            return (jnp.cos(a), jnp.sin(a))

        def _rope(x, cos, sin):
            S = x.shape[-2]
            c = cos[:S][None, None]
            s = sin[:S][None, None]
            x1, x2 = jnp.split(x, 2, axis=-1)
            return jnp.concatenate([x1 * c - x2 * s, x1 * s + x2 * c], axis=-1)

        def _rms(x, g, eps=EPS):
            return x * jax.lax.rsqrt(jnp.mean(x * x, axis=-1, keepdims=True) + eps) * g

        def _attn(q, k, v, causal):
            scale = 1.0 / math.sqrt(q.shape[-1])
            s = jnp.einsum('bhqd,bhkd->bhqk', q, k) * scale
            if causal:
                Tq, Tk = (s.shape[-2], s.shape[-1])
                mask = jnp.tril(jnp.ones((Tq, Tk), dtype=bool))
                s = jnp.where(mask, s, jnp.finfo(s.dtype).min)
            return jnp.einsum('bhqk,bhkd->bhqd', jax.nn.softmax(s, axis=-1), v)

        def _forward(x, w_cq, g_qnorm, w_dq_nope, w_dq_rope, w_ckv, g_kvnorm, w_dk_nope, w_dv, w_krope, w_imp, w_selk, w_selv, w_wink, w_winv, w_gate, w_proj):
            B, T, C = x.shape
            cos, sin = _freqs(T)
            nq = _rms(x @ w_cq, g_qnorm)
            q_nope = (nq @ w_dq_nope).reshape(B, T, N_HEAD, NOPE).transpose(0, 2, 1, 3)
            q_rope = (nq @ w_dq_rope).reshape(B, T, N_HEAD, ROPE_D).transpose(0, 2, 1, 3)
            q_rope = _rope(q_rope, cos, sin)
            q = jnp.concatenate([q_nope, q_rope], axis=-1)
            gate = jax.nn.softmax((x @ w_gate).mean(axis=1), axis=-1)
            ckv = _rms(x @ w_ckv, g_kvnorm)
            k_nope = (ckv @ w_dk_nope).reshape(B, T, N_HEAD, NOPE).transpose(0, 2, 1, 3)
            v1 = (ckv @ w_dv).reshape(B, T, N_HEAD, V_HEAD).transpose(0, 2, 1, 3)
            k_rope = (x @ w_krope).reshape(B, T, 1, ROPE_D).transpose(0, 2, 1, 3) / N_HEAD
            k_rope = _rope(k_rope, cos, sin)
            k1 = jnp.concatenate([k_nope, jnp.broadcast_to(k_rope, (B, N_HEAD, T, ROPE_D))], axis=-1)
            scores = (x @ w_imp)[..., 0]
            _, idx = jax.lax.top_k(scores, KEEP)
            idx = jnp.sort(idx, axis=1)
            sel = jnp.take_along_axis(x, idx[:, :, None], axis=1)
            ks = (sel @ w_selk).reshape(B, KEEP, N_HEAD, NOPE + ROPE_D).transpose(0, 2, 1, 3)
            vs = (sel @ w_selv).reshape(B, KEEP, N_HEAD, V_HEAD).transpose(0, 2, 1, 3)
            ks = jnp.concatenate([ks[..., :NOPE], _rope(ks[..., NOPE:], cos, sin)], axis=-1)
            kw = (x @ w_wink).reshape(B, T, N_HEAD, NOPE + ROPE_D).transpose(0, 2, 1, 3)
            vw = (x @ w_winv).reshape(B, T, N_HEAD, V_HEAD).transpose(0, 2, 1, 3)
            kw = jnp.concatenate([kw[..., :NOPE], _rope(kw[..., NOPE:], cos, sin)], axis=-1)
            a1 = _attn(q, k1, v1, causal=True)
            a2 = _attn(q, ks, vs, causal=False)
            a3 = _attn(q, kw, vw, causal=True)
            g = gate[:, :, None, None, None]
            out = g[:, 0] * a1 + g[:, 1] * a2 + g[:, 2] * a3
            out = out.transpose(0, 2, 1, 3).reshape(B, T, N_HEAD * V_HEAD)
            return out @ w_proj
        key = jax.random.key(seed)
        ks = jax.random.split(key, 20)
        B, T, C = (2, 256, 256)
        q_lora, kv_lora = (96, 32)
        std = 0.02

        def w(k, shape):
            return jax.random.normal(k, shape, dtype=jnp.float32) * std
        return {'x': jax.random.normal(ks[0], (B, T, C), dtype=jnp.float32), 'w_cq': w(ks[1], (C, q_lora)), 'g_qnorm': jnp.ones((q_lora,), jnp.float32), 'w_dq_nope': w(ks[2], (q_lora, N_HEAD * NOPE)), 'w_dq_rope': w(ks[3], (q_lora, N_HEAD * ROPE_D)), 'w_ckv': w(ks[4], (C, kv_lora)), 'g_kvnorm': jnp.ones((kv_lora,), jnp.float32), 'w_dk_nope': w(ks[5], (kv_lora, N_HEAD * NOPE)), 'w_dv': w(ks[6], (kv_lora, N_HEAD * V_HEAD)), 'w_krope': w(ks[7], (C, ROPE_D)), 'w_imp': w(ks[8], (C, 1)), 'w_selk': w(ks[9], (C, N_HEAD * (NOPE + ROPE_D))), 'w_selv': w(ks[10], (C, N_HEAD * V_HEAD)), 'w_wink': w(ks[11], (C, N_HEAD * (NOPE + ROPE_D))), 'w_winv': w(ks[12], (C, N_HEAD * V_HEAD)), 'w_gate': w(ks[13], (C, 3)), 'w_proj': w(ks[14], (N_HEAD * V_HEAD, C))}
    _L3_attn_all = _L3_attn_setup()
    _L3_attn_in = {k: v for k, v in _L3_attn_all.items() if k in ('w_cq', 'g_qnorm', 'w_dq_nope', 'w_dq_rope', 'w_ckv', 'g_kvnorm', 'w_dk_nope', 'w_dv', 'w_krope', 'w_imp', 'w_selk', 'w_selv', 'w_wink', 'w_winv', 'w_gate', 'w_proj')}
    del _L3_attn_all

    def _L3_ffn_setup():
        import jax, jax.numpy as jnp
        import numpy as np
        N_EXPERTS = 32
        TOP_K = 8
        N_GROUP = 4
        TOPK_GROUP = 2
        ROUTED_SCALING = 2.5

        def _gate(x, gate_w, gate_bias):
            T, E = (x.shape[0], gate_w.shape[0])
            logits = jnp.einsum('th,eh->te', x, gate_w)
            scores = jax.nn.sigmoid(logits)
            scores_choice = scores + gate_bias[None, :]
            grp = scores_choice.reshape(T, N_GROUP, E // N_GROUP)
            top2, _ = jax.lax.top_k(grp, 2)
            group_scores = top2.sum(-1)
            _, grp_idx = jax.lax.top_k(group_scores, TOPK_GROUP)
            group_mask = jax.nn.one_hot(grp_idx, N_GROUP, dtype=scores.dtype).sum(1)
            expert_mask = jnp.repeat(group_mask, E // N_GROUP, axis=1)
            masked = jnp.where(expert_mask > 0, scores_choice, 0.0)
            _, topk_idx = jax.lax.top_k(masked, TOP_K)
            topk_w = jnp.take_along_axis(scores, topk_idx, axis=1)
            topk_w = topk_w / (topk_w.sum(-1, keepdims=True) + 1e-20)
            topk_w = topk_w * ROUTED_SCALING
            return (topk_idx, topk_w)

        def _mlp(x, wg, wu, wd):
            return jnp.einsum('...i,hi->...h', jax.nn.silu(jnp.einsum('...h,ih->...i', x, wg)) * jnp.einsum('...h,ih->...i', x, wu), wd)
        key = jax.random.key(seed)
        ks = jax.random.split(key, 9)
        B, S, H, I = (2, 128, 256, 128)
        w = 0.02
        return {'hidden_states': jax.random.normal(ks[0], (B, S, H), jnp.float32), 'gate_w': jax.random.normal(ks[1], (N_EXPERTS, H), jnp.float32) * w, 'gate_bias': jax.random.normal(ks[2], (N_EXPERTS,), jnp.float32) * w, 'expert_gate': jax.random.normal(ks[3], (N_EXPERTS, I, H), jnp.float32) * w, 'expert_up': jax.random.normal(ks[4], (N_EXPERTS, I, H), jnp.float32) * w, 'expert_down': jax.random.normal(ks[5], (N_EXPERTS, H, I), jnp.float32) * w, 'shared_gate': jax.random.normal(ks[6], (2 * I, H), jnp.float32) * w, 'shared_up': jax.random.normal(ks[7], (2 * I, H), jnp.float32) * w, 'shared_down': jax.random.normal(ks[8], (H, 2 * I), jnp.float32) * w}
    _L3_ffn_all = _L3_ffn_setup()
    _L3_ffn_in = {k: v for k, v in _L3_ffn_all.items() if k in ('gate_w', 'gate_bias', 'expert_gate', 'expert_up', 'expert_down', 'shared_gate', 'shared_up', 'shared_down')}
    del _L3_ffn_all
    return {'x': x, 'ctx_1024': ctx_1024, 'mask_BxS2_bf1': mask_BxS2_bf1, 'mask_1x1xSxS2_ff0': mask_1x1xSxS2_ff0, 'L0_xattn_Wq': _L0_xattn_in['Wq'], 'L0_xattn_Wk': _L0_xattn_in['Wk'], 'L0_xattn_Wv': _L0_xattn_in['Wv'], 'L0_xattn_Wo': _L0_xattn_in['Wo'], 'L0_attn_W_in': _L0_attn_in['W_in'], 'L0_attn_b_in': _L0_attn_in['b_in'], 'L0_attn_W_x': _L0_attn_in['W_x'], 'L0_attn_b_x': _L0_attn_in['b_x'], 'L0_attn_W_dt': _L0_attn_in['W_dt'], 'L0_attn_b_dt': _L0_attn_in['b_dt'], 'L0_attn_A_log': _L0_attn_in['A_log'], 'L0_attn_D': _L0_attn_in['D'], 'L0_attn_W_out': _L0_attn_in['W_out'], 'L0_attn_b_out': _L0_attn_in['b_out'], 'L0_ffn_W1': _L0_ffn_in['W1'], 'L0_ffn_b1': _L0_ffn_in['b1'], 'L0_ffn_W2': _L0_ffn_in['W2'], 'L0_ffn_b2': _L0_ffn_in['b2'], 'L0_ffn_gate_W': _L0_ffn_in['gate_W'], 'L0_ffn_shared_W': _L0_ffn_in['shared_W'], 'L0_ffn_shared_b': _L0_ffn_in['shared_b'], 'L0_ffn_gamma': _L0_ffn_in['gamma'], 'L0_ffn_beta': _L0_ffn_in['beta'], 'L1_xattn_ln_x_g': _L1_xattn_in['ln_x_g'], 'L1_xattn_ln_x_b': _L1_xattn_in['ln_x_b'], 'L1_xattn_ln_l_g': _L1_xattn_in['ln_l_g'], 'L1_xattn_ln_l_b': _L1_xattn_in['ln_l_b'], 'L1_xattn_qn_g': _L1_xattn_in['qn_g'], 'L1_xattn_kn_g': _L1_xattn_in['kn_g'], 'L1_xattn_Wq': _L1_xattn_in['Wq'], 'L1_xattn_Wkv': _L1_xattn_in['Wkv'], 'L1_xattn_Wout': _L1_xattn_in['Wout'], 'L1_xattn_bout': _L1_xattn_in['bout'], 'L1_attn_wq': _L1_attn_in['wq'], 'L1_attn_bq': _L1_attn_in['bq'], 'L1_attn_wk': _L1_attn_in['wk'], 'L1_attn_bk': _L1_attn_in['bk'], 'L1_attn_wv': _L1_attn_in['wv'], 'L1_attn_bv': _L1_attn_in['bv'], 'L1_attn_wo': _L1_attn_in['wo'], 'L1_attn_bo': _L1_attn_in['bo'], 'L1_attn_gamma': _L1_attn_in['gamma'], 'L1_attn_beta': _L1_attn_in['beta'], 'L1_attn_pe': _L1_attn_in['pe'], 'L1_ffn_w1_w': _L1_ffn_in['w1_w'], 'L1_ffn_w1_s': _L1_ffn_in['w1_s'], 'L1_ffn_w2_w': _L1_ffn_in['w2_w'], 'L1_ffn_w2_s': _L1_ffn_in['w2_s'], 'L1_ffn_h1_w': _L1_ffn_in['h1_w'], 'L1_ffn_h1_s': _L1_ffn_in['h1_s'], 'L1_ffn_h2_w': _L1_ffn_in['h2_w'], 'L1_ffn_h2_s': _L1_ffn_in['h2_s'], 'L1_ffn_w3_w': _L1_ffn_in['w3_w'], 'L1_ffn_w3_s': _L1_ffn_in['w3_s'], 'L2_xattn_w_sim': _L2_xattn_in['w_sim'], 'L2_xattn_b_sim': _L2_xattn_in['b_sim'], 'L2_xattn_W_qv': _L2_xattn_in['W_qv'], 'L2_xattn_b_qv': _L2_xattn_in['b_qv'], 'L2_attn_wq': _L2_attn_in['wq'], 'L2_attn_wk': _L2_attn_in['wk'], 'L2_attn_wv': _L2_attn_in['wv'], 'L2_ffn_w1': _L2_ffn_in['w1'], 'L2_ffn_b1': _L2_ffn_in['b1'], 'L2_ffn_w2': _L2_ffn_in['w2'], 'L2_ffn_b2': _L2_ffn_in['b2'], 'L3_xattn_wq': _L3_xattn_in['wq'], 'L3_xattn_wk': _L3_xattn_in['wk'], 'L3_xattn_wv': _L3_xattn_in['wv'], 'L3_xattn_wo': _L3_xattn_in['wo'], 'L3_attn_w_cq': _L3_attn_in['w_cq'], 'L3_attn_g_qnorm': _L3_attn_in['g_qnorm'], 'L3_attn_w_dq_nope': _L3_attn_in['w_dq_nope'], 'L3_attn_w_dq_rope': _L3_attn_in['w_dq_rope'], 'L3_attn_w_ckv': _L3_attn_in['w_ckv'], 'L3_attn_g_kvnorm': _L3_attn_in['g_kvnorm'], 'L3_attn_w_dk_nope': _L3_attn_in['w_dk_nope'], 'L3_attn_w_dv': _L3_attn_in['w_dv'], 'L3_attn_w_krope': _L3_attn_in['w_krope'], 'L3_attn_w_imp': _L3_attn_in['w_imp'], 'L3_attn_w_selk': _L3_attn_in['w_selk'], 'L3_attn_w_selv': _L3_attn_in['w_selv'], 'L3_attn_w_wink': _L3_attn_in['w_wink'], 'L3_attn_w_winv': _L3_attn_in['w_winv'], 'L3_attn_w_gate': _L3_attn_in['w_gate'], 'L3_attn_w_proj': _L3_attn_in['w_proj'], 'L3_ffn_gate_w': _L3_ffn_in['gate_w'], 'L3_ffn_gate_bias': _L3_ffn_in['gate_bias'], 'L3_ffn_expert_gate': _L3_ffn_in['expert_gate'], 'L3_ffn_expert_up': _L3_ffn_in['expert_up'], 'L3_ffn_expert_down': _L3_ffn_in['expert_down'], 'L3_ffn_shared_gate': _L3_ffn_in['shared_gate'], 'L3_ffn_shared_up': _L3_ffn_in['shared_up'], 'L3_ffn_shared_down': _L3_ffn_in['shared_down']}

def reference(x, ctx_1024, mask_BxS2_bf1, mask_1x1xSxS2_ff0, L0_xattn_Wq, L0_xattn_Wk, L0_xattn_Wv, L0_xattn_Wo, L0_attn_W_in, L0_attn_b_in, L0_attn_W_x, L0_attn_b_x, L0_attn_W_dt, L0_attn_b_dt, L0_attn_A_log, L0_attn_D, L0_attn_W_out, L0_attn_b_out, L0_ffn_W1, L0_ffn_b1, L0_ffn_W2, L0_ffn_b2, L0_ffn_gate_W, L0_ffn_shared_W, L0_ffn_shared_b, L0_ffn_gamma, L0_ffn_beta, L1_xattn_ln_x_g, L1_xattn_ln_x_b, L1_xattn_ln_l_g, L1_xattn_ln_l_b, L1_xattn_qn_g, L1_xattn_kn_g, L1_xattn_Wq, L1_xattn_Wkv, L1_xattn_Wout, L1_xattn_bout, L1_attn_wq, L1_attn_bq, L1_attn_wk, L1_attn_bk, L1_attn_wv, L1_attn_bv, L1_attn_wo, L1_attn_bo, L1_attn_gamma, L1_attn_beta, L1_attn_pe, L1_ffn_w1_w, L1_ffn_w1_s, L1_ffn_w2_w, L1_ffn_w2_s, L1_ffn_h1_w, L1_ffn_h1_s, L1_ffn_h2_w, L1_ffn_h2_s, L1_ffn_w3_w, L1_ffn_w3_s, L2_xattn_w_sim, L2_xattn_b_sim, L2_xattn_W_qv, L2_xattn_b_qv, L2_attn_wq, L2_attn_wk, L2_attn_wv, L2_ffn_w1, L2_ffn_b1, L2_ffn_w2, L2_ffn_b2, L3_xattn_wq, L3_xattn_wk, L3_xattn_wv, L3_xattn_wo, L3_attn_w_cq, L3_attn_g_qnorm, L3_attn_w_dq_nope, L3_attn_w_dq_rope, L3_attn_w_ckv, L3_attn_g_kvnorm, L3_attn_w_dk_nope, L3_attn_w_dv, L3_attn_w_krope, L3_attn_w_imp, L3_attn_w_selk, L3_attn_w_selv, L3_attn_w_wink, L3_attn_w_winv, L3_attn_w_gate, L3_attn_w_proj, L3_ffn_gate_w, L3_ffn_gate_bias, L3_ffn_expert_gate, L3_ffn_expert_up, L3_ffn_expert_down, L3_ffn_shared_gate, L3_ffn_shared_up, L3_ffn_shared_down):
    import jax
    import jax.numpy as jnp

    def _L0_xattn_ref(query, key, value, Wq, Wk, Wv, Wo):
        import jax, jax.numpy as jnp
        import numpy as np
        EMBED_DIM = 256
        NUM_HEADS = 16
        HEAD_DIM = EMBED_DIM // NUM_HEADS
        B, L, E = query.shape
        H, D = (NUM_HEADS, HEAD_DIM)
        scale = D ** (-0.5)
        q = (query @ Wq.T).reshape(B, L, H, D) * scale
        k = (key @ Wk.T).reshape(B, -1, H, D)
        v = (value @ Wv.T).reshape(B, -1, H, D)
        scores = jax.nn.sigmoid(jnp.einsum('blhd,bshd->bhls', q, k))
        o = jnp.einsum('bhls,bshd->blhd', scores, v).reshape(B, L, E)
        return o @ Wo.T

    def _L0_attn_ref(u, W_in, b_in, W_x, b_x, W_dt, b_dt, A_log, D, W_out, b_out):
        import jax, jax.numpy as jnp
        import numpy as np
        D_MODEL = 256
        D_STATE = 16
        EXPAND = 2
        D_INNER = D_MODEL * EXPAND
        DT_RANK = D_MODEL // 16

        def _ssm_forward(u, W_in, b_in, W_x, b_x, W_dt, b_dt, A_log, D, W_out, b_out):
            B, T, _ = u.shape
            u_inner = u @ W_in.T + b_in
            x, z = jnp.split(u_inner, 2, axis=-1)
            dbc = x @ W_x.T + b_x
            delta_raw = dbc[..., :DT_RANK]
            B_ssm = dbc[..., DT_RANK:DT_RANK + D_STATE]
            C_ssm = dbc[..., DT_RANK + D_STATE:]
            delta = jax.nn.softplus(delta_raw @ W_dt.T + b_dt)
            A = -jnp.exp(A_log)

            def step(h, xs):
                dt_t, x_t, Bt, Ct = xs
                dA = jnp.exp(dt_t[..., None] * A)
                dB = dt_t[..., None] * Bt[:, None, :]
                h = h * dA + x_t[..., None] * dB
                y_t = jnp.einsum('bdn,bn->bd', h, Ct)
                return (h, y_t)
            h0 = jnp.zeros((B, D_INNER, D_STATE), u.dtype)
            xs = (jnp.swapaxes(delta, 0, 1), jnp.swapaxes(x, 0, 1), jnp.swapaxes(B_ssm, 0, 1), jnp.swapaxes(C_ssm, 0, 1))
            _, y = jax.lax.scan(step, h0, xs)
            y = jnp.swapaxes(y, 0, 1)
            y = y + x * D
            y = y * (z * jax.nn.sigmoid(z))
            return y @ W_out.T + b_out
        return _ssm_forward(u, W_in, b_in, W_x, b_x, W_dt, b_dt, A_log, D, W_out, b_out)

    def _L0_ffn_ref(x, W1, b1, W2, b2, gate_W, shared_W, shared_b, gamma, beta):
        import jax, jax.numpy as jnp
        import numpy as np
        B, S, D, E, H, DO = (4, 512, 256, 8, 1024, 256)
        TOP_K = 2
        LN_EPS = 1e-05
        d = x.shape[-1]
        flat = x.reshape(-1, d)
        n_exp = gate_W.shape[-1]
        probs = jax.nn.softmax(flat @ gate_W, axis=-1)
        topk_w, topk_idx = jax.lax.top_k(probs, TOP_K)
        topk_w = topk_w / topk_w.sum(axis=-1, keepdims=True)
        combine = (jax.nn.one_hot(topk_idx, n_exp, dtype=flat.dtype) * topk_w[..., None]).sum(axis=1)
        out = 0.5 * jax.nn.gelu(flat @ shared_W + shared_b, approximate=False)
        for e in range(n_exp):
            h = jax.nn.gelu(flat @ W1[e] + b1[e], approximate=False)
            out = out + combine[:, e:e + 1] * (h @ W2[e] + b2[e])
        mean = out.mean(axis=-1, keepdims=True)
        var = ((out - mean) ** 2).mean(axis=-1, keepdims=True)
        out = (out - mean) * jax.lax.rsqrt(var + LN_EPS) * gamma + beta
        return out.reshape(*x.shape[:-1], out.shape[-1])

    def _L1_xattn_ref(x, latents, mask, ln_x_g, ln_x_b, ln_l_g, ln_l_b, qn_g, kn_g, Wq, Wkv, Wout, bout):
        import jax, jax.numpy as jnp
        import numpy as np
        DIM = 256
        DIM_LATENT = 256
        DIM_HEAD = 64
        HEADS = 16
        INNER = HEADS * DIM_HEAD

        def layernorm(x, g, b, eps=1e-05):
            m = jnp.mean(x, axis=-1, keepdims=True)
            v = jnp.mean((x - m) ** 2, axis=-1, keepdims=True)
            return (x - m) / jnp.sqrt(v + eps) * g + b

        def rmsnorm(x, gamma, eps=1e-08):
            n = jnp.linalg.norm(x, axis=-1, keepdims=True) * x.shape[-1] ** (-0.5)
            return x / jnp.maximum(n, eps) * gamma
        b, n, _ = x.shape
        m = latents.shape[1]
        h, d = (HEADS, DIM_HEAD)
        scale = d ** (-0.5)
        xn = layernorm(x, ln_x_g, ln_x_b)
        ln = layernorm(latents, ln_l_g, ln_l_b)
        q = (ln @ Wq).reshape(b, m, h, d).transpose(0, 2, 1, 3)
        kv = jnp.concatenate([xn @ Wkv, ln @ Wkv], axis=1)
        kv = kv.reshape(b, n + m, 2, h, d)
        k = kv[:, :, 0].transpose(0, 2, 1, 3)
        v = kv[:, :, 1].transpose(0, 2, 1, 3)
        qn = rmsnorm(q, qn_g) * scale
        kn = rmsnorm(k, kn_g)
        sim = jnp.einsum('bhid,bhjd->bhij', qn, kn)
        max_neg = -jnp.finfo(sim.dtype).max
        padded_mask = jnp.concatenate([mask, jnp.ones((b, m), bool)], axis=1)
        sim = jnp.where(padded_mask[:, None, None, :], sim, max_neg)
        attn = jax.nn.softmax(sim.astype(jnp.float32), axis=-1).astype(sim.dtype)
        out = jnp.einsum('bhij,bhjd->bhid', attn, v)
        out = out.transpose(0, 2, 1, 3).reshape(b, m, h * d)
        return out @ Wout + bout

    def _L1_attn_ref(x, wq, bq, wk, bk, wv, bv, wo, bo, gamma, beta, pe):
        import jax, jax.numpy as jnp
        import numpy as np
        import math
        EMBED_DIM = 256
        NUM_HEADS = 16
        HEAD_DIM = EMBED_DIM // NUM_HEADS
        MAX_LEN = 1250
        LN_EPS = 1e-05

        def _positional_encoding(max_len, embed_dim):
            pos = np.arange(max_len, dtype=np.float32)[:, None]
            div = np.exp(np.arange(0, embed_dim, 2, dtype=np.float32) * (-math.log(10000.0) / embed_dim))
            pe = np.zeros((max_len, embed_dim), dtype=np.float32)
            pe[:, 0::2] = np.sin(pos * div)
            pe[:, 1::2] = np.cos(pos * div)
            return jnp.asarray(pe)[None]
        B, S, D = x.shape
        H, Hd = (NUM_HEADS, HEAD_DIM)
        x = x + pe[:, :S, :]
        q = (x @ wq + bq).reshape(B, S, H, Hd).transpose(0, 2, 1, 3)
        k = (x @ wk + bk).reshape(B, S, H, Hd).transpose(0, 2, 1, 3)
        v = (x @ wv + bv).reshape(B, S, H, Hd).transpose(0, 2, 1, 3)
        scores = jnp.einsum('bhqd,bhkd->bhqk', q, k) / math.sqrt(Hd)
        attn = jax.nn.softmax(scores, axis=-1)
        out = jnp.einsum('bhqk,bhkd->bhqd', attn, v)
        out = out.transpose(0, 2, 1, 3).reshape(B, S, D)
        out = out @ wo + bo
        h = out + x
        mu = jnp.mean(h, axis=-1, keepdims=True)
        var = jnp.var(h, axis=-1, keepdims=True)
        return (h - mu) * jax.lax.rsqrt(var + LN_EPS) * gamma + beta

    def _L1_ffn_ref(x, w1_w, w1_s, w2_w, w2_s, h1_w, h1_s, h2_w, h2_s, w3_w, w3_s):
        import jax, jax.numpy as jnp
        import numpy as np
        D_IN, D_HID = (256, 1024)

        def _ternary(key, shape):
            return jax.random.randint(key, shape, -1, 2).astype(jnp.float32)

        def _tlin(x, w, s):
            return jnp.einsum('bsi,oi->bso', x, w) * s
        h = jax.nn.silu(_tlin(x, w1_w, w1_s)) * _tlin(x, w2_w, w2_s)
        h = jax.nn.gelu(_tlin(h, h1_w, h1_s), approximate=False)
        h = jax.nn.gelu(_tlin(h, h2_w, h2_s), approximate=False)
        return _tlin(h, w3_w, w3_s)

    def _L2_xattn_ref(encoder_hc, decoder_hq, w_sim, b_sim, W_qv, b_qv):
        import jax, jax.numpy as jnp
        import numpy as np
        B, L_ENC, L_DEC, D = (16, 128, 128, 256)
        d = encoder_hc.shape[-1]
        w1, w2, w3 = (w_sim[:d], w_sim[d:2 * d], w_sim[2 * d:])
        Sim = (encoder_hc @ w1)[:, :, None] + (decoder_hq @ w2)[:, None, :] + jnp.einsum('bid,bjd->bij', encoder_hc * w3, decoder_hq) + b_sim[0]
        A = jax.nn.softmax(Sim, axis=2)
        hq_hat = jnp.einsum('bij,bjd->bid', A, decoder_hq)
        Batt = jax.nn.softmax(jnp.max(Sim, axis=2), axis=1)
        hc_bar = jnp.einsum('bi,bid->bd', Batt, encoder_hc)[:, None, :]
        hc_hat = jnp.broadcast_to(hc_bar, encoder_hc.shape)
        feats = jnp.concatenate([encoder_hc, hq_hat, encoder_hc * hq_hat, encoder_hc * hc_hat], axis=-1)
        hcq = feats @ W_qv + b_qv
        return hcq

    def _L2_attn_ref(x, wq, wk, wv):
        import jax, jax.numpy as jnp
        import numpy as np
        B, M, D = (8, 512, 256)

        def _rope_tables(m, d):
            i = jnp.arange(d // 2, dtype=jnp.float32)
            theta = jnp.power(jnp.float32(10000.0), -2.0 * (i - 1.0) / d)
            ang = jnp.arange(m, dtype=jnp.float32)[:, None] * theta[None, :]
            return (jnp.cos(ang), jnp.sin(ang))

        def _rotate(t, cos, sin):
            te, to = (t[..., 0::2], t[..., 1::2])
            re = te * cos + to * sin
            ro = -te * sin + to * cos
            return jnp.stack([re, ro], axis=-1).reshape(t.shape)
        b, m, d = x.shape
        q = x @ wq.T
        k = x @ wk.T
        v = x @ wv.T
        cos, sin = _rope_tables(m, d)
        qr = _rotate(q, cos, sin)
        kr = _rotate(k, cos, sin)
        scale = 1.0 / jnp.sqrt(jnp.float32(d))
        scores = jnp.einsum('bqd,bkd->bqk', qr, kr) * scale
        attn = jax.nn.softmax(scores, axis=-1)
        return jnp.einsum('bqk,bkd->bqd', attn, v)

    def _L2_ffn_ref(x, w1, b1, w2, b2):
        import jax, jax.numpy as jnp
        import numpy as np

        def _binarize(w):
            alpha = jax.lax.stop_gradient(jnp.mean(jnp.abs(w), axis=1, keepdims=True))
            bw = alpha * jnp.sign(w)
            return w + jax.lax.stop_gradient(bw - w)
        bw1 = _binarize(w1)
        h = jnp.einsum('bsd,hd->bsh', x, bw1) + b1
        h = jax.nn.gelu(h, approximate=False)
        bw2 = _binarize(w2)
        out = jnp.einsum('bsh,dh->bsd', h, bw2) + b2
        return out

    def _L3_xattn_ref(q, k, v, mask, wq, wk, wv, wo):
        import jax, jax.numpy as jnp
        import numpy as np
        import math
        B, S, D, H = (4, 512, 256, 16)
        HD = D // H
        bsz, seqlen, _ = q.shape
        xq = (q @ wq).reshape(bsz, seqlen, H, HD).transpose(0, 2, 1, 3)
        xk = (k @ wk).reshape(bsz, k.shape[1], H, HD).transpose(0, 2, 1, 3)
        xv = (v @ wv).reshape(bsz, v.shape[1], H, HD).transpose(0, 2, 1, 3)
        scores = jnp.einsum('bhqd,bhkd->bhqk', xq, xk) / math.sqrt(HD)
        scores = scores + mask
        attn = jax.nn.softmax(scores.astype(jnp.float32), axis=-1)
        out = jnp.einsum('bhqk,bhkd->bhqd', attn, xv)
        out = out.transpose(0, 2, 1, 3).reshape(bsz, seqlen, -1)
        return out @ wo

    def _L3_attn_ref(x, w_cq, g_qnorm, w_dq_nope, w_dq_rope, w_ckv, g_kvnorm, w_dk_nope, w_dv, w_krope, w_imp, w_selk, w_selv, w_wink, w_winv, w_gate, w_proj):
        import jax, jax.numpy as jnp
        import numpy as np
        import math
        N_HEAD = 16
        V_HEAD = 32
        NOPE = 32
        ROPE_D = 64
        KEEP = 64
        EPS = 1e-06

        def _freqs(T, dim=ROPE_D, theta=10000.0):
            f = 1.0 / theta ** (jnp.arange(0, dim, 2, dtype=jnp.float32) / dim)
            t = jnp.arange(T, dtype=jnp.float32)
            a = jnp.outer(t, f)
            return (jnp.cos(a), jnp.sin(a))

        def _rope(x, cos, sin):
            S = x.shape[-2]
            c = cos[:S][None, None]
            s = sin[:S][None, None]
            x1, x2 = jnp.split(x, 2, axis=-1)
            return jnp.concatenate([x1 * c - x2 * s, x1 * s + x2 * c], axis=-1)

        def _rms(x, g, eps=EPS):
            return x * jax.lax.rsqrt(jnp.mean(x * x, axis=-1, keepdims=True) + eps) * g

        def _attn(q, k, v, causal):
            scale = 1.0 / math.sqrt(q.shape[-1])
            s = jnp.einsum('bhqd,bhkd->bhqk', q, k) * scale
            if causal:
                Tq, Tk = (s.shape[-2], s.shape[-1])
                mask = jnp.tril(jnp.ones((Tq, Tk), dtype=bool))
                s = jnp.where(mask, s, jnp.finfo(s.dtype).min)
            return jnp.einsum('bhqk,bhkd->bhqd', jax.nn.softmax(s, axis=-1), v)

        def _forward(x, w_cq, g_qnorm, w_dq_nope, w_dq_rope, w_ckv, g_kvnorm, w_dk_nope, w_dv, w_krope, w_imp, w_selk, w_selv, w_wink, w_winv, w_gate, w_proj):
            B, T, C = x.shape
            cos, sin = _freqs(T)
            nq = _rms(x @ w_cq, g_qnorm)
            q_nope = (nq @ w_dq_nope).reshape(B, T, N_HEAD, NOPE).transpose(0, 2, 1, 3)
            q_rope = (nq @ w_dq_rope).reshape(B, T, N_HEAD, ROPE_D).transpose(0, 2, 1, 3)
            q_rope = _rope(q_rope, cos, sin)
            q = jnp.concatenate([q_nope, q_rope], axis=-1)
            gate = jax.nn.softmax((x @ w_gate).mean(axis=1), axis=-1)
            ckv = _rms(x @ w_ckv, g_kvnorm)
            k_nope = (ckv @ w_dk_nope).reshape(B, T, N_HEAD, NOPE).transpose(0, 2, 1, 3)
            v1 = (ckv @ w_dv).reshape(B, T, N_HEAD, V_HEAD).transpose(0, 2, 1, 3)
            k_rope = (x @ w_krope).reshape(B, T, 1, ROPE_D).transpose(0, 2, 1, 3) / N_HEAD
            k_rope = _rope(k_rope, cos, sin)
            k1 = jnp.concatenate([k_nope, jnp.broadcast_to(k_rope, (B, N_HEAD, T, ROPE_D))], axis=-1)
            scores = (x @ w_imp)[..., 0]
            _, idx = jax.lax.top_k(scores, KEEP)
            idx = jnp.sort(idx, axis=1)
            sel = jnp.take_along_axis(x, idx[:, :, None], axis=1)
            ks = (sel @ w_selk).reshape(B, KEEP, N_HEAD, NOPE + ROPE_D).transpose(0, 2, 1, 3)
            vs = (sel @ w_selv).reshape(B, KEEP, N_HEAD, V_HEAD).transpose(0, 2, 1, 3)
            ks = jnp.concatenate([ks[..., :NOPE], _rope(ks[..., NOPE:], cos, sin)], axis=-1)
            kw = (x @ w_wink).reshape(B, T, N_HEAD, NOPE + ROPE_D).transpose(0, 2, 1, 3)
            vw = (x @ w_winv).reshape(B, T, N_HEAD, V_HEAD).transpose(0, 2, 1, 3)
            kw = jnp.concatenate([kw[..., :NOPE], _rope(kw[..., NOPE:], cos, sin)], axis=-1)
            a1 = _attn(q, k1, v1, causal=True)
            a2 = _attn(q, ks, vs, causal=False)
            a3 = _attn(q, kw, vw, causal=True)
            g = gate[:, :, None, None, None]
            out = g[:, 0] * a1 + g[:, 1] * a2 + g[:, 2] * a3
            out = out.transpose(0, 2, 1, 3).reshape(B, T, N_HEAD * V_HEAD)
            return out @ w_proj
        return _forward(x, w_cq, g_qnorm, w_dq_nope, w_dq_rope, w_ckv, g_kvnorm, w_dk_nope, w_dv, w_krope, w_imp, w_selk, w_selv, w_wink, w_winv, w_gate, w_proj)

    def _L3_ffn_ref(hidden_states, gate_w, gate_bias, expert_gate, expert_up, expert_down, shared_gate, shared_up, shared_down):
        import jax, jax.numpy as jnp
        import numpy as np
        N_EXPERTS = 32
        TOP_K = 8
        N_GROUP = 4
        TOPK_GROUP = 2
        ROUTED_SCALING = 2.5

        def _gate(x, gate_w, gate_bias):
            T, E = (x.shape[0], gate_w.shape[0])
            logits = jnp.einsum('th,eh->te', x, gate_w)
            scores = jax.nn.sigmoid(logits)
            scores_choice = scores + gate_bias[None, :]
            grp = scores_choice.reshape(T, N_GROUP, E // N_GROUP)
            top2, _ = jax.lax.top_k(grp, 2)
            group_scores = top2.sum(-1)
            _, grp_idx = jax.lax.top_k(group_scores, TOPK_GROUP)
            group_mask = jax.nn.one_hot(grp_idx, N_GROUP, dtype=scores.dtype).sum(1)
            expert_mask = jnp.repeat(group_mask, E // N_GROUP, axis=1)
            masked = jnp.where(expert_mask > 0, scores_choice, 0.0)
            _, topk_idx = jax.lax.top_k(masked, TOP_K)
            topk_w = jnp.take_along_axis(scores, topk_idx, axis=1)
            topk_w = topk_w / (topk_w.sum(-1, keepdims=True) + 1e-20)
            topk_w = topk_w * ROUTED_SCALING
            return (topk_idx, topk_w)

        def _mlp(x, wg, wu, wd):
            return jnp.einsum('...i,hi->...h', jax.nn.silu(jnp.einsum('...h,ih->...i', x, wg)) * jnp.einsum('...h,ih->...i', x, wu), wd)
        orig_shape = hidden_states.shape
        H = orig_shape[-1]
        residuals = hidden_states
        x = hidden_states.reshape(-1, H)
        topk_idx, topk_w = _gate(x, gate_w, gate_bias)
        g = jnp.einsum('th,eih->eti', x, expert_gate)
        u = jnp.einsum('th,eih->eti', x, expert_up)
        outs = jnp.einsum('eti,ehi->eth', jax.nn.silu(g) * u, expert_down)
        outs_t = jnp.transpose(outs, (1, 0, 2))
        gathered = jnp.take_along_axis(outs_t, topk_idx[:, :, None], axis=1)
        final = (gathered * topk_w[:, :, None]).sum(1)
        shared = _mlp(residuals, shared_gate, shared_up, shared_down)
        return final.reshape(orig_shape) + shared
    x = x + _L0_xattn_ref(_layernorm(x, axis=-1), ctx_1024, ctx_1024, L0_xattn_Wq, L0_xattn_Wk, L0_xattn_Wv, L0_xattn_Wo)
    x = x + _L0_attn_ref(_layernorm(x, axis=-1), L0_attn_W_in, L0_attn_b_in, L0_attn_W_x, L0_attn_b_x, L0_attn_W_dt, L0_attn_b_dt, L0_attn_A_log, L0_attn_D, L0_attn_W_out, L0_attn_b_out)
    x = x + _L0_ffn_ref(_layernorm(x, axis=-1), L0_ffn_W1, L0_ffn_b1, L0_ffn_W2, L0_ffn_b2, L0_ffn_gate_W, L0_ffn_shared_W, L0_ffn_shared_b, L0_ffn_gamma, L0_ffn_beta)
    x = x + _L1_xattn_ref(ctx_1024, _layernorm(x, axis=-1), mask_BxS2_bf1, L1_xattn_ln_x_g, L1_xattn_ln_x_b, L1_xattn_ln_l_g, L1_xattn_ln_l_b, L1_xattn_qn_g, L1_xattn_kn_g, L1_xattn_Wq, L1_xattn_Wkv, L1_xattn_Wout, L1_xattn_bout)
    x = x + _L1_attn_ref(_layernorm(x, axis=-1), L1_attn_wq, L1_attn_bq, L1_attn_wk, L1_attn_bk, L1_attn_wv, L1_attn_bv, L1_attn_wo, L1_attn_bo, L1_attn_gamma, L1_attn_beta, L1_attn_pe)
    x = x + _L1_ffn_ref(_layernorm(x, axis=-1), L1_ffn_w1_w, L1_ffn_w1_s, L1_ffn_w2_w, L1_ffn_w2_s, L1_ffn_h1_w, L1_ffn_h1_s, L1_ffn_h2_w, L1_ffn_h2_s, L1_ffn_w3_w, L1_ffn_w3_s)
    x = x + _L2_xattn_ref(_layernorm(x, axis=-1), ctx_1024, L2_xattn_w_sim, L2_xattn_b_sim, L2_xattn_W_qv, L2_xattn_b_qv)
    x = x + _L2_attn_ref(_layernorm(x, axis=-1), L2_attn_wq, L2_attn_wk, L2_attn_wv)
    x = x + _L2_ffn_ref(_layernorm(x, axis=-1), L2_ffn_w1, L2_ffn_b1, L2_ffn_w2, L2_ffn_b2)
    x = x + _L3_xattn_ref(_layernorm(x, axis=-1), ctx_1024, ctx_1024, mask_1x1xSxS2_ff0, L3_xattn_wq, L3_xattn_wk, L3_xattn_wv, L3_xattn_wo)
    x = x + _L3_attn_ref(_layernorm(x, axis=-1), L3_attn_w_cq, L3_attn_g_qnorm, L3_attn_w_dq_nope, L3_attn_w_dq_rope, L3_attn_w_ckv, L3_attn_g_kvnorm, L3_attn_w_dk_nope, L3_attn_w_dv, L3_attn_w_krope, L3_attn_w_imp, L3_attn_w_selk, L3_attn_w_selv, L3_attn_w_wink, L3_attn_w_winv, L3_attn_w_gate, L3_attn_w_proj)
    x = x + _L3_ffn_ref(_layernorm(x, axis=-1), L3_ffn_gate_w, L3_ffn_gate_bias, L3_ffn_expert_gate, L3_ffn_expert_up, L3_ffn_expert_down, L3_ffn_shared_gate, L3_ffn_shared_up, L3_ffn_shared_down)
    return x

_drawn_inputs = setup_inputs


def setup_inputs(seed=0):
    import zlib

    import numpy as np

    out = dict(_drawn_inputs(seed))
    spreads = {'L0_attn_D': (1.0, 0.2),
     'L0_ffn_b1': (0.0, 0.1),
     'L0_ffn_b2': (0.0, 0.1),
     'L0_ffn_shared_b': (0.0, 0.1),
     'L0_ffn_gamma': (1.0, 0.2),
     'L0_ffn_beta': (0.0, 0.1),
     'L1_xattn_ln_x_g': (1.0, 0.2),
     'L1_xattn_ln_x_b': (0.0, 0.1),
     'L1_xattn_ln_l_g': (1.0, 0.2),
     'L1_xattn_ln_l_b': (0.0, 0.1),
     'L1_xattn_qn_g': (1.0, 0.2),
     'L1_xattn_kn_g': (1.0, 0.2),
     'L1_xattn_bout': (0.0, 0.1),
     'L1_attn_gamma': (1.0, 0.2),
     'L1_attn_beta': (0.0, 0.1),
     'L3_attn_g_qnorm': (1.0, 0.2),
     'L3_attn_g_kvnorm': (1.0, 0.2)}
    factors = {}
    for name, (base, spread) in spreads.items():
        noise = np.random.default_rng([zlib.crc32(name.encode()), seed]).standard_normal(out[name].shape)
        drawn = base * np.exp(spread * noise) if base else spread * noise
        out[name] = jnp.asarray(drawn.astype(out[name].dtype))
    for name, factor in factors.items():
        out[name] = (out[name] * factor).astype(out[name].dtype)
    return out
```

```python
from contextlib import ExitStack, contextmanager

import numpy as np

import concourse.bass as bass
from concourse import mybir

F32 = mybir.dt.float32
ALU = mybir.AluOpType
ACT = mybir.ActivationFunctionType
AX = mybir.AxisListType

P = 128
BATCH, SEQ, D = 8, 64, 256
CTX = 1024
T = BATCH * SEQ
TT = T // P
KD = D // P
BANK = 512
LN_EPS = 1e-5

ONLY = list(range(12))


class Env:
    pass


@contextmanager
def stage(nc, *names):
    first = nc.stage_sem_base
    sems = [nc.alloc_semaphore(n, num=first + i) for i, n in enumerate(names)]
    with nc.Block() as block:
        yield (block, *sems)
    nc.all_engine_barrier(sems_to_clear=range(first, first + len(sems)))
    for s in sems:
        nc.release_semaphore(s)


def wait(eng, sem, value):
    if not isinstance(value, int) or value > 0:
        eng.wait_ge(sem, value)


class Chain:

    def __init__(self, eng, sem):
        self.eng, self.sem, self.base, self.n = eng, sem, 0, 0

    def restart(self, base):
        self.base, self.n = base, 0

    def __call__(self, ins):
        ins.then_inc(self.sem, 1)
        self.n += 1
        self.eng.wait_ge(self.sem, self.base + self.n)


def project(nc, out, weight, chunks, moving, **kw):
    for k in range(chunks):
        last = nc.tensor.matmul(out, weight(k), moving(k), start=(k == 0), stop=(k == chunks - 1), **kw)
    return last


def layernorm(nc, env, positions=None):
    with ExitStack() as mem, stage(nc, "pe_in", "normed", "stats_done", "moments_done", "std_done", "rstd_done", "h_ready",
                                   "transposed", "hT_ready") as (
            block, pe_in, normed, stats_done, moments_done, std_done, rstd_done, h_ready, transposed, hT_ready):
        sb = lambda name, shape: mem.enter_context(nc.sbuf_tensor(name, shape, F32, allow_name_mangling=True))
        stats, mv, std, rstd = (sb("ln_stats", [P, TT, 6]), sb("ln_mv", [P, TT, 2]), sb("ln_std", [P, TT]),
                                sb("ln_rstd", [P, TT]))
        pos = sb("ln_pos", [P, D])

        @block.sync
        def _(sp):
            if positions is not None:
                for i in range(2):
                    sp.dma_start(pos[i * SEQ:(i + 1) * SEQ, :], positions).then_inc(pe_in, 16)

        @block.vector
        def _(dve):
            for t in range(TT):
                nc.vector.bn_stats(stats[:, t, :], env.x[:, t, :]).then_inc(stats_done, 1)
            for t in range(TT):
                dve.wait_ge(stats_done, t + 1)
                nc.vector.bn_aggr(mv[:, t, :], stats[:, t, :]).then_inc(moments_done, 1)
            dve.wait_ge(std_done, 1)
            nc.vector.reciprocal(rstd[:], std[:]).then_inc(rstd_done, 1)
            dve.wait_ge(rstd_done, 1)
            for t in range(TT):
                nc.vector.tensor_scalar(env.h[:, t, :], env.x[:, t, :], mv[:, t, 0:1], rstd[:, t:t + 1],
                                        ALU.subtract, ALU.mult).then_inc(h_ready if positions is None else normed, 1)
                if positions is not None:
                    dve.wait_ge(pe_in, 32)
                    dve.wait_ge(normed, t + 1)
                    nc.vector.tensor_tensor(env.h[:, t, :], env.h[:, t, :], pos[:], ALU.add).then_inc(h_ready, 1)
            dve.wait_ge(transposed, 2)
            nc.vector.tensor_copy(env.hT[:, 1, :], env.ps[:, 1, :]).then_inc(hT_ready, 1)

        @block.scalar
        def _(act):
            act.wait_ge(moments_done, TT)
            nc.scalar.activation(std[:], mv[:, :, 1], ACT.Sqrt, bias=env.eps[:, 0:1]).then_inc(std_done, 1)
            act.wait_ge(transposed, 1)
            nc.scalar.copy(env.hT[:, 0, :], env.ps[:, 0, :]).then_inc(hT_ready, 1)

        @block.tensor
        def _(pe):
            pe.wait_ge(h_ready, TT)
            for k in range(KD):
                for t in range(TT):
                    last = nc.tensor.transpose(env.ps[:, k, t * P:(t + 1) * P], env.h[:, t, k * P:(k + 1) * P],
                                               env.ident[:])
                last.then_inc(transposed, 1)


HEADS, HD = 16, 16
HG = 8
GROUPS = HEADS // HG
CC = CTX // P


def sigmoid_cross_attention(nc, env, w, ctxT):
    UNITS = 8
    STEPS = CC * GROUPS
    LAG = 2
    RING = 4
    with ExitStack() as mem, stage(
            nc, "weights_in", "ctx_in0", "ctx_in1", "q_done", "q_ready", "unit_done", "unit_taken", "qbd_ready",
            "scores_done", "probs_ready", "pv_done", "masked", "o_ready", "out_done", "x_added") as (
            block, weights_in, ctx_in0, ctx_in1, q_done, q_ready, unit_done, unit_taken, qbd_ready,
            scores_done, probs_ready, pv_done, masked, o_ready, out_done, x_added):
        sb = lambda name, shape: mem.enter_context(nc.sbuf_tensor(name, shape, F32, allow_name_mangling=True))
        wq, wk, wv, wo = (sb(n, [P, KD, D]) for n in ("wq", "wk", "wv", "wo"))
        cT = sb("ctxT", [P, 2, KD, CTX])
        kT = sb("kT", [P, 2, GROUPS, CTX])
        v = sb("v", [P, 2, CC, D])
        qT = sb("qT", [P, GROUPS, T])
        qbd = sb("qbd", [P, 2, GROUPS, HG, SEQ])
        probs = sb("probs", [P, RING, BANK])
        prod = sb("prod", [P, GROUPS, 2, SEQ])
        oT = sb("oT", [P, GROUPS, T])
        ps = env.ps
        ctx_in = (ctx_in0, ctx_in1)
        O_BANK = 6

        def pairs(body, lead):
            body(0, False)
            with body.eng.Fori(1, BATCH // 2 - 1) as j:
                body(j, False)
            body(BATCH // 2 - 1, True)

        @block.sync
        def _(sp):
            for dst, src in ((wq, w["WqT"]), (wk, w["WkT"]), (wv, w["WvT"]), (wo, w["WoT"])):
                sp.dma_start(dst[:], src.rearrange("(k p) n -> p k n", p=P)).then_inc(weights_in, 16)
            for b in range(BATCH):
                wait(sp, unit_done, UNITS * (b - 1))
                sp.dma_start(cT[:, b % 2], ctxT[b].rearrange("(k p) s -> p k s", p=P)).then_inc(ctx_in[b % 2], 16)

        @block.tensor
        def _(pe):
            def proj(b, i):
                pe.wait_ge(ctx_in[i], 16 * (b // 2 + 1) if isinstance(b, int) else b * 8 + 16 - 8 * i)
                for u in range(UNITS):
                    wait(pe, unit_taken, UNITS * b + u - 1)
                    bank = u % 2
                    if u < 4:
                        g, half = u // 2, u % 2
                        last = project(nc, ps[:, bank, :], lambda k: wk[:, k, g * P:(g + 1) * P], KD,
                                       lambda k: cT[:, i, k, half * BANK:(half + 1) * BANK])
                    else:
                        for cc in range(2):
                            c = 2 * (u - 4) + cc
                            last = project(nc, ps[:, bank, cc * D:(cc + 1) * D],
                                           lambda k: cT[:, i, k, c * P:(c + 1) * P], KD, lambda k: wv[:, k, :])
                    last.then_inc(unit_done, 1)

            def attend(b, i):
                pe.wait_ge(qbd_ready, GROUPS * (b + 1))
                wait(pe, unit_taken, UNITS * (b + 1))
                for m in range(STEPS + LAG):
                    if m < STEPS:
                        c, g = m // GROUPS, m % GROUPS
                        wait(pe, probs_ready, STEPS * b + m - RING + 1)
                        nc.tensor.matmul(ps[:, 2 + m % RING, :], kT[:, i, g, c * P:(c + 1) * P],
                                         qbd[:, i, g].rearrange("p h l -> p (h l)"),
                                         start=True, stop=True).then_inc(scores_done, 1)
                    if m >= LAG:
                        n = m - LAG
                        c, g = n // GROUPS, n % GROUPS
                        pe.wait_ge(probs_ready, STEPS * b + n + 1)
                        if c == 0 and g == 0:
                            wait(pe, masked, GROUPS * b)
                        for j in range(4):
                            first = g * P + 2 * HD * j
                            last = nc.tensor.matmul(ps[32 * j:32 * j + 32, O_BANK + g, 0:P],
                                                    v[:, i, c, first:first + 2 * HD],
                                                    probs[:, n % RING, j * P:(j + 1) * P],
                                                    start=(c == 0), stop=(c == CC - 1))
                        last.then_inc(pv_done, 1)

            pe.wait_ge(weights_in, 64)
            for g in range(GROUPS):
                project(nc, ps[:, 2 + g, :], lambda k: wq[:, k, g * P:(g + 1) * P], KD,
                        lambda k: env.hT[:, k, :]).then_inc(q_done, 1)
            proj(0, 0)
            pe.wait_ge(q_ready, GROUPS)

            def pair(j, last):
                proj(2 * j + 1, 1)
                attend(2 * j, 0)
                if not last:
                    proj(2 * j + 2, 0)
                attend(2 * j + 1, 1)

            pair(0, False)
            with pe.Fori(1, BATCH // 2 - 1) as j:
                pair(j, False)
            pair(BATCH // 2 - 1, True)

            for t in range(TT):
                if t == 0:
                    pe.wait_ge(o_ready, GROUPS * BATCH)
                project(nc, ps[:, t, 0:D], lambda k: oT[:, k, t * P:(t + 1) * P], KD,
                        lambda k: wo[:, k, :]).then_inc(out_done, 1)

        @block.scalar
        def _(act):
            for g in range(GROUPS):
                act.wait_ge(q_done, g + 1)
                nc.scalar.mul(qT[:, g, :], ps[:, 2 + g, :], HD ** -0.5).then_inc(q_ready, 1)

            def sample(b):
                for m in range(STEPS):
                    act.wait_ge(scores_done, STEPS * b + m + 1)
                    wait(act, pv_done, STEPS * b + m - RING + 1)
                    nc.scalar.activation(probs[:, m % RING, :], ps[:, 2 + m % RING, :],
                                         ACT.Sigmoid).then_inc(probs_ready, 1)

            sample(0)
            with act.Fori(1, BATCH) as b:
                sample(b)

        @block.vector
        def _(dve):
            def take(b, i):
                for u in range(UNITS):
                    dve.wait_ge(unit_done, UNITS * b + u + 1)
                    if u == 0:
                        if isinstance(b, int) and b == 0:
                            dve.wait_ge(q_ready, GROUPS)
                        for g in range(GROUPS):
                            nc.vector.tensor_tensor(
                                qbd[:, i, g], qT[:, g, bass.ds(b * SEQ, SEQ)].unsqueeze(1).broadcast_to([P, HG, SEQ]),
                                env.head_mask[:].unsqueeze(2).broadcast_to([P, HG, SEQ]),
                                ALU.mult).then_inc(qbd_ready, 1)
                    if u < 4:
                        dst = kT[:, i, u // 2, (u % 2) * BANK:(u % 2 + 1) * BANK]
                    else:
                        dst = v[:, i, 2 * (u - 4):2 * (u - 4) + 2, :].rearrange("p c n -> p (c n)")
                    nc.vector.tensor_copy(dst, ps[:, u % 2, :]).then_inc(unit_taken, 1)

            def extract(b):
                dve.wait_ge(pv_done, STEPS * (b + 1))
                for g in range(GROUPS):
                    wait(dve, o_ready, GROUPS * b)
                    nc.vector.tensor_tensor(prod[:, g], ps[:, O_BANK + g, 0:P].rearrange("p (h l) -> p h l", h=2),
                                            env.pair_mask[:].unsqueeze(2).broadcast_to([P, 2, SEQ]),
                                            ALU.mult).then_inc(masked, 1)
                for g in range(GROUPS):
                    dve.wait_ge(masked, GROUPS * b + g + 1)
                    nc.vector.tensor_tensor(oT[:, g, bass.ds(b * SEQ, SEQ)], prod[:, g, 0, :], prod[:, g, 1, :],
                                            ALU.add).then_inc(o_ready, 1)

            def pair(j, last):
                take(2 * j + 1, 1)
                extract(2 * j)
                if not last:
                    take(2 * j + 2, 0)
                extract(2 * j + 1)

            take(0, 0)
            pair(0, False)
            with dve.Fori(1, BATCH // 2 - 1) as j:
                pair(j, False)
            pair(BATCH // 2 - 1, True)
            for t in range(TT):
                dve.wait_ge(out_done, t + 1)
                nc.vector.tensor_tensor(env.x[:, t, :], env.x[:, t, :], ps[:, t, 0:D],
                                        ALU.add).then_inc(x_added, 1)


def project_out(nc, env, pe, oT, wo, chunks, out_done, bias=None):
    for t in range(TT):
        if bias is not None:
            nc.tensor.matmul(env.ps[:, t, 0:D], env.ones[0:1, 0:P], bias, start=True, stop=False)
        for k in range(chunks):
            last = nc.tensor.matmul(env.ps[:, t, 0:D], oT[:, k, t * P:(t + 1) * P], wo[:, k, :],
                                    start=(k == 0 and bias is None), stop=(k == chunks - 1))
        last.then_inc(out_done, 1)


def add_out(nc, env, dve, out_done, x_added):
    for t in range(TT):
        dve.wait_ge(out_done, t + 1)
        nc.vector.tensor_tensor(env.x[:, t, :], env.x[:, t, :], env.ps[:, t, 0:D], ALU.add).then_inc(x_added, 1)


def allocator(nc, mem):
    return lambda name, shape: mem.enter_context(nc.sbuf_tensor(name, shape, F32, allow_name_mangling=True))


def rows_of(ap, n=P):
    return ap.partition_broadcast(n)


def normalize_rows(nc, env, link, src, dst, stats, mv, std, moments_done, std_done, dve,
                   gamma=None, beta=None):
    for t in range(TT):
        link(nc.vector.bn_stats(stats[:, t, :], src[:, t, :]))
    for t in range(TT):
        nc.vector.bn_aggr(mv[:, t, :], stats[:, t, :]).then_inc(moments_done, 1)
    dve.wait_ge(std_done, 1)
    link(nc.vector.reciprocal(std[:], std[:]))
    for t in range(TT):
        link(nc.vector.tensor_scalar(dst[:, t, :], src[:, t, :], mv[:, t, 0:1], std[:, t:t + 1],
                                     ALU.subtract, ALU.mult))
        if gamma is not None:
            link(nc.vector.tensor_tensor(dst[:, t, :], dst[:, t, :], gamma, ALU.mult))
            link(nc.vector.tensor_tensor(dst[:, t, :], dst[:, t, :], beta, ALU.add))


def moe_top2(nc, env, ins):
    E, HID = 8, 1024
    HC = HID // P
    PAD = 6
    with ExitStack() as mem, stage(
            nc, "consts_in", "norm_in", "expert_in0", "expert_in1", "gate_done", "exp_done", "vstep", "combine_ready",
            "shared_done", "shared_gelu", "up_done", "gelu_done", "down_done", "down_taken", "moments_done",
            "std_done", "astep") as (
            block, consts_in, norm_in, expert_in0, expert_in1, gate_done, exp_done, vstep, combine_ready,
            shared_done, shared_gelu, up_done, gelu_done, down_done, down_taken, moments_done, std_done, astep):
        sb = allocator(nc, mem)
        ps = env.ps
        w1 = sb("w1", [P, 2, KD, HID])
        w2 = sb("w2", [P, 2, HC, D])
        b1, b2 = sb("b1", [P, E, HC]), sb("b2", [1, E, D])
        hid = sb("hid", [P, 2, HC, T])
        gw, ws, bs = sb("gate_w", [P, KD, E]), sb("shared_w", [P, KD, D]), sb("shared_b", [1, D])
        gamma, beta = sb("gamma", [P, D]), sb("beta", [P, D])
        acc = sb("acc", [P, TT, D])
        probs = sb("probs", [P, TT, E + PAD])
        top, rest = sb("top", [P, TT, 8]), sb("rest", [P, TT, E + PAD])
        neg_max, total, combine = sb("neg_max", [P, TT]), sb("total", [P, TT]), sb("combine", [P, TT, E])
        stats, mv, std = sb("stats", [P, TT, 6]), sb("mv", [P, TT, 2]), sb("std", [P, TT])
        expert_in = (expert_in0, expert_in1)

        @block.sync
        def _(sp):
            sp.dma_start(gw[:], ins["L0_ffn_gate_W"].rearrange("(k p) e -> p k e", p=P)).then_inc(consts_in, 16)
            sp.dma_start(ws[:], ins["L0_ffn_shared_W"].rearrange("(k p) n -> p k n", p=P)).then_inc(consts_in, 16)
            sp.dma_start(bs[:], ins["L0_ffn_shared_b"].unsqueeze(0)).then_inc(consts_in, 16)
            sp.dma_start(b1[:], ins["L0_ffn_b1"]).then_inc(consts_in, 16)
            sp.dma_start(b2[:], ins["L0_ffn_b2"].unsqueeze(0)).then_inc(consts_in, 16)
            for e in range(E):
                wait(sp, down_done, TT * (e - 1))
                sp.dma_start(w1[:, e % 2], ins["L0_ffn_W1"][e].rearrange("(k p) n -> p k n", p=P))\
                    .then_inc(expert_in[e % 2], 16)
                sp.dma_start(w2[:, e % 2], ins["L0_ffn_W2"][e].rearrange("(k p) n -> p k n", p=P))\
                    .then_inc(expert_in[e % 2], 16)
                if e == 1:
                    sp.dma_start(gamma[:], rows_of(ins["L0_ffn_gamma"])).then_inc(norm_in, 16)
                    sp.dma_start(beta[:], rows_of(ins["L0_ffn_beta"])).then_inc(norm_in, 16)

        @block.tensor
        def _(pe):
            pe.wait_ge(consts_in, 80)
            for t in range(TT):
                last = project(nc, ps[:, 4, t * E:(t + 1) * E], lambda k: env.hT[:, k, t * P:(t + 1) * P], KD,
                               lambda k: gw[:, k, :])
            last.then_inc(gate_done, 1)
            for t in range(TT):
                nc.tensor.matmul(ps[:, t, 0:D], env.ones[0:1, 0:P], bs[:], start=True, stop=False)
                for k in range(KD):
                    last = nc.tensor.matmul(ps[:, t, 0:D], env.hT[:, k, t * P:(t + 1) * P], ws[:, k, :],
                                            start=False, stop=(k == KD - 1))
                last.then_inc(shared_done, 1)
            pe.wait_ge(shared_gelu, TT)

            def up(e, i):
                pe.wait_ge(expert_in[i], e * 16 + 32 - 16 * i)
                for u in range(HC):
                    wait(pe, gelu_done, HC * e + u - 3)
                    project(nc, ps[:, u % 4, :], lambda k: w1[:, i, k, u * P:(u + 1) * P], KD,
                            lambda k: env.hT[:, k, :]).then_inc(up_done, 1)

            def down(e, i):
                wait(pe, gelu_done, HC * (e + 1))
                for t in range(TT):
                    wait(pe, down_taken, TT * e + t - 3)
                    for k in range(HC):
                        nc.tensor.matmul(ps[:, 4 + t, 0:D], hid[:, i, k, t * P:(t + 1) * P], w2[:, i, k, :],
                                         start=(k == 0), stop=False)
                    last = nc.tensor.matmul(ps[:, 4 + t, 0:D], env.ones[0:1, 0:P], b2[0:1, bass.ds(e, 1), :].rearrange(
                        "p e n -> p (e n)"), start=False, stop=True)
                    last.then_inc(down_done, 1)

            def pair(j, last):
                up(2 * j + 1, 1)
                down(2 * j, 0)
                if not last:
                    up(2 * j + 2, 0)
                down(2 * j + 1, 1)

            up(0, 0)
            pe.wait_ge(combine_ready, 1)
            pair(0, False)
            with pe.Fori(1, E // 2 - 1) as j:
                pair(j, False)
            pair(E // 2 - 1, True)

        @block.scalar
        def _(act):
            act.wait_ge(vstep, 1)
            for t in range(TT):
                nc.scalar.activation(probs[:, t, 0:E], ps[:, 4, t * E:(t + 1) * E], ACT.Exp,
                                     bias=neg_max[:, t:t + 1]).then_inc(exp_done, 1)
            for t in range(TT):
                act.wait_ge(shared_done, t + 1)
                nc.scalar.activation(acc[:, t, :], ps[:, t, 0:D], ACT.Gelu).then_inc(shared_gelu, 1)

            def gelus(e, i):
                for u in range(HC):
                    act.wait_ge(up_done, HC * e + u + 1)
                    nc.scalar.activation(hid[:, i, u, :], ps[:, u % 4, :], ACT.Gelu,
                                         bias=b1[:, bass.ds(e, 1), u:u + 1].rearrange("p e u -> p (e u)"))\
                        .then_inc(gelu_done, 1)

            gelus(0, 0)
            with act.Fori(0, E // 2 - 1) as j:
                gelus(2 * j + 1, 1)
                gelus(2 * j + 2, 0)
            gelus(E - 1, 1)
            act.wait_ge(moments_done, TT)
            nc.scalar.activation(std[:], mv[:, :, 1], ACT.Sqrt, bias=env.eps[:, 0:1]).then_inc(std_done, 1)

        @block.vector
        def _(dve):
            link = Chain(dve, vstep)
            dve.wait_ge(gate_done, 1)
            link(nc.vector.tensor_reduce(neg_max[:], ps[:, 4, 0:TT * E].rearrange("p (t e) -> p t e", t=TT),
                                         AX.X, ALU.max, negate=True))
            link(nc.vector.memset(probs[:, :, E:], -1.0))
            dve.wait_ge(exp_done, TT)
            for t in range(TT):
                link(nc.vector.max(top[:, t, :], probs[:, t, :]))
            link(nc.vector.memset(top[:, :, 2:8], -1.0))
            for t in range(TT):
                link(nc.vector.match_replace(rest[:, t, :], top[:, t, :], probs[:, t, :], -2.0))
            link(nc.vector.tensor_tensor(total[:], top[:, :, 0], top[:, :, 1], ALU.add))
            link(nc.vector.reciprocal(total[:], total[:]))
            link(nc.vector.tensor_scalar(rest[:, :, 0:E], rest[:, :, 0:E], -1.5, None, ALU.is_lt))
            link(nc.vector.tensor_tensor(combine[:], rest[:, :, 0:E], probs[:, :, 0:E], ALU.mult))
            link(nc.vector.tensor_tensor(combine[:], combine[:], total[:].unsqueeze(2).broadcast_to([P, TT, E]),
                                         ALU.mult))
            dve.wait_ge(shared_gelu, TT)
            link(nc.vector.tensor_scalar(acc[:], acc[:], 0.5, None, ALU.mult))
            nc.vector.engine_nop().then_inc(combine_ready, 1)

            def take(e):
                for t in range(TT):
                    dve.wait_ge(down_done, TT * e + t + 1)
                    wait(dve, down_taken, TT * e + t - 3)
                    nc.vector.scalar_tensor_tensor(out=acc[:, t, :], in0=ps[:, 4 + t, 0:D],
                                                   scalar=combine[:, t, bass.ds(e, 1)], in1=acc[:, t, :],
                                                   op0=ALU.mult, op1=ALU.add).then_inc(down_taken, 1)

            take(0)
            with dve.Fori(1, E) as e:
                take(e)
            dve.wait_ge(down_taken, TT * E)
            dve.wait_ge(norm_in, 32)
            normalize_rows(nc, env, link, acc, acc, stats, mv, std, moments_done, std_done, dve,
                           gamma[:], beta[:])
            link(nc.vector.tensor_tensor(env.x[:], env.x[:], acc[:], ALU.add))


def grouped_moe(nc, env, ins):
    E, GR, HID = 32, 4, 128
    ALL = E + 2
    EG = E // GR
    PAD = 6
    NONE = -1e30
    with ExitStack() as mem, stage(
            nc, "consts_in", "expert_in0", "expert_in1", "gate_done", "scores_ready", "vstep", "combine_ready",
            "up_done", "silu_done", "hid_ready", "down_done", "down_taken", "weights_used") as (
            block, consts_in, expert_in0, expert_in1, gate_done, scores_ready, vstep, combine_ready,
            up_done, silu_done, hid_ready, down_done, down_taken, weights_used):
        sb = allocator(nc, mem)
        ps = env.ps
        wg, wu, wd = sb("wg", [P, 2, KD, HID]), sb("wu", [P, 2, KD, HID]), sb("wd", [P, 2, D])
        gw, bias = sb("gate_w", [P, KD, E]), sb("gate_bias", [P, E])
        silu, hid = sb("silu", [P, 2, T]), sb("hid", [P, 2, T])
        scores, choice, rest = sb("scores", [P, TT, E]), sb("choice", [P, TT, E]), sb("rest", [P, TT, E])
        top = sb("top", [P, TT, GR, 8])
        group, gtop, grest = sb("group", [P, TT, GR + PAD]), sb("gtop", [P, TT, 8]), sb("grest", [P, TT, GR + PAD])
        total, combine = sb("total", [P, TT]), sb("combine", [P, TT, ALL])
        expert_in = (expert_in0, expert_in1)

        @block.sync
        def _(sp):
            sp.dma_start(gw[:], ins["L3_ffn_gate_wT"].rearrange("(k p) e -> p k e", p=P)).then_inc(consts_in, 16)
            sp.dma_start(bias[:], rows_of(ins["L3_ffn_gate_bias"])).then_inc(consts_in, 16)

            def load(e, i):
                wait(sp, down_done, TT * e - TT)
                sp.dma_start(wg[:, i], ins["L3_ffn_gateT"][bass.ds(e, 1)].rearrange("e (k p) n -> p (e k) n", p=P))\
                    .then_inc(expert_in[i], 16)
                sp.dma_start(wu[:, i], ins["L3_ffn_upT"][bass.ds(e, 1)].rearrange("e (k p) n -> p (e k) n", p=P))\
                    .then_inc(expert_in[i], 16)
                sp.dma_start(wd[:, i], ins["L3_ffn_downT"][bass.ds(e, 1)].rearrange("e p n -> p (e n)"))\
                    .then_inc(expert_in[i], 16)

            load(0, 0)
            load(1, 1)
            with sp.Fori(1, ALL // 2) as j:
                load(2 * j, 0)
                load(2 * j + 1, 1)

        @block.tensor
        def _(pe):
            pe.wait_ge(consts_in, 32)
            for t in range(TT):
                last = project(nc, ps[:, 4, t * E:(t + 1) * E], lambda k: env.hT[:, k, t * P:(t + 1) * P], KD,
                               lambda k: gw[:, k, :])
            last.then_inc(gate_done, 1)

            def up(e, i):
                pe.wait_ge(expert_in[i], e * 24 + 48 - 24 * i)
                wait(pe, hid_ready, e - 1)
                project(nc, ps[:, 2 * i, :], lambda k: wg[:, i, k, :], KD, lambda k: env.hT[:, k, :])\
                    .then_inc(up_done, 1)
                project(nc, ps[:, 2 * i + 1, :], lambda k: wu[:, i, k, :], KD, lambda k: env.hT[:, k, :])\
                    .then_inc(up_done, 1)

            def down(e, i):
                wait(pe, hid_ready, e + 1)
                for t in range(TT):
                    wait(pe, down_taken, TT * e + t - 3)
                    nc.tensor.matmul(ps[:, 4 + t, 0:D], hid[:, i, t * P:(t + 1) * P], wd[:, i, :],
                                     start=True, stop=True).then_inc(down_done, 1)

            def pair(j, last):
                up(2 * j + 1, 1)
                down(2 * j, 0)
                if not last:
                    up(2 * j + 2, 0)
                down(2 * j + 1, 1)

            up(0, 0)
            pe.wait_ge(combine_ready, 1)
            pair(0, False)
            with pe.Fori(1, ALL // 2 - 1) as j:
                pair(j, False)
            pair(ALL // 2 - 1, True)

        @block.scalar
        def _(act):
            act.wait_ge(gate_done, 1)
            nc.scalar.activation(scores[:], ps[:, 4, 0:TT * E].rearrange("p (t e) -> p t e", t=TT),
                                 ACT.Sigmoid).then_inc(scores_ready, 1)

            def silus(e, i):
                act.wait_ge(up_done, 2 * e + 1)
                wait(act, hid_ready, e - 1)
                nc.scalar.activation(silu[:, i, :], ps[:, 2 * i, :], ACT.Silu).then_inc(silu_done, 1)

            silus(0, 0)
            silus(1, 1)
            with act.Fori(1, ALL // 2) as j:
                silus(2 * j, 0)
                silus(2 * j + 1, 1)

        @block.vector
        def _(dve):
            link = Chain(dve, vstep)

            def gating():
                dve.wait_ge(scores_ready, 1)
                dve.wait_ge(consts_in, 32)
                link(nc.vector.memset(group[:, :, GR:], NONE))
                link(nc.vector.tensor_tensor(choice[:], scores[:], bias[:].unsqueeze(1).broadcast_to([P, TT, E]),
                                             ALU.add))
                for t in range(TT):
                    for g in range(GR):
                        ins_ = nc.vector.max(top[:, t, g, :], choice[:, t, g * EG:(g + 1) * EG])
                        if t < TT - 1 or g < GR - 1:
                            ins_.then_inc(vstep, 1)
                            link.n += 1
                        else:
                            link(ins_)
                link(nc.vector.tensor_tensor(group[:, :, 0:GR], top[:, :, :, 0], top[:, :, :, 1], ALU.add))
                for t in range(TT):
                    link(nc.vector.max(gtop[:, t, :], group[:, t, :]))
                link(nc.vector.memset(gtop[:, :, 2:8], NONE))
                for t in range(TT):
                    link(nc.vector.match_replace(grest[:, t, :], gtop[:, t, :], group[:, t, :], 2 * NONE))
                link(nc.vector.tensor_scalar(grest[:, :, 0:GR], grest[:, :, 0:GR], 1.5 * NONE, None, ALU.is_lt))
                link(nc.vector.tensor_tensor(
                    choice[:].rearrange("p t (g e) -> p t g e", g=GR), choice[:].rearrange("p t (g e) -> p t g e", g=GR),
                    grest[:, :, 0:GR].unsqueeze(3).broadcast_to([P, TT, GR, EG]), ALU.mult))
                for t in range(TT):
                    link(nc.vector.max(gtop[:, t, :], choice[:, t, :]))
                    link(nc.vector.match_replace(rest[:, t, :], gtop[:, t, :], choice[:, t, :], NONE))
                link(nc.vector.tensor_scalar(rest[:], rest[:], 0.5 * NONE, None, ALU.is_lt))
                link(nc.vector.tensor_tensor(scores[:], scores[:], rest[:], ALU.mult))
                link(nc.vector.tensor_reduce(total[:], scores[:], AX.X, ALU.add))
                link(nc.vector.tensor_scalar(total[:], total[:], 1e-20, None, ALU.add))
                link(nc.vector.reciprocal(total[:], total[:]))
                link(nc.vector.tensor_tensor(combine[:, :, 0:E], scores[:],
                                             total[:].unsqueeze(2).broadcast_to([P, TT, E]), ALU.mult))
                link(nc.vector.tensor_scalar(combine[:, :, 0:E], combine[:, :, 0:E], 2.5, None, ALU.mult))
                nc.vector.memset(combine[:, :, E:ALL], 1.0).then_inc(combine_ready, 1)
                dve.wait_ge(combine_ready, 1)

            def hidden(e, i):
                dve.wait_ge(silu_done, e + 1)
                dve.wait_ge(up_done, 2 * e + 2)
                wait(dve, down_done, TT * e - TT)
                nc.vector.tensor_tensor(hid[:, i, :], ps[:, 2 * i + 1, :], silu[:, i, :], ALU.mult)\
                    .then_inc(hid_ready, 1)

            def take(e):
                for t in range(TT):
                    dve.wait_ge(down_done, TT * e + t + 1)
                    wait(dve, down_taken, TT * e + t - 3)
                    nc.vector.scalar_tensor_tensor(out=env.x[:, t, :], in0=ps[:, 4 + t, 0:D],
                                                   scalar=combine[:, t, bass.ds(e, 1)], in1=env.x[:, t, :],
                                                   op0=ALU.mult, op1=ALU.add).then_inc(down_taken, 1)

            def pair(j, last):
                hidden(2 * j + 1, 1)
                take(2 * j)
                if not last:
                    hidden(2 * j + 2, 0)
                take(2 * j + 1)

            gating()
            hidden(0, 0)
            pair(0, False)
            with dve.Fori(1, ALL // 2 - 1) as j:
                pair(j, False)
            pair(ALL // 2 - 1, True)


def ternary_mlp(nc, env, ins):
    HID = 1024
    HC = HID // P
    with ExitStack() as mem, stage(
            nc, "scales_in", "w12_in", "h1_in", "h2_in", "w3_in", "up_done", "silu_done", "a_ready", "h1_done",
            "b_ready", "h2_done", "c_ready", "out_done", "scaled", "x_added") as (
            block, scales_in, w12_in, h1_in, h2_in, w3_in, up_done, silu_done, a_ready, h1_done,
            b_ready, h2_done, c_ready, out_done, scaled, x_added):
        sb = allocator(nc, mem)
        ps = env.ps
        w1, w2 = sb("w1", [P, HC, KD, P]), sb("w2", [P, HC, KD, P])
        h1, h2 = sb("h1", [P, HC, HC, P]), sb("h2", [P, HC, HC, P])
        w3 = sb("w3", [P, HC, D])
        scales, s3 = sb("scales", [P, 4, HC]), sb("s3", [P, D])
        silu = sb("silu", [P, 2, T])
        a, b = sb("a", [P, HC, T]), sb("b", [P, HC, T])
        tmp = sb("tmp", [P, TT, D])

        @block.sync
        def _(sp):
            sp.dma_start(scales[:], ins["L1_ffn_scales"]).then_inc(scales_in, 16)
            sp.dma_start(s3[:], rows_of(ins["L1_ffn_w3_s"])).then_inc(scales_in, 16)
            for o in range(HC):
                sp.dma_start(w1[:, o], ins["L1_ffn_w1"][o]).then_inc(w12_in, 16)
                sp.dma_start(w2[:, o], ins["L1_ffn_w2"][o]).then_inc(w12_in, 16)
            for o in range(HC):
                sp.dma_start(h1[:, o], ins["L1_ffn_h1"][o]).then_inc(h1_in, 16)
            for o in range(HC):
                sp.dma_start(h2[:, o], ins["L1_ffn_h2"][o]).then_inc(h2_in, 16)
            sp.dma_start(w3[:], ins["L1_ffn_w3T"].rearrange("(k p) n -> p k n", p=P)).then_inc(w3_in, 16)

        @block.tensor
        def _(pe):
            pe.wait_ge(w12_in, 32 * HC)
            for o in range(HC):
                wait(pe, a_ready, o - 1)
                for s, w in enumerate((w1, w2)):
                    project(nc, ps[:, 2 * (o % 2) + s, :], lambda k: w[:, o, k, :], KD, lambda k: env.hT[:, k, :])\
                        .then_inc(up_done, 1)
            for base, w, w_in, src, ready, done, taken in ((4, h1, h1_in, a, a_ready, h1_done, b_ready),
                                                           (0, h2, h2_in, b, b_ready, h2_done, c_ready)):
                pe.wait_ge(w_in, 16 * HC)
                pe.wait_ge(ready, HC)
                for o in range(HC):
                    wait(pe, taken, o - 3)
                    project(nc, ps[:, base + o % 4, :], lambda k: w[:, o, k, :], HC, lambda k: src[:, k, :])\
                        .then_inc(done, 1)
            pe.wait_ge(w3_in, 16)
            pe.wait_ge(c_ready, HC)
            project_out(nc, env, pe, a, w3, HC, out_done)

        @block.scalar
        def _(act):
            act.wait_ge(scales_in, 32)
            for o in range(HC):
                act.wait_ge(up_done, 2 * o + 1)
                wait(act, a_ready, o - 1)
                nc.scalar.activation(silu[:, o % 2, :], ps[:, 2 * (o % 2), :], ACT.Silu,
                                     scale=scales[:, 0, o:o + 1]).then_inc(silu_done, 1)
            for base, s, dst, done, ready in ((4, 2, b, h1_done, b_ready), (0, 3, a, h2_done, c_ready)):
                for o in range(HC):
                    act.wait_ge(done, o + 1)
                    if s == 3 and o == 0:
                        act.wait_ge(h1_done, HC)
                    nc.scalar.activation(dst[:, o, :], ps[:, base + o % 4, :], ACT.Gelu,
                                         scale=scales[:, s, o:o + 1]).then_inc(ready, 1)

        @block.vector
        def _(dve):
            dve.wait_ge(scales_in, 32)
            for o in range(HC):
                dve.wait_ge(silu_done, o + 1)
                dve.wait_ge(up_done, 2 * o + 2)
                nc.vector.scalar_tensor_tensor(out=a[:, o, :], in0=ps[:, 2 * (o % 2) + 1, :],
                                               scalar=scales[:, 1, o:o + 1], in1=silu[:, o % 2, :],
                                               op0=ALU.mult, op1=ALU.mult).then_inc(a_ready, 1)
            for t in range(TT):
                dve.wait_ge(out_done, t + 1)
                nc.vector.tensor_tensor(tmp[:, t, :], ps[:, t, 0:D], s3[:], ALU.mult).then_inc(scaled, 1)
                dve.wait_ge(scaled, t + 1)
                nc.vector.tensor_tensor(env.x[:, t, :], env.x[:, t, :], tmp[:, t, :], ALU.add).then_inc(x_added, 1)


def binary_mlp(nc, env, ins):
    HID = 1024
    HC = HID // P
    with ExitStack() as mem, stage(
            nc, "w1_in", "w2_in", "vstep", "signed1", "signed2", "bw1_ready", "bw2_ready", "turned1", "turned2",
            "w1T_ready", "w2T_ready", "up_done", "gelu_done", "out_done", "x_added", "vstep2") as (
            block, w1_in, w2_in, vstep, signed1, signed2, bw1_ready, bw2_ready, turned1, turned2,
            w1T_ready, w2T_ready, up_done, gelu_done, out_done, x_added, vstep2):
        sb = allocator(nc, mem)
        ps = env.ps
        w1, sg1 = sb("w1", [P, HC, D]), sb("sg1", [P, HC, D])
        w2, sg2 = sb("w2", [P, KD, HID]), sb("sg2", [P, KD, HID])
        w1T, w2T = sb("w1T", [P, KD, HID]), sb("w2T", [P, HC, D])
        b1, b2 = sb("b1", [P, HC]), sb("b2", [1, D])
        alpha1, alpha2 = sb("alpha1", [P, HC]), sb("alpha2", [P, KD])
        hid = sb("hid", [P, HC, T])

        @block.sync
        def _(sp):
            sp.dma_start(w1[:], ins["L2_ffn_w1"].rearrange("(o p) n -> p o n", p=P)).then_inc(w1_in, 16)
            sp.dma_start(w2[:], ins["L2_ffn_w2"].rearrange("(o p) n -> p o n", p=P)).then_inc(w2_in, 16)
            sp.dma_start(b1[:], ins["L2_ffn_b1"]).then_inc(w2_in, 16)
            sp.dma_start(b2[:], ins["L2_ffn_b2"].unsqueeze(0)).then_inc(w2_in, 16)

        @block.scalar
        def _(act):
            act.wait_ge(w1_in, 16)
            nc.scalar.activation(sg1[:], w1[:], ACT.Sign).then_inc(signed1, 1)
            act.wait_ge(w2_in, 48)
            nc.scalar.activation(sg2[:], w2[:], ACT.Sign).then_inc(signed2, 1)
            for n in range(4):
                act.wait_ge(turned1, n + 1)
                nc.scalar.copy(w1T[:, n // 2, (n % 2) * BANK:(n % 2 + 1) * BANK], ps[:, n, :]).then_inc(w1T_ready, 1)
            for o in range(HC):
                act.wait_ge(up_done, o + 1)
                nc.scalar.activation(hid[:, o, :], ps[:, o % 4, :], ACT.Gelu, bias=b1[:, o:o + 1])\
                    .then_inc(gelu_done, 1)

        @block.vector
        def _(dve):
            link = Chain(dve, vstep)
            for w, sg, alpha, rows, cols, w_in, n_in, signed, ready in (
                    (w1, sg1, alpha1, HC, D, w1_in, 16, signed1, bw1_ready),
                    (w2, sg2, alpha2, KD, HID, w2_in, 48, signed2, bw2_ready)):
                dve.wait_ge(w_in, n_in)
                link(nc.vector.tensor_reduce(alpha[:], w[:], AX.X, ALU.add, apply_absolute_value=True))
                link(nc.vector.tensor_scalar(alpha[:], alpha[:], 1.0 / cols, None, ALU.mult))
                dve.wait_ge(signed, 1)
                for r in range(rows):
                    link(nc.vector.scalar_tensor_tensor(out=sg[:, r, :], in0=sg[:, r, :], scalar=alpha[:, r:r + 1],
                                                        in1=w[:, r, :], op0=ALU.mult, op1=ALU.subtract))
                    nc.vector.tensor_tensor(w[:, r, :], w[:, r, :], sg[:, r, :], ALU.add).then_inc(ready, 1)
            for n in range(4):
                dve.wait_ge(turned2, n + 1)
                nc.vector.tensor_copy(w2T[:, 2 * n:2 * n + 2, :].rearrange("p c n -> p (c n)"), ps[:, 4 + n, :])\
                    .then_inc(w2T_ready, 1)
            add_out(nc, env, dve, out_done, x_added)

        @block.tensor
        def _(pe):
            pe.wait_ge(bw1_ready, HC)
            for n in range(4):
                k, half = n // 2, n % 2
                for o in range(4):
                    last = nc.tensor.transpose(ps[:, n, o * P:(o + 1) * P], w1[:, 4 * half + o, k * P:(k + 1) * P],
                                               env.ident[:])
                last.then_inc(turned1, 1)
            pe.wait_ge(bw2_ready, KD)
            for n in range(4):
                for c in range(2):
                    for r in range(KD):
                        last = nc.tensor.transpose(ps[:, 4 + n, c * D + r * P:c * D + (r + 1) * P],
                                                   w2[:, r, (2 * n + c) * P:(2 * n + c + 1) * P], env.ident[:])
                last.then_inc(turned2, 1)
            pe.wait_ge(w1T_ready, 4)
            for o in range(HC):
                wait(pe, gelu_done, o - 3)
                project(nc, ps[:, o % 4, :], lambda k: w1T[:, k, o * P:(o + 1) * P], KD, lambda k: env.hT[:, k, :])\
                    .then_inc(up_done, 1)
            pe.wait_ge(w2T_ready, 4)
            pe.wait_ge(gelu_done, HC)
            project_out(nc, env, pe, hid, w2T, HC, out_done, b2[:])


def selective_scan(nc, env, ins):
    INNER, STATES, RANK = 512, 16, 16
    IC = INNER // P
    R = RANK + 2 * STATES
    PT = SEQ + 1
    with ExitStack() as mem, stage(
            nc, "consts_in", "w_in_in", "proj_done", "x_ready", "z_ready", "dbc_done", "dbc_ready", "dt_done",
            "astep", "dstep", "A_ready", "delta_ready", "dtx_ready", "row_ready", "spread_done", "B_ready", "dA_ready",
            "u_ready", "scanned", "prod_ready", "y_done", "y_ready", "out_done", "x_added", "pads_set") as (
            block, consts_in, w_in_in, proj_done, x_ready, z_ready, dbc_done, dbc_ready, dt_done,
            astep, dstep, A_ready, delta_ready, dtx_ready, row_ready, spread_done, B_ready, dA_ready,
            u_ready, scanned, prod_ready, y_done, y_ready, out_done, x_added, pads_set):
        sb = allocator(nc, mem)
        ps = env.ps
        w_in, b_in = sb("w_in", [P, KD, 2 * INNER]), sb("b_in", [P, 2 * IC])
        w_x, b_x = sb("w_x", [P, IC, R]), sb("b_x", [R, 1])
        w_dt, b_dt = sb("w_dt", [RANK, INNER]), sb("b_dt", [P, IC])
        A, Dskip = sb("A", [P, IC, STATES]), sb("Dskip", [P, IC])
        w_out, b_out = sb("w_out", [P, IC, D]), sb("b_out", [1, D])
        pick = sb("pick", [P, 2 * STATES])
        xT, zT = sb("xT", [P, IC, T]), sb("zT", [P, IC, T])
        dbc = sb("dbc", [P, T])
        mag, delta, dtx = sb("mag", [P, IC, T]), sb("delta", [P, IC, T]), sb("dtx", [P, IC, T])
        row = sb("row", [P, 2, 2, T])
        B_all = sb("B_all", [P, 2, T])
        dA, u = sb("dA", [P, 2, IC, BATCH, PT]), sb("u", [P, 2, IC, BATCH, PT])
        state = sb("state", [P, IC, BATCH, PT])
        prod = sb("prod", [P, 2, IC, T])
        by_sample = lambda ap: ap.rearrange("p (b t) -> p b t", b=BATCH)
        flat = lambda ap: ap.rearrange("p b t -> p (b t)")

        @block.sync
        def _(sp):
            sp.dma_start(w_in[:], ins["L0_attn_W_inT"].rearrange("(k p) n -> p k n", p=P)).then_inc(w_in_in, 16)
            sp.dma_start(b_in[:], ins["L0_attn_b_in"]).then_inc(w_in_in, 16)
            for dst, src in ((w_x, ins["L0_attn_W_xT"].rearrange("(k p) n -> p k n", p=P)),
                             (b_x, ins["L0_attn_b_x"].unsqueeze(1)), (w_dt, ins["L0_attn_W_dtT"]),
                             (b_dt, ins["L0_attn_b_dt"]), (A, ins["L0_attn_A_log"].rearrange("(k p) n -> p k n", p=P)),
                             (Dskip, ins["L0_attn_D"]),
                             (w_out, ins["L0_attn_W_outT"].rearrange("(k p) n -> p k n", p=P)),
                             (b_out, ins["L0_attn_b_out"].unsqueeze(0)), (pick, env.consts["pick"])):
                sp.dma_start(dst[:], src).then_inc(consts_in, 16)

        @block.tensor
        def _(pe):
            pe.wait_ge(w_in_in, 32)
            for o in range(2 * IC):
                project(nc, ps[:, o, :], lambda k: w_in[:, k, o * P:(o + 1) * P], KD, lambda k: env.hT[:, k, :])\
                    .then_inc(proj_done, 1)
            pe.wait_ge(consts_in, 144)
            pe.wait_ge(x_ready, IC)
            project(nc, ps[0:R, 0, :], lambda k: w_x[:, k, :], IC, lambda k: xT[:, k, :]).then_inc(dbc_done, 1)
            pe.wait_ge(dbc_ready, 1)
            pe.wait_ge(z_ready, IC)
            for c in range(IC):
                nc.tensor.matmul(ps[:, 4 + c, :], w_dt[:, c * P:(c + 1) * P], dbc[0:RANK, :],
                                 start=True, stop=True).then_inc(dt_done, 1)

            def state_step(n, i, first=False, last=False):
                for s in range(2):
                    pe.wait_ge(row_ready, 2 * n + s + 1)
                    if s == 0:
                        wait(pe, B_ready, n - 1)
                    else:
                        wait(pe, prod_ready, IC * (n - 1))
                    nc.tensor.matmul(ps[:, 2 * s + i, :], env.ones[:, 0:P], row[:, i, s, :],
                                     start=True, stop=True).then_inc(spread_done, 1)

            def sum_step(n, i, first=False, last=False):
                for c in range(IC):
                    pe.wait_ge(prod_ready, IC * n + c + 1)
                    nc.tensor.matmul(ps[:, 4 + c, :], env.ident[:], prod[:, i, c, :], start=first, stop=last,
                                     skip_group_check=True).then_inc(y_done, 1)

            pe.wait_ge(delta_ready, IC)
            state_step(0, 0)
            state_step(1, 1)
            sum_step(0, 0, first=True)
            with pe.Fori(1, STATES // 2) as j:
                state_step(2 * j, 0)
                sum_step(2 * j - 1, 1)
                state_step(2 * j + 1, 1)
                sum_step(2 * j, 0)
            sum_step(STATES - 1, 1, last=True)
            pe.wait_ge(y_ready, IC)
            project_out(nc, env, pe, xT, w_out, IC, out_done, b_out[:])

        @block.scalar
        def _(act):
            link = Chain(act, astep)
            act.wait_ge(w_in_in, 32)
            for c in range(IC):
                act.wait_ge(proj_done, c + 1)
                nc.scalar.activation(xT[:, c, :], ps[:, c, :], ACT.Identity, bias=b_in[:, c:c + 1]).then_inc(x_ready, 1)
            for c in range(IC):
                act.wait_ge(proj_done, IC + c + 1)
                nc.scalar.activation(zT[:, c, :], ps[:, IC + c, :], ACT.Silu,
                                     bias=b_in[:, IC + c:IC + c + 1]).then_inc(z_ready, 1)
            act.wait_ge(consts_in, 144)
            act.wait_ge(dbc_done, 1)
            act.wait_ge(pads_set, 4)
            nc.scalar.activation(dbc[0:R, :], ps[0:R, 0, :], ACT.Identity, bias=b_x[:]).then_inc(dbc_ready, 1)
            nc.scalar.activation(A[:], A[:], ACT.Exp).then_inc(A_ready, 1)
            for c in range(IC):
                act.wait_ge(dt_done, c + 1)
                nc.scalar.activation(delta[:, c, :], ps[:, 4 + c, :], ACT.Relu, bias=b_dt[:, c:c + 1])\
                    .then_inc(astep, 1)
                link.n += 1
                link(nc.scalar.activation(mag[:, c, :], ps[:, 4 + c, :], ACT.Abs, bias=b_dt[:, c:c + 1]))
            link(nc.scalar.activation(mag[:], mag[:], ACT.Exp, scale=-1.0))
            link(nc.scalar.activation(mag[:], mag[:], ACT.Ln, bias=env.eps[:, 2:3]))

            def state_step(n, i):
                act.wait_ge(spread_done, 2 * n + 1)
                wait(act, u_ready, IC * (n - 1))
                nc.scalar.copy(B_all[:, i, :], ps[:, i, :]).then_inc(B_ready, 1)
                for c in range(IC):
                    wait(act, scanned, IC * (n - 2) + c + 1)
                    nc.scalar.activation(dA[:, i, c, :, 1:], by_sample(delta[:, c, :]), ACT.Exp,
                                         scale=A[:, c, bass.ds(n, 1)]).then_inc(dA_ready, 1)

            act.wait_ge(delta_ready, IC)
            act.wait_ge(dtx_ready, 1)
            act.wait_ge(pads_set, 4)
            state_step(0, 0)
            state_step(1, 1)
            with act.Fori(1, STATES // 2) as j:
                state_step(2 * j, 0)
                state_step(2 * j + 1, 1)

        @block.gpsimd
        def _(pool):
            nc.gpsimd.memset(dA[:, :, :, :, 0:1].rearrange("p i c b o -> p (i c b) o"), 0.0).then_inc(pads_set, 1)
            nc.gpsimd.memset(u[:, :, :, :, 0:1].rearrange("p i c b o -> p (i c b) o"), 0.0).then_inc(pads_set, 1)

            def inputs(n, i):
                pool.wait_ge(B_ready, n + 1)
                for c in range(IC):
                    wait(pool, scanned, IC * (n - 2) + c + 1)
                    nc.gpsimd.tensor_tensor(u[:, i, c, :, 1:], by_sample(dtx[:, c, :]), by_sample(B_all[:, i, :]),
                                            ALU.mult).then_inc(u_ready, 1)

            pool.wait_ge(pads_set, 4)
            pool.wait_ge(dtx_ready, 1)
            inputs(0, 0)
            inputs(1, 1)
            with pool.Fori(1, STATES // 2) as j:
                inputs(2 * j, 0)
                inputs(2 * j + 1, 1)

        @block.vector
        def _(dve):
            nc.vector.memset(dbc[32:64, :], 0.0).then_inc(pads_set, 1)
            nc.vector.memset(dbc[64:P, :], 0.0).then_inc(pads_set, 1)
            dve.wait_ge(A_ready, 1)
            nc.vector.tensor_scalar(A[:], A[:], -1.0, None, ALU.mult).then_inc(dstep, 1)
            dve.wait_ge(astep, 2 * IC + 2)
            for c in range(IC):
                nc.vector.tensor_tensor(delta[:, c, :], delta[:, c, :], mag[:, c, :], ALU.add).then_inc(delta_ready, 1)
            dve.wait_ge(delta_ready, IC)
            dve.wait_ge(dstep, 1)
            dve.wait_ge(x_ready, IC)
            nc.vector.tensor_tensor(dtx[:], delta[:], xT[:], ALU.mult).then_inc(dtx_ready, 1)

            def pick_rows(n, i):
                wait(dve, spread_done, 2 * n - 2)
                for s in range(2):
                    nc.vector.tensor_scalar(row[:, i, s, :], dbc[:], pick[:, bass.ds(n + s * STATES, 1)], None,
                                            ALU.mult).then_inc(row_ready, 1)

            def state_step(n, i):
                dve.wait_ge(spread_done, 2 * n + 2)
                for c in range(IC):
                    dve.wait_ge(dA_ready, IC * n + c + 1)
                    dve.wait_ge(u_ready, IC * n + c + 1)
                    wait(dve, prod_ready, IC * (n - 1) + c + 1)
                    nc.vector.tensor_tensor_scan(flat(state[:, c]), flat(dA[:, i, c]), flat(u[:, i, c]), 0.0,
                                                 ALU.mult, ALU.add).then_inc(scanned, 1)
                for c in range(IC):
                    dve.wait_ge(scanned, IC * n + c + 1)
                    wait(dve, y_done, IC * (n - 2) + c + 1)
                    nc.vector.tensor_tensor(by_sample(prod[:, i, c, :]), state[:, c, :, 1:],
                                            by_sample(ps[:, 2 + i, :]), ALU.mult).then_inc(prod_ready, 1)

            dve.wait_ge(dbc_ready, 1)
            pick_rows(0, 0)
            pick_rows(1, 1)
            state_step(0, 0)
            pick_rows(2, 0)
            state_step(1, 1)
            with dve.Fori(1, STATES // 2 - 1) as j:
                pick_rows(2 * j + 1, 1)
                state_step(2 * j, 0)
                pick_rows(2 * j + 2, 0)
                state_step(2 * j + 1, 1)
            pick_rows(STATES - 1, 1)
            state_step(STATES - 2, 0)
            state_step(STATES - 1, 1)
            for c in range(IC):
                dve.wait_ge(y_done, IC * (STATES - 1) + c + 1)
                nc.vector.scalar_tensor_tensor(out=xT[:, c, :], in0=xT[:, c, :], scalar=Dskip[:, c:c + 1],
                                               in1=ps[:, 4 + c, :], op0=ALU.mult, op1=ALU.add).then_inc(dstep, 1)
                dve.wait_ge(dstep, 2 + c)
                nc.vector.tensor_tensor(xT[:, c, :], xT[:, c, :], zT[:, c, :], ALU.mult).then_inc(y_ready, 1)
            add_out(nc, env, dve, out_done, x_added)


def self_attention(nc, env, ins):
    W = HG * P
    with ExitStack() as mem, stage(
            nc, "weights_in", "qkv_done", "qT_ready", "kT_ready", "kbd_ready", "v_ready", "scores_done", "max_ready",
            "probs_ready", "normed", "turned", "probsT_ready", "pv_done", "masked", "oT_ready", "out_done",
            "vstep", "moments_done", "std_done") as (
            block, weights_in, qkv_done, qT_ready, kT_ready, kbd_ready, v_ready, scores_done, max_ready,
            probs_ready, normed, turned, probsT_ready, pv_done, masked, oT_ready, out_done,
            vstep, moments_done, std_done):
        sb = allocator(nc, mem)
        ps = env.ps
        wq, wk, wv, wo = (sb(n, [P, KD, D]) for n in ("wq", "wk", "wv", "wo"))
        bq, bk = sb("bq", [P, KD]), sb("bk", [P, KD])
        bv, bo = sb("bv", [1, D]), sb("bo", [1, D])
        gamma, beta = sb("gamma", [P, D]), sb("beta", [P, D])
        qT, kT = sb("qT", [P, GROUPS, T]), sb("kT", [P, GROUPS, T])
        kbd = sb("kbd", [P, 2, HG, P])
        v = sb("v", [P, TT, D])
        scores = sb("scores", [P, 2, HG, P])
        probs = sb("probs", [P, 2, HG, P])
        probsT = sb("probsT", [P, 2, HG, P])
        top, total = sb("top", [P, TT * HEADS]), sb("total", [P, TT * HEADS])
        prod = sb("prod", [P, 2, 2, P])
        oT = sb("oT", [P, GROUPS, T])
        acc = sb("acc", [P, TT, D])
        stats, mv, std = sb("stats", [P, TT, 6]), sb("mv", [P, TT, 2]), sb("std", [P, TT])
        STEPS = TT * GROUPS

        @block.sync
        def _(sp):
            for n, dst in (("wq", wq), ("wk", wk), ("wv", wv), ("wo", wo)):
                sp.dma_start(dst[:], ins["L1_attn_" + n].rearrange("(k p) n -> p k n", p=P)).then_inc(weights_in, 16)
            sp.dma_start(bq[:], ins["L1_attn_bq"]).then_inc(weights_in, 16)
            sp.dma_start(bk[:], ins["L1_attn_bk"]).then_inc(weights_in, 16)
            sp.dma_start(bv[:], ins["L1_attn_bv"].unsqueeze(0)).then_inc(weights_in, 16)
            sp.dma_start(bo[:], ins["L1_attn_bo"].unsqueeze(0)).then_inc(weights_in, 16)
            sp.dma_start(gamma[:], rows_of(ins["L1_attn_gamma"])).then_inc(weights_in, 16)
            sp.dma_start(beta[:], rows_of(ins["L1_attn_beta"])).then_inc(weights_in, 16)

        @block.tensor
        def _(pe):
            pe.wait_ge(weights_in, 160)
            for s, w in ((0, wk), (2, wq)):
                for g in range(GROUPS):
                    project(nc, ps[:, s + g, :], lambda k: w[:, k, g * P:(g + 1) * P], KD,
                            lambda k: env.hT[:, k, :]).then_inc(qkv_done, 1)
            for t in range(TT):
                nc.tensor.matmul(ps[:, 4 + t, 0:D], env.ones[0:1, 0:P], bv[:], start=True, stop=False)
                for k in range(KD):
                    last = nc.tensor.matmul(ps[:, 4 + t, 0:D], env.hT[:, k, t * P:(t + 1) * P], wv[:, k, :],
                                            start=False, stop=(k == KD - 1))
                last.then_inc(qkv_done, 1)

            def score(s):
                t, g = s // GROUPS, s % GROUPS
                pe.wait_ge(kbd_ready, s + 1)
                if s == 0:
                    pe.wait_ge(qT_ready, GROUPS)
                wait(pe, max_ready, HG * s)
                for half in range(2):
                    last = nc.tensor.matmul(ps[:, half, :], qT[:, g, t * P:(t + 1) * P],
                                            kbd[:, s % 2, 4 * half:4 * half + 4, :].rearrange("p h k -> p (h k)"),
                                            start=True, stop=True)
                last.then_inc(scores_done, 1)

            def attend(s):
                g = s % GROUPS
                pe.wait_ge(normed, s + 1)
                wait(pe, probsT_ready, 2 * s)
                for half in range(2):
                    for h in range(4):
                        last = nc.tensor.transpose(ps[:, 2 + half, h * P:(h + 1) * P], probs[:, s % 2, 4 * half + h, :],
                                                   env.ident[:])
                    last.then_inc(turned, 1)
                pe.wait_ge(probsT_ready, 2 * s + 2)
                if s == 0:
                    pe.wait_ge(v_ready, TT)
                wait(pe, masked, s - 1)
                for j in range(4):
                    c = (4 * g + j) * 2 * HD
                    last = nc.tensor.matmul(ps[32 * j:32 * j + 32, 4 + s % 2, 0:2 * P], v[:, s // GROUPS, c:c + 2 * HD],
                                            probsT[:, s % 2, 2 * j:2 * j + 2, :].rearrange("p h q -> p (h q)"),
                                            start=True, stop=True)
                last.then_inc(pv_done, 1)

            score(0)
            for s in range(STEPS):
                if s + 1 < STEPS:
                    score(s + 1)
                attend(s)
            pe.wait_ge(oT_ready, STEPS)
            pe.wait_ge(v_ready, TT)
            project_out(nc, env, pe, oT, wo, KD, out_done, bo[:])

        @block.scalar
        def _(act):
            act.wait_ge(weights_in, 160)
            for t in range(TT):
                act.wait_ge(qkv_done, 2 * GROUPS + t + 1)
                nc.scalar.copy(v[:, t, :], ps[:, 4 + t, 0:D]).then_inc(v_ready, 1)
            for s in range(STEPS):
                act.wait_ge(max_ready, HG * (s + 1))
                wait(act, turned, 2 * (s - 1))
                for h in range(HG):
                    i = HG * s + h
                    nc.scalar.activation(probs[:, s % 2, h, :], scores[:, s % 2, h, :], ACT.Exp, bias=top[:, i:i + 1],
                                         scale=-1.0, accum_out=total[:, i:i + 1]).then_inc(probs_ready, 1)
                if s >= 1:
                    act.wait_ge(turned, 2 * s)
                    nc.scalar.copy(probsT[:, (s - 1) % 2, 4:8, :].rearrange("p h q -> p (h q)"), ps[:, 3, :])\
                        .then_inc(probsT_ready, 1)
            act.wait_ge(turned, 2 * STEPS)
            nc.scalar.copy(probsT[:, (STEPS - 1) % 2, 4:8, :].rearrange("p h q -> p (h q)"), ps[:, 3, :])\
                .then_inc(probsT_ready, 1)
            act.wait_ge(moments_done, TT)
            nc.scalar.activation(std[:], mv[:, :, 1], ACT.Sqrt, bias=env.eps[:, 0:1]).then_inc(std_done, 1)

        @block.vector
        def _(dve):
            link = Chain(dve, vstep)
            dve.wait_ge(weights_in, 160)
            for g in range(GROUPS):
                dve.wait_ge(qkv_done, g + 1)
                nc.vector.tensor_scalar(kT[:, g, :], ps[:, g, :], bk[:, g:g + 1], None, ALU.add).then_inc(kT_ready, 1)
            for g in range(GROUPS):
                dve.wait_ge(qkv_done, GROUPS + g + 1)
                nc.vector.tensor_scalar(qT[:, g, :], ps[:, 2 + g, :], bq[:, g:g + 1], HD ** -0.5, ALU.add, ALU.mult)\
                    .then_inc(qT_ready, 1)
            dve.wait_ge(kT_ready, GROUPS)

            def spread(s):
                t, g = s // GROUPS, s % GROUPS
                wait(dve, scores_done, s - 1)
                nc.vector.tensor_tensor(kbd[:, s % 2], kT[:, g, t * P:(t + 1) * P].unsqueeze(1).broadcast_to([P, HG, P]),
                                        env.head_mask[:].unsqueeze(2).broadcast_to([P, HG, P]),
                                        ALU.mult).then_inc(kbd_ready, 1)

            def softmax(s):
                dve.wait_ge(scores_done, s + 1)
                wait(dve, probs_ready, HG * (s - 1))
                for h in range(HG):
                    i = HG * s + h
                    nc.vector.tensor_tensor_reduce(
                        out=scores[:, s % 2, h, :], in0=ps[:, h // 4, (h % 4) * P:(h % 4 + 1) * P],
                        in1=env.same_sample[:], scale=-1.0, scalar=3e38, op0=ALU.add, op1=ALU.min,
                        accum_out=top[:, i:i + 1]).then_inc(max_ready, 1)

            def norm(s):
                dve.wait_ge(probs_ready, HG * (s + 1))
                i = HG * s
                link(nc.vector.reciprocal(total[:, i:i + HG], total[:, i:i + HG]))
                nc.vector.tensor_tensor(probs[:, s % 2], probs[:, s % 2],
                                        total[:, i:i + HG].unsqueeze(2).broadcast_to([P, HG, P]),
                                        ALU.mult).then_inc(normed, 1)

            def turn(s):
                dve.wait_ge(turned, 2 * s + 1)
                nc.vector.tensor_copy(probsT[:, s % 2, 0:4, :].rearrange("p h q -> p (h q)"), ps[:, 2, :])\
                    .then_inc(probsT_ready, 1)

            def extract(s):
                t, g = s // GROUPS, s % GROUPS
                dve.wait_ge(pv_done, s + 1)
                wait(dve, oT_ready, s - 1)
                nc.vector.tensor_tensor(prod[:, s % 2], ps[:, 4 + s % 2, 0:2 * P].rearrange("p (h q) -> p h q", h=2),
                                        env.pair_mask[:].unsqueeze(2).broadcast_to([P, 2, P]), ALU.mult)\
                    .then_inc(masked, 1)
                dve.wait_ge(masked, s + 1)
                nc.vector.tensor_tensor(oT[:, g, t * P:(t + 1) * P], prod[:, s % 2, 0, :], prod[:, s % 2, 1, :], ALU.add)\
                    .then_inc(oT_ready, 1)

            spread(0)
            spread(1)
            softmax(0)
            for s in range(STEPS):
                if s + 2 < STEPS:
                    spread(s + 2)
                if s + 1 < STEPS:
                    softmax(s + 1)
                norm(s)
                if s >= 1:
                    extract(s - 1)
                turn(s)
            extract(STEPS - 1)
            for t in range(TT):
                dve.wait_ge(out_done, t + 1)
                link(nc.vector.tensor_tensor(acc[:, t, :], env.h[:, t, :], ps[:, t, 0:D], ALU.add))
            normalize_rows(nc, env, link, acc, acc, stats, mv, std, moments_done, std_done, dve, gamma[:], beta[:])
            link(nc.vector.tensor_tensor(env.x[:], env.x[:], acc[:], ALU.add))


def rotary_attention(nc, env, ins):
    with ExitStack() as mem, stage(
            nc, "weights_in", "proj_done", "vstep", "rotated", "v_ready", "scores_done", "max_ready", "probs_ready",
            "turned", "probsT_ready", "out_done", "x_added") as (
            block, weights_in, proj_done, vstep, rotated, v_ready, scores_done, max_ready, probs_ready,
            turned, probsT_ready, out_done, x_added):
        sb = allocator(nc, mem)
        ps = env.ps
        wq, wk, wv = (sb(n, [P, KD, D]) for n in ("wq", "wk", "wv"))
        cos, sin = sb("cos", [P, SEQ]), sb("sin", [P, SEQ])
        rot = sb("rot", [P, 2, KD, T])
        tmp = sb("tmp", [P, 2, T])
        v = sb("v", [P, TT, D])
        scores, probs, probsT = sb("scores", [P, TT, P]), sb("probs", [P, TT, P]), sb("probsT", [P, TT, P])
        top, total = sb("top", [P, TT]), sb("total", [P, TT])

        @block.sync
        def _(sp):
            for n, dst in (("wqT", wq), ("wkT", wk), ("wvT", wv)):
                sp.dma_start(dst[:], ins["L2_attn_" + n].rearrange("(k p) n -> p k n", p=P)).then_inc(weights_in, 16)
            sp.dma_start(cos[:], env.consts["cos256"]).then_inc(weights_in, 16)
            sp.dma_start(sin[:], env.consts["sin256"]).then_inc(weights_in, 16)

        @block.tensor
        def _(pe):
            pe.wait_ge(weights_in, 80)
            for s, w in ((0, wq), (2, wk)):
                for c in range(KD):
                    project(nc, ps[:, s + c, :], lambda k: w[:, k, c * P:(c + 1) * P], KD, lambda k: env.hT[:, k, :])\
                        .then_inc(proj_done, 1)
            for t in range(TT):
                project(nc, ps[:, 4 + t, 0:D], lambda k: env.hT[:, k, t * P:(t + 1) * P], KD, lambda k: wv[:, k, :])\
                    .then_inc(proj_done, 1)
            pe.wait_ge(rotated, 4)
            for t in range(TT):
                project(nc, ps[:, t, 0:P], lambda k: rot[:, 0, k, t * P:(t + 1) * P], KD,
                        lambda k: rot[:, 1, k, t * P:(t + 1) * P]).then_inc(scores_done, 1)
            pe.wait_ge(v_ready, TT)
            for t in range(TT):
                pe.wait_ge(probs_ready, t + 1)
                nc.tensor.transpose(ps[:, 4 + t, 0:P], probs[:, t, :], env.ident[:]).then_inc(turned, 1)
            for t in range(TT):
                pe.wait_ge(probsT_ready, t + 1)
                nc.tensor.matmul(ps[:, t, 0:D], probsT[:, t, :], v[:, t, :], start=True, stop=True)\
                    .then_inc(out_done, 1)

        @block.scalar
        def _(act):
            for t in range(TT):
                act.wait_ge(proj_done, 4 + t + 1)
                nc.scalar.copy(v[:, t, :], ps[:, 4 + t, 0:D]).then_inc(v_ready, 1)
            for t in range(TT):
                act.wait_ge(max_ready, t + 1)
                nc.scalar.activation(probs[:, t, :], scores[:, t, :], ACT.Exp, bias=top[:, t:t + 1],
                                     scale=-1.0, accum_out=total[:, t:t + 1]).then_inc(probs_ready, 1)
            for t in range(TT):
                act.wait_ge(turned, t + 1)
                nc.scalar.copy(probsT[:, t, :], ps[:, 4 + t, 0:P]).then_inc(probsT_ready, 1)

        @block.vector
        def _(dve):
            link = Chain(dve, vstep)
            dve.wait_ge(weights_in, 80)
            table = lambda tab: tab[:].unsqueeze(1).broadcast_to([P, BATCH, SEQ])
            wide = lambda ap: ap.rearrange("p (b t) -> p b t", b=BATCH)
            for s in range(2):
                dve.wait_ge(proj_done, 2 * s + 2)
                even, odd = ps[:, 2 * s, :], ps[:, 2 * s + 1, :]
                for c, a, b, op in ((0, even, odd, ALU.add), (1, odd, even, ALU.subtract)):
                    nc.vector.tensor_tensor(wide(tmp[:, 0, :]), wide(a), table(cos), ALU.mult).then_inc(vstep, 1)
                    link.n += 1
                    link(nc.vector.tensor_tensor(wide(tmp[:, 1, :]), wide(b), table(sin), ALU.mult))
                    nc.vector.tensor_tensor(rot[:, s, c, :], tmp[:, 0, :], tmp[:, 1, :], op).then_inc(rotated, 1)
                    dve.wait_ge(rotated, 2 * s + c + 1)
                if s == 0:
                    link(nc.vector.tensor_scalar(rot[:, 0], rot[:, 0], D ** -0.5, None, ALU.mult))
            for t in range(TT):
                dve.wait_ge(scores_done, t + 1)
                nc.vector.tensor_tensor_reduce(out=scores[:, t, :], in0=ps[:, t, 0:P], in1=env.same_sample[:],
                                               scale=-1.0, scalar=3e38, op0=ALU.add, op1=ALU.min,
                                               accum_out=top[:, t:t + 1]).then_inc(max_ready, 1)
            dve.wait_ge(probs_ready, TT)
            link(nc.vector.reciprocal(total[:], total[:]))
            for t in range(TT):
                dve.wait_ge(out_done, t + 1)
                nc.vector.scalar_tensor_tensor(out=env.x[:, t, :], in0=ps[:, t, 0:D], scalar=total[:, t:t + 1],
                                               in1=env.x[:, t, :], op0=ALU.mult, op1=ALU.add).then_inc(x_added, 1)


def context_fusion(nc, env, ins):
    FEATS = 4 * KD
    with ExitStack() as mem, stage(
            nc, "consts_in", "ctx_in0", "ctx_in1", "qw_ready", "scores_done", "max_ready", "probs_ready", "turned",
            "probsT_ready", "pv_done", "hq_ready", "vstep", "wqv_in", "own_ready", "line_ready", "exp_done", "sums_turned", "weights_ready", "weights_turned",
            "spread_ready", "mix_done", "feats_ready", "feats_turned", "featsT_ready", "out_done", "x_added") as (
            block, consts_in, ctx_in0, ctx_in1, qw_ready, scores_done, max_ready, probs_ready, turned,
            probsT_ready, pv_done, hq_ready, vstep, wqv_in, own_ready, line_ready, exp_done, sums_turned, weights_ready, weights_turned,
            spread_ready, mix_done, feats_ready, feats_turned, featsT_ready, out_done, x_added):
        sb = allocator(nc, mem)
        ps = env.ps
        w23, w1, b_sim = sb("w23", [P, 2, KD]), sb("w1", [P, D]), sb("b_sim", [P, 1])
        wqv, bqv = sb("wqv", [P, FEATS, D]), sb("bqv", [1, D])
        same = sb("same", [P, P])
        cT, ctx = sb("ctxT", [P, 2, 2, KD, CTX]), sb("ctx", [P, 2, 2, CC, D])
        qw = sb("qw", [P, KD, T])
        probs, probsT = sb("probs", [P, 2, CTX]), sb("probsT", [P, 2, CC, P])
        top, total, own = sb("top", [P, TT]), sb("total", [P, TT]), sb("own", [P, TT])
        junk = sb("junk", [P, D])
        line, peak, norm = sb("line", [TT, P]), sb("peak", [TT, 2]), sb("norm", [TT, 2])
        weights, spread = sb("weights", [P, TT]), sb("spread", [P, TT, P])
        feats = sb("feats", [P, 3, TT, D])
        featsT = sb("featsT", [P, 3 * KD, T])
        ctx_in = (ctx_in0, ctx_in1)
        split = lambda ap: ap.rearrange("p (b i) -> p b i", b=2)

        @block.sync
        def _(sp):
            for dst, src in ((w23, ins["L2_xattn_w23"]), (w1, rows_of(ins["L2_xattn_w1"])),
                             (b_sim, rows_of(ins["L2_xattn_b_sim"])), (same, env.consts["same"])):
                sp.dma_start(dst[:], src).then_inc(consts_in, 16)
            for t in range(TT):
                wait(sp, pv_done, t - 1)
                for i in range(2):
                    sp.dma_start(cT[:, t % 2, i], ins["ctxT"][2 * t + i].rearrange("(k p) s -> p k s", p=P))\
                        .then_inc(ctx_in[t % 2], 16)
                for i in range(2):
                    sp.dma_start(ctx[:, t % 2, i], ins["ctx"][2 * t + i].rearrange("(c p) d -> p c d", p=P))\
                        .then_inc(ctx_in[t % 2], 16)
            sp.dma_start(wqv[:], ins["L2_xattn_W_qv"].rearrange("(f p) n -> p f n", p=P)).then_inc(wqv_in, 16)
            sp.dma_start(bqv[:], ins["L2_xattn_b_qv"].unsqueeze(0)).then_inc(wqv_in, 16)

        @block.tensor
        def _(pe):
            def score(t):
                pe.wait_ge(ctx_in[t % 2], 64 * (t // 2 + 1))
                pe.wait_ge(qw_ready, KD)
                wait(pe, probs_ready, t - 1)
                for half in range(2):
                    for k in range(KD):
                        for i in range(2):
                            last = nc.tensor.matmul(
                                ps[SEQ * i:SEQ * (i + 1), 2 * (t % 2) + half, :],
                                qw[:, k, (2 * t + i) * SEQ:(2 * t + i + 1) * SEQ],
                                cT[:, t % 2, i, k, half * BANK:(half + 1) * BANK], start=(k == 0), stop=(k == KD - 1))
                last.then_inc(scores_done, 1)

            def attend(t):
                pe.wait_ge(probs_ready, t + 1)
                wait(pe, probsT_ready, 2 * t)
                for half in range(2):
                    for c in range(4):
                        last = nc.tensor.transpose(ps[:, 4 + half, c * P:(c + 1) * P],
                                                   probs[:, t % 2, (4 * half + c) * P:(4 * half + c + 1) * P],
                                                   env.ident[:])
                    last.then_inc(turned, 1)
                pe.wait_ge(probsT_ready, 2 * t + 2)
                wait(pe, hq_ready, t - 1)
                for c in range(CC):
                    for i in range(2):
                        last = nc.tensor.matmul(ps[SEQ * i:SEQ * (i + 1), 6 + t % 2, 0:D],
                                                probsT[:, t % 2, c, SEQ * i:SEQ * (i + 1)], ctx[:, t % 2, i, c, :],
                                                start=(c == 0), stop=(c == CC - 1))
                last.then_inc(pv_done, 1)

            score(0)
            for t in range(TT):
                if t + 1 < TT:
                    score(t + 1)
                attend(t)
            pe.wait_ge(own_ready, 1)
            nc.tensor.transpose(ps[0:TT, 0, 0:P], own[:], env.ident[:]).then_inc(sums_turned, 1)
            pe.wait_ge(weights_ready, 1)
            nc.tensor.transpose(ps[:, 1, 0:TT], line[:], env.ident[0:TT, 0:TT]).then_inc(weights_turned, 1)
            for t in range(TT):
                pe.wait_ge(spread_ready, t + 1)
                nc.tensor.matmul(ps[:, 2 + t, 0:D], spread[:, t, :], env.h[:, t, :], start=True, stop=True)\
                    .then_inc(mix_done, 1)
            for n in range(3 * KD):
                pe.wait_ge(feats_ready, (n // KD + 1) * TT)
                wait(pe, featsT_ready, n - 3)
                for t in range(TT):
                    last = nc.tensor.transpose(ps[:, (0, 1, 6, 7)[n % 4], t * P:(t + 1) * P],
                                               feats[:, n // KD, t, (n % KD) * P:(n % KD + 1) * P], env.ident[:])
                last.then_inc(feats_turned, 1)
            pe.wait_ge(featsT_ready, 3 * KD)
            pe.wait_ge(wqv_in, 32)
            for t in range(TT):
                nc.tensor.matmul(ps[:, t, 0:D], env.ones[0:1, 0:P], bqv[:], start=True, stop=False)
                for f in range(FEATS):
                    src = env.hT[:, f, t * P:(t + 1) * P] if f < KD else featsT[:, f - KD, t * P:(t + 1) * P]
                    last = nc.tensor.matmul(ps[:, t, 0:D], src, wqv[:, f, :], start=False, stop=(f == FEATS - 1))
                last.then_inc(out_done, 1)

        @block.scalar
        def _(act):
            for t in range(TT):
                act.wait_ge(max_ready, t + 1)
                wait(act, turned, 2 * (t - 1))
                nc.scalar.activation(probs[:, t % 2, :], ps[:, 2 * (t % 2):2 * (t % 2) + 2, :].rearrange(
                    "p b n -> p (b n)"), ACT.Exp, bias=top[:, t:t + 1], accum_out=total[:, t:t + 1])\
                    .then_inc(probs_ready, 1)
                act.wait_ge(turned, 2 * t + 1)
                nc.scalar.copy(probsT[:, t % 2, 0:4, :].rearrange("p c q -> p (c q)"), ps[:, 4, :])\
                    .then_inc(probsT_ready, 1)
            act.wait_ge(line_ready, 1)
            nc.scalar.activation(line[:], line[:], ACT.Exp).then_inc(exp_done, 1)

        @block.vector
        def _(dve):
            link = Chain(dve, vstep)
            dve.wait_ge(consts_in, 64)
            for k in range(KD):
                nc.vector.tensor_scalar(qw[:, k, :], env.hT[:, k, :], w23[:, 1, k:k + 1], w23[:, 0, k:k + 1],
                                        ALU.mult, ALU.add).then_inc(qw_ready, 1)
            for t in range(TT):
                link(nc.vector.tensor_tensor_reduce(out=junk[:], in0=env.h[:, t, :], in1=w1[:], scale=1.0, scalar=0.0,
                                                    op0=ALU.mult, op1=ALU.add, accum_out=own[:, t:t + 1]))
            for t in range(TT):
                dve.wait_ge(scores_done, t + 1)
                nc.vector.tensor_reduce(top[:, t:t + 1], ps[:, 2 * (t % 2):2 * (t % 2) + 2, :].rearrange(
                    "p b n -> p (b n)"), AX.X, ALU.max, negate=True).then_inc(max_ready, 1)
                dve.wait_ge(turned, 2 * t + 2)
                nc.vector.tensor_copy(probsT[:, t % 2, 4:8, :].rearrange("p c q -> p (c q)"), ps[:, 5, :])\
                    .then_inc(probsT_ready, 1)
                link(nc.vector.reciprocal(total[:, t:t + 1], total[:, t:t + 1]))
                dve.wait_ge(pv_done, t + 1)
                nc.vector.tensor_scalar(feats[:, 0, t, :], ps[:, 6 + t % 2, 0:D], total[:, t:t + 1], None, ALU.mult)\
                    .then_inc(hq_ready, 1)
            dve.wait_ge(max_ready, TT)
            nc.vector.scalar_tensor_tensor(out=own[:], in0=own[:], scalar=b_sim[:], in1=top[:],
                                           op0=ALU.add, op1=ALU.subtract).then_inc(own_ready, 1)
            dve.wait_ge(sums_turned, 1)
            link(nc.vector.tensor_reduce(peak[:], split(ps[0:TT, 0, 0:P]), AX.X, ALU.max))
            nc.vector.tensor_tensor(split(line[:]), split(ps[0:TT, 0, 0:P]),
                                    peak[:].unsqueeze(2).broadcast_to([TT, 2, SEQ]), ALU.subtract)\
                .then_inc(line_ready, 1)
            dve.wait_ge(hq_ready, TT)
            for t in range(TT):
                nc.vector.engine_nop().then_inc(feats_ready, 1)
            for t in range(TT):
                nc.vector.tensor_tensor(feats[:, 1, t, :], feats[:, 0, t, :], env.h[:, t, :], ALU.mult)\
                    .then_inc(feats_ready, 1)
            dve.wait_ge(exp_done, 1)
            link(nc.vector.tensor_reduce(norm[:], split(line[:]), AX.X, ALU.add))
            link(nc.vector.reciprocal(norm[:], norm[:]))
            nc.vector.tensor_tensor(split(line[:]), split(line[:]), norm[:].unsqueeze(2).broadcast_to([TT, 2, SEQ]),
                                    ALU.mult).then_inc(weights_ready, 1)
            dve.wait_ge(weights_turned, 1)
            link(nc.vector.tensor_copy(weights[:], ps[:, 1, 0:TT]))
            for t in range(TT):
                nc.vector.tensor_scalar(spread[:, t, :], same[:], weights[:, t:t + 1], None, ALU.mult)\
                    .then_inc(spread_ready, 1)
            for t in range(TT):
                dve.wait_ge(mix_done, t + 1)
                nc.vector.tensor_tensor(feats[:, 2, t, :], ps[:, 2 + t, 0:D], env.h[:, t, :], ALU.mult)\
                    .then_inc(feats_ready, 1)
            for n in range(3 * KD):
                dve.wait_ge(feats_turned, n + 1)
                nc.vector.tensor_copy(featsT[:, n, :], ps[:, (0, 1, 6, 7)[n % 4], :]).then_inc(featsT_ready, 1)
            add_out(nc, env, dve, out_done, x_added)


def softmax_cross_attention(nc, env, ins):
    PAIRS = HEADS // 2
    PG = PAIRS // GROUPS
    K_UNITS, UNITS = 4, 8
    with ExitStack() as mem, stage(
            nc, "weights_in", "mask_in", "ctx_in0", "ctx_in1", "q_done", "q_ready", "unit_done", "unit_taken",
            "qbd_ready", "scores_done", "max_ready", "exp_done", "probs_ready", "turned_a", "turned_b", "probsT_a",
            "probsT_b", "pv_done", "masked", "o_ready", "out_done", "x_added", "total_ready", "spare_set") as (
            block, weights_in, mask_in, ctx_in0, ctx_in1, q_done, q_ready, unit_done, unit_taken,
            qbd_ready, scores_done, max_ready, exp_done, probs_ready, turned_a, turned_b, probsT_a,
            probsT_b, pv_done, masked, o_ready, out_done, x_added, total_ready, spare_set):
        sb = allocator(nc, mem)
        ps = env.ps
        wq, wk, wv, wo = (sb(n, [P, KD, D]) for n in ("wq", "wk", "wv", "wo"))
        mask = sb("mask", [P, CTX])
        cT = sb("ctxT", [P, 2, KD, CTX])
        kT, v = sb("kT", [P, 2, GROUPS, CTX]), sb("v", [P, 2, CC, D])
        qT = sb("qT", [P, GROUPS, T])
        qbd = sb("qbd", [P, 2, GROUPS, HG, SEQ])
        scores, probs = sb("scores", [P, 2, CTX]), sb("probs", [P, 2, CTX])
        probsT = sb("probsT", [P, GROUPS, CC, PG, P])
        spare = sb("spare", [P, 1])
        top, total = sb("top", [P, PAIRS]), sb("total", [P, PAIRS])
        prod, oT = sb("prod", [P, GROUPS, 2, SEQ]), sb("oT", [P, GROUPS, T])
        ctx_in = (ctx_in0, ctx_in1)
        UNIT_BANK, O_BANK, S_BANK, T_BANK = 0, 1, 2, 6
        halves = lambda ap: ap.rearrange("p b n -> p (b n)")

        def samples(eng, body):
            body(0, 0, False)
            with eng.Fori(0, BATCH // 2 - 1) as j:
                body(2 * j + 1, 1, False)
                body(2 * j + 2, 0, False)
            body(BATCH - 1, 1, True)

        @block.sync
        def _(sp):
            for n, dst in (("wq", wq), ("wk", wk), ("wv", wv), ("wo", wo)):
                sp.dma_start(dst[:], ins["L3_xattn_" + n].rearrange("(k p) n -> p k n", p=P)).then_inc(weights_in, 16)
            for b in range(BATCH):
                wait(sp, unit_done, UNITS * (b - 1))
                sp.dma_start(cT[:, b % 2], ins["ctxT"][b].rearrange("(k p) s -> p k s", p=P))\
                    .then_inc(ctx_in[b % 2], 16)
                if b == 0:
                    for i in range(2):
                        sp.dma_start(mask[i * SEQ:(i + 1) * SEQ, :], ins["mask"]).then_inc(mask_in, 16)

        @block.tensor
        def _(pe):
            def unit(b, i, u):
                if u == 0:
                    pe.wait_ge(ctx_in[i], 16 if isinstance(b, int) and b < 2 else 8 * b + 16 - 8 * i)
                wait(pe, unit_taken, UNITS * b + u)
                if u < K_UNITS:
                    g, half = u // 2, u % 2
                    last = project(nc, ps[:, UNIT_BANK, :], lambda k: wk[:, k, g * P:(g + 1) * P], KD,
                                   lambda k: cT[:, i, k, half * BANK:(half + 1) * BANK])
                else:
                    for cc in range(2):
                        c = 2 * (u - K_UNITS) + cc
                        last = project(nc, ps[:, UNIT_BANK, cc * D:(cc + 1) * D],
                                       lambda k: cT[:, i, k, c * P:(c + 1) * P], KD, lambda k: wv[:, k, :])
                last.then_inc(unit_done, 1)

            def score(b, i, p):
                g, j = p // PG, p % PG
                if p == 0:
                    pe.wait_ge(qbd_ready, GROUPS * b + GROUPS)
                    wait(pe, unit_taken, UNITS * b + K_UNITS)
                wait(pe, max_ready, PAIRS * b + p - 1)
                for half in range(2):
                    last = nc.tensor.matmul(ps[:, S_BANK + 2 * (p % 2) + half, :],
                                            qbd[:, i, g, 2 * j:2 * j + 2, :].rearrange("p h l -> p (h l)"),
                                            kT[:, i, g, half * BANK:(half + 1) * BANK], start=True, stop=True)
                last.then_inc(scores_done, 1)

            def turn(b, p):
                wait(pe, probs_ready, PAIRS * b + p + 1)
                for half, taken, done in ((0, probsT_a, turned_a), (1, probsT_b, turned_b)):
                    wait(pe, taken, PAIRS * b + p)
                    for c in range(4):
                        last = nc.tensor.transpose(ps[:, T_BANK + half, c * P:(c + 1) * P],
                                                   probs[:, p % 2, (4 * half + c) * P:(4 * half + c + 1) * P],
                                                   env.ident[:])
                    last.then_inc(done, 1)

            def values(b, i, g):
                pe.wait_ge(probsT_a, PAIRS * b + PG * (g + 1))
                pe.wait_ge(probsT_b, PAIRS * b + PG * (g + 1))
                if g == 0:
                    wait(pe, masked, GROUPS * b)
                    wait(pe, unit_taken, UNITS * b + UNITS)
                for c in range(CC):
                    for j in range(PG):
                        first = g * P + 2 * HD * j
                        last = nc.tensor.matmul(ps[32 * j:32 * j + 32, O_BANK, g * P:(g + 1) * P],
                                                v[:, i, c, first:first + 2 * HD], probsT[:, g, c, j, :],
                                                start=(c == 0), stop=(c == CC - 1))
                last.then_inc(pv_done, 1)

            def sample(b, i, last):
                for p in range(PAIRS):
                    if not last:
                        unit(b + 1, 1 - i, p)
                    if p == 0 and not (isinstance(b, int) and b == 0):
                        values(b - 1, 1 - i, 1)
                    if p == PG:
                        values(b, i, 0)
                    turn(b, p)
                    if p + 2 < PAIRS:
                        score(b, i, p + 2)
                    elif not last:
                        score(b + 1, 1 - i, p + 2 - PAIRS)
                if last:
                    values(b, i, 1)

            pe.wait_ge(weights_in, 64)
            for g in range(GROUPS):
                project(nc, ps[:, S_BANK + g, :], lambda k: wq[:, k, g * P:(g + 1) * P], KD,
                        lambda k: env.hT[:, k, :]).then_inc(q_done, 1)
            for u in range(UNITS):
                unit(0, 0, u)
            pe.wait_ge(q_ready, GROUPS)
            score(0, 0, 0)
            score(0, 0, 1)
            samples(pe, sample)
            pe.wait_ge(o_ready, GROUPS * BATCH)
            project_out(nc, env, pe, oT, wo, KD, out_done)

        @block.scalar
        def _(act):
            for g in range(GROUPS):
                act.wait_ge(q_done, g + 1)
                nc.scalar.mul(qT[:, g, :], ps[:, S_BANK + g, :], HD ** -0.5).then_inc(q_ready, 1)

            def exponentials(b, p):
                n = PAIRS * b + p
                act.wait_ge(max_ready, n + 1)
                wait(act, turned_b, n - 1)
                nc.scalar.activation(probs[:, p % 2, :], scores[:, p % 2, :], ACT.Exp, bias=top[:, p:p + 1],
                                     scale=-1.0, accum_out=total[:, p:p + 1]).then_inc(exp_done, 1)

            def sample(b, i, last):
                for p in range(PAIRS):
                    if p + 1 < PAIRS:
                        exponentials(b, p + 1)
                    elif not last:
                        exponentials(b + 1, 0)
                    act.wait_ge(turned_a, PAIRS * b + p + 1)
                    if p == 0:
                        wait(act, pv_done, GROUPS * b - 1)
                    if p == PG:
                        wait(act, pv_done, GROUPS * b)
                    nc.scalar.copy(probsT[:, p // PG, 0:4, p % PG, :],
                                   ps[:, T_BANK, :].rearrange("p (c q) -> p c q", c=4)).then_inc(probsT_a, 1)

            exponentials(0, 0)
            samples(act, sample)

        @block.vector
        def _(dve):
            def spread(b, i):
                for g in range(GROUPS):
                    nc.vector.tensor_tensor(
                        qbd[:, i, g], qT[:, g, bass.ds(b * SEQ, SEQ)].unsqueeze(1).broadcast_to([P, HG, SEQ]),
                        env.head_mask[:].unsqueeze(2).broadcast_to([P, HG, SEQ]), ALU.mult).then_inc(qbd_ready, 1)

            def take(b, i, u):
                dve.wait_ge(unit_done, UNITS * b + u + 1)
                if u < K_UNITS:
                    dst = kT[:, i, u // 2, (u % 2) * BANK:(u % 2 + 1) * BANK]
                else:
                    dst = v[:, i, 2 * (u - K_UNITS):2 * (u - K_UNITS) + 2, :].rearrange("p c n -> p (c n)")
                nc.vector.tensor_copy(dst, ps[:, UNIT_BANK, :]).then_inc(unit_taken, 1)

            def maxima(b, p):
                n = PAIRS * b + p
                dve.wait_ge(scores_done, n + 1)
                wait(dve, exp_done, n - 1)
                wait(dve, spare_set, n)
                nc.vector.memset(spare[:], 0.0).then_inc(spare_set, 1)
                nc.vector.tensor_tensor_reduce(
                    out=scores[:, p % 2, :], in0=halves(ps[:, S_BANK + 2 * (p % 2):S_BANK + 2 * (p % 2) + 2, :]),
                    in1=mask[:], scale=-1.0, scalar=3e38, op0=ALU.add, op1=ALU.min,
                    accum_out=top[:, p:p + 1]).then_inc(max_ready, 1)

            def normalize(b, p):
                n = PAIRS * b + p
                dve.wait_ge(exp_done, n + 1)
                nc.vector.reciprocal(total[:, p:p + 1], total[:, p:p + 1]).then_inc(total_ready, 1)
                dve.wait_ge(total_ready, n + 1)
                nc.vector.tensor_scalar(probs[:, p % 2, :], probs[:, p % 2, :], total[:, p:p + 1], None, ALU.mult)\
                    .then_inc(probs_ready, 1)

            def extract(b):
                dve.wait_ge(pv_done, GROUPS * b + GROUPS)
                for g in range(GROUPS):
                    wait(dve, o_ready, GROUPS * b)
                    nc.vector.tensor_tensor(
                        prod[:, g], ps[:, O_BANK, g * P:(g + 1) * P].rearrange("p (h l) -> p h l", h=2),
                        env.pair_mask[:].unsqueeze(2).broadcast_to([P, 2, SEQ]), ALU.mult).then_inc(masked, 1)
                for g in range(GROUPS):
                    dve.wait_ge(masked, GROUPS * b + g + 1)
                    nc.vector.tensor_tensor(oT[:, g, bass.ds(b * SEQ, SEQ)], prod[:, g, 0, :], prod[:, g, 1, :],
                                            ALU.add).then_inc(o_ready, 1)

            def sample(b, i, last):
                for p in range(PAIRS):
                    if not last:
                        take(b + 1, 1 - i, p)
                        if p == 0:
                            spread(b + 1, 1 - i)
                    dve.wait_ge(turned_b, PAIRS * b + p + 1)
                    nc.vector.tensor_copy(probsT[:, p // PG, 4:8, p % PG, :],
                                          ps[:, T_BANK + 1, :].rearrange("p (c q) -> p c q", c=4)).then_inc(probsT_b, 1)
                    if p + 2 < PAIRS:
                        maxima(b, p + 2)
                    elif not last:
                        maxima(b + 1, p + 2 - PAIRS)
                    if p + 1 < PAIRS:
                        normalize(b, p + 1)
                    elif not last:
                        normalize(b + 1, 0)
                    if p == 1 and not (isinstance(b, int) and b == 0):
                        extract(b - 1)
                if last:
                    extract(b)

            for u in range(UNITS):
                take(0, 0, u)
            dve.wait_ge(q_ready, GROUPS)
            spread(0, 0)
            dve.wait_ge(mask_in, 32)
            maxima(0, 0)
            maxima(0, 1)
            normalize(0, 0)
            samples(dve, sample)
            add_out(nc, env, dve, out_done, x_added)


def latent_cross_attention(nc, env, ins):
    LH, LD = 16, 64
    INNER = LH * LD
    PAIRS = LH // 2
    PG = 4
    JOBS = CC
    FIRST = 2 * TT
    with ExitStack() as mem, stage(
            nc, "consts_in", "wq_in", "wout_in", "ctx_in0", "ctx_in1", "mask_in0", "mask_in1", "vstep", "pstep",
            "lat_normed", "lat_ready", "stats_ready", "rstd_ready", "centred", "xn_ready", "rows_turned", "xnT_ready",
            "k_done", "squared", "sums_ready", "factor_ready", "kn_ready", "kn_turned", "kT_a", "kT_b", "qbd_ready",
            "mask_ready", "slat_done", "slat_ready", "scores_done", "max_ready", "exp_done", "probs_ready",
            "turned_a", "turned_b", "probsT_a", "probsT_b", "lat_turned", "latT_ready", "y_done", "y_taken",
            "o_done", "o_ready", "out_done", "x_added", "spare_set", "latb_ready", "reduced", "scaled") as (
            block, consts_in, wq_in, wout_in, ctx_in0, ctx_in1, mask_in0, mask_in1, vstep, pstep,
            lat_normed, lat_ready, stats_ready, rstd_ready, centred, xn_ready, rows_turned, xnT_ready,
            k_done, squared, sums_ready, factor_ready, kn_ready, kn_turned, kT_a, kT_b, qbd_ready,
            mask_ready, slat_done, slat_ready, scores_done, max_ready, exp_done, probs_ready,
            turned_a, turned_b, probsT_a, probsT_b, lat_turned, latT_ready, y_done, y_taken,
            o_done, o_ready, out_done, x_added, spare_set, latb_ready, reduced, scaled):
        sb = allocator(nc, mem)
        ps = env.ps
        wqo = sb("wqo", [P, 8 * D])
        wq = wqo[:].rearrange("p (k n) -> p k n", k=KD)
        wout = wqo[:].rearrange("p (k n) -> p k n", k=INNER // P)
        wk, wv = sb("wk", [P, KD, INNER]), sb("wv", [P, KD, INNER])
        bout = sb("bout", [1, D])
        xg, xb, lg, lb = (sb(n, [P, D]) for n in ("xg", "xb", "lg", "lb"))
        gains = sb("gains", [P, 2])
        lat = sb("lat", [P, TT, D])
        latb = sb("latb", [P, D])
        xn = sb("xn", [P, 2, CC, D])
        mv = sb("mv", [P, CC, 2])
        stats = sb("stats", [P, CC, 6])
        rstd = sb("rstd", [P, CC])
        xnT = sb("xnT", [P, 2, KD, P])
        sq, kn = sb("sq", [P, INNER]), sb("kn", [P, 2, INNER])
        sums, factor = sb("sums", [P, 2, LH]), sb("factor", [P, 2, LH])
        half_less = sb("half_less", [P, 1])
        qT, kTl = sb("qT", [P, PAIRS, T]), sb("kT_lat", [P, PAIRS, T])
        kT = sb("kT", [P, PAIRS, CTX])
        qbd = sb("qbd", [P, PAIRS, 2, SEQ])
        mask8, mask = mem.enter_context(nc.sbuf_tensor("mask8", [P, 2, CTX], mybir.dt.uint8)), sb("mask", [P, CTX])
        slat, lmin = sb("slat", [P, PAIRS, SEQ]), sb("lmin", [P, PAIRS])
        scores, probs = sb("scores", [P, CTX]), sb("probs", [P, 2, CTX])
        plat = sb("plat", [P, PAIRS, SEQ])
        top, total, tlat = sb("top", [P, PAIRS]), sb("total", [P, PAIRS]), sb("tlat", [P, PAIRS])
        probsT, platT = sb("probsT", [P, CC, PG, P]), sb("platT", [P, PG * P])
        y = sb("y", [P, 2, KD, HG, SEQ])
        oT = qT
        spare, step = sb("spare", [P, 1]), sb("step", [P, 1])
        ctx_in, mask_in = (ctx_in0, ctx_in1), (mask_in0, mask_in1)
        halves = lambda ap: ap.rearrange("p b n -> p (b n)")
        Y_BANK, O_BANK, L_BANK, S_BANK, T_BANK = 4, 1, 0, 2, 6

        def samples(eng, body):
            body(0, 0, False)
            with eng.Fori(0, BATCH // 2 - 1) as j:
                body(2 * j + 1, 1, False)
                body(2 * j + 2, 0, False)
            body(BATCH - 1, 1, True)

        @block.sync
        def _(sp):
            sp.dma_start(wq, ins["L1_xattn_Wq"].rearrange("(k p) n -> p k n", p=P)).then_inc(wq_in, 16)
            for dst, src in ((wk, ins["L1_xattn_Wk"].rearrange("(k p) n -> p k n", p=P)),
                             (wv, ins["L1_xattn_Wv"].rearrange("(k p) n -> p k n", p=P)),
                             (lg, rows_of(ins["L1_xattn_ln_l_g"])), (lb, rows_of(ins["L1_xattn_ln_l_b"])),
                             (xg, rows_of(ins["L1_xattn_ln_x_g"])), (xb, rows_of(ins["L1_xattn_ln_x_b"])),
                             (gains, ins["L1_xattn_gains"]), (bout, ins["L1_xattn_bout"].unsqueeze(0))):
                sp.dma_start(dst[:], src).then_inc(consts_in, 16)
            for b in range(BATCH):
                wait(sp, y_done, 4 * (b - 1))
                wait(sp, mask_ready, b - 1)
                sp.dma_start(xn[:, b % 2], ins["ctx"][b].rearrange("(c p) d -> p c d", p=P)).then_inc(ctx_in[b % 2], 16)
                sp.dma_start(mask8[:, b % 2, :], rows_of(ins["mask_ctx"][b])).then_inc(mask_in[b % 2], 16)
                if b == 2:
                    sp.wait_ge(k_done, TT)
                    sp.dma_start(wout, ins["L1_xattn_Wout"].rearrange("(k p) n -> p k n", p=P)).then_inc(wout_in, 16)

        @block.tensor
        def _(pe):
            def jobs(n0, count, source, ready, weight):
                def turn_rows(c):
                    wait(pe, ready, c + 1 if isinstance(n0, int) and n0 < FIRST else n0 - FIRST + c + 1)
                    wait(pe, xnT_ready, n0 + c)
                    for k in range(KD):
                        last = nc.tensor.transpose(ps[:, T_BANK, k * P:(k + 1) * P], source(c)[:, k * P:(k + 1) * P],
                                                   env.ident[:])
                    last.then_inc(rows_turned, 1)

                def product(c):
                    wait(pe, xnT_ready, n0 + c + 1)
                    wait(pe, kn_ready, n0 + c - 1)
                    for half in range(2):
                        last = project(nc, ps[:, 2 * (c % 2) + half, :], lambda k: xnT[:, c % 2, k, :], KD,
                                       lambda k: weight[:, k, half * BANK:(half + 1) * BANK])
                    last.then_inc(k_done, 1)

                def turn_k(c):
                    wait(pe, kn_ready, n0 + c + 1)
                    wait(pe, kT_a, n0 + c)
                    wait(pe, kT_b, n0 + c)
                    for p in range(PAIRS):
                        last = nc.tensor.transpose(ps[:, Y_BANK + p // PG, (p % PG) * P:(p % PG + 1) * P],
                                                   kn[:, c % 2, p * P:(p + 1) * P], env.ident[:])
                    last.then_inc(kn_turned, 1)

                turn_rows(0)
                for c in range(count + 2):
                    if c + 1 < count:
                        turn_rows(c + 1)
                    if c < count:
                        product(c)
                    if c >= 2:
                        turn_k(c - 2)

            def score(b, p):
                wait(pe, max_ready, PAIRS * b + p)
                for half in range(2):
                    last = nc.tensor.matmul(ps[:, S_BANK + half, :], qbd[:, p].rearrange("p h l -> p (h l)"),
                                            kT[:, p, half * BANK:(half + 1) * BANK], start=True, stop=True)
                last.then_inc(scores_done, 1)

            def turn(b, p):
                wait(pe, probs_ready, PAIRS * b + p + 1)
                for half, taken, done in ((0, probsT_a, turned_a), (1, probsT_b, turned_b)):
                    wait(pe, taken, PAIRS * b + p)
                    for c in range(4):
                        last = nc.tensor.transpose(ps[:, T_BANK + half, c * P:(c + 1) * P],
                                                   probs[:, p % 2, (4 * half + c) * P:(4 * half + c + 1) * P],
                                                   env.ident[:])
                    last.then_inc(done, 1)

            def values(b, i, g):
                for j in range(PG):
                    last = nc.tensor.transpose(ps[0:SEQ, L_BANK, j * P:(j + 1) * P], plat[:, PG * g + j, :], env.ident[:])
                last.then_inc(lat_turned, 1)
                wait(pe, probsT_a, PAIRS * b + PG * (g + 1))
                wait(pe, probsT_b, PAIRS * b + PG * (g + 1))
                wait(pe, latb_ready, b + 2 - i)
                for k in range(KD):
                    wait(pe, y_taken, 4 * b + 2 * g + k - 1)
                    for c in range(CC):
                        nc.tensor.matmul(ps[:, Y_BANK + k, :], xn[:, i, c, k * P:(k + 1) * P],
                                         probsT[:, c].rearrange("p j q -> p (j q)"), start=(c == 0), stop=False)
                    if k == 0:
                        wait(pe, latT_ready, 2 * b + g + 1)
                    rows = slice(i * SEQ, (i + 1) * SEQ)
                    nc.tensor.matmul(ps[:, Y_BANK + k, :], latb[rows, k * P:(k + 1) * P], platT[rows, :],
                                     start=False, stop=True).then_inc(y_done, 1)

            def outputs(b, g):
                wait(pe, y_taken, 4 * b + 2 * g + 2)
                for j in range(PG):
                    for k in range(KD):
                        for s in range(2):
                            head = HG * g + 2 * j + s
                            last = nc.tensor.matmul(ps[s * LD:(s + 1) * LD, O_BANK, (PG * g + j) * SEQ:(PG * g + j + 1) * SEQ],
                                                    wv[:, k, head * LD:(head + 1) * LD], y[:, g, k, 2 * j + s, :],
                                                    start=(k == 0), stop=(k == KD - 1))
                last.then_inc(o_done, 1)

            def sample(b, i, last):
                wait(pe, o_ready, b)
                jobs(FIRST + JOBS * b, JOBS, lambda c: xn[:, i, c, :], xn_ready, wk)
                wait(pe, qbd_ready, b + 1)
                wait(pe, kT_a, FIRST + JOBS * (b + 1))
                wait(pe, kT_b, FIRST + JOBS * (b + 1))
                for p in range(PAIRS):
                    ins_ = nc.tensor.matmul(ps[:, L_BANK, p * SEQ:(p + 1) * SEQ], qbd[:, p].rearrange("p h l -> p (h l)"),
                                            kTl[:, p, bass.ds(b * SEQ, SEQ)], start=True, stop=True)
                ins_.then_inc(slat_done, 1)
                score(b, 0)
                for p in range(PAIRS):
                    if p + 1 < PAIRS:
                        score(b, p + 1)
                    if p == PG:
                        values(b, i, 0)
                    turn(b, p)
                values(b, i, 1)
                outputs(b, 0)
                outputs(b, 1)

            pe.wait_ge(wq_in, 16)
            jobs(0, TT, lambda c: lat[:, c, :], lat_ready, wq)
            pe.wait_ge(consts_in, 128)
            jobs(TT, TT, lambda c: lat[:, c, :], lat_ready, wk)
            samples(pe, sample)
            pe.wait_ge(o_ready, BATCH)
            pe.wait_ge(wout_in, 16)
            project_out(nc, env, pe, oT, wout, INNER // P, out_done, bout[:])

        @block.scalar
        def _(act):
            def jobs(n0, count, take):
                def take_rows(c):
                    act.wait_ge(rows_turned, n0 + c + 1)
                    wait(act, k_done, n0 + c - 1)
                    nc.scalar.copy(xnT[:, c % 2].rearrange("p k n -> p (k n)"), ps[:, T_BANK, 0:D])\
                        .then_inc(xnT_ready, 1)

                take_rows(0)
                for c in range(count + 2):
                    if c + 1 < count:
                        take_rows(c + 1)
                    if c < count:
                        act.wait_ge(k_done, n0 + c + 1)
                        wait(act, reduced, n0 + c)
                        nc.scalar.activation(sq[:], halves(ps[:, 2 * (c % 2):2 * (c % 2) + 2, :]), ACT.Square)\
                            .then_inc(squared, 1)
                    if c >= 2:
                        act.wait_ge(kn_turned, n0 + c - 1)
                        take(c - 2).then_inc(kT_a, 1)

            def turned_keys():
                return ps[:, Y_BANK, :].rearrange("p (j r) -> p j r", j=PG)

            def exponentials(b, p):
                act.wait_ge(max_ready, PAIRS * b + p + 1)
                wait(act, turned_b, PAIRS * b + p - 1)
                nc.scalar.activation(probs[:, p % 2, :], scores[:], ACT.Exp, bias=top[:, p:p + 1], scale=-1.0,
                                     accum_out=total[:, p:p + 1]).then_inc(exp_done, 1)
                nc.scalar.activation(plat[:, p, :], slat[:, p, :], ACT.Exp, bias=top[:, p:p + 1], scale=-1.0,
                                     accum_out=tlat[:, p:p + 1]).then_inc(exp_done, 1)

            def take_y(b, g):
                act.wait_ge(y_done, 4 * b + 2 * g + 1)
                nc.scalar.copy(y[:, g, 0].rearrange("p h l -> p (h l)"), ps[:, Y_BANK, :]).then_inc(y_taken, 1)

            def sample(b, i, last):
                jobs(FIRST + JOBS * b, JOBS,
                     lambda c: nc.scalar.copy(kT[:, 0:PG, c * P:(c + 1) * P], turned_keys()))
                act.wait_ge(slat_done, b + 1)
                nc.scalar.activation(slat[:], ps[:, L_BANK, :].rearrange("p (j l) -> p j l", j=PAIRS), ACT.Copy,
                                     scale=-1.0).then_inc(slat_ready, 1)
                exponentials(b, 0)
                for p in range(PAIRS):
                    if p + 1 < PAIRS:
                        exponentials(b, p + 1)
                    if p == PG:
                        take_y(b, 0)
                    act.wait_ge(turned_a, PAIRS * b + p + 1)
                    nc.scalar.copy(probsT[:, 0:4, p % PG, :], ps[:, T_BANK, :].rearrange("p (c q) -> p c q", c=4))\
                        .then_inc(probsT_a, 1)
                take_y(b, 1)

            act.wait_ge(lat_normed, 1)
            gained = lambda dst: nc.scalar.activation(dst, turned_keys(), ACT.Copy, scale=gains[:, 0:1])
            jobs(0, TT, lambda c: gained(qT[:, 0:PG, c * P:(c + 1) * P]))
            jobs(TT, TT, lambda c: nc.scalar.copy(kTl[:, 0:PG, c * P:(c + 1) * P], turned_keys()))
            samples(act, sample)

        @block.gpsimd
        def _(pool):
            def power(dst, src, done):
                return nc.gpsimd.tensor_tensor(dst, src, half_less[:].broadcast_to(list(src.shape)), ALU.pow)\
                    .then_inc(done, 1)

            def affine(buf, c, index):
                wait(pool, centred, index + 1)
                nc.gpsimd.tensor_tensor(buf[:, c, :], buf[:, c, :], xg[:], ALU.mult).then_inc(scaled, 1)
                wait(pool, scaled, index + 1)
                nc.gpsimd.tensor_tensor(buf[:, c, :], buf[:, c, :], xb[:], ALU.add).then_inc(xn_ready, 1)

            def factors(n0, count):
                for c in range(count):
                    wait(pool, sums_ready, n0 + c + 1)
                    power(factor[:, c % 2, :], sums[:, c % 2, :], factor_ready)

            def rows(b, i):
                wait(pool, stats_ready, b + 2)
                power(rstd[:], mv[:, :, 1], rstd_ready)
                for c in range(CC):
                    affine(xn[:, i], c, JOBS * b + c)

            nc.gpsimd.memset(half_less[:], -0.5).then_inc(pstep, 1)
            pool.wait_ge(pstep, 1)
            pool.wait_ge(stats_ready, 1)
            power(rstd[:, 0:TT], mv[:, 0:TT, 1], rstd_ready)
            pool.wait_ge(consts_in, 128)
            rows(0, 0)
            factors(0, TT)
            factors(TT, TT)

            def paired(j):
                pool.wait_ge(lat_ready, TT)
                wait(pool, y_done, 8 * j)
                nc.gpsimd.tensor_copy(latb[:], lat[:, j, :] if isinstance(j, int) else
                                      lat[:, bass.ds(j, 1), :].rearrange("p t d -> p (t d)")).then_inc(latb_ready, 2)

            def body(b, i, last):
                factors(FIRST + JOBS * b, JOBS)
                if not last:
                    rows(b + 1, 1 - i)

            paired(0)
            body(0, 0, False)
            with pool.Fori(0, BATCH // 2 - 1) as j:
                body(2 * j + 1, 1, False)
                paired(j + 1)
                body(2 * j + 2, 0, False)
            body(BATCH - 1, 1, True)

        @block.vector
        def _(dve):
            link = Chain(dve, vstep)

            def jobs(n0, count, take):
                for c in range(count + 2):
                    if 1 <= c <= count:
                        n = n0 + c - 1
                        wait(dve, factor_ready, n + 1)
                        wait(dve, kn_turned, n - 1)
                        nc.vector.tensor_tensor(
                            kn[:, (c - 1) % 2].rearrange("p (h d) -> p h d", h=LH),
                            halves(ps[:, 2 * ((c - 1) % 2):2 * ((c - 1) % 2) + 2, :]).rearrange("p (h d) -> p h d", h=LH),
                            factor[:, (c - 1) % 2, :].unsqueeze(2).broadcast_to([P, LH, LD]), ALU.mult)\
                            .then_inc(kn_ready, 1)
                    if c < count:
                        n = n0 + c
                        wait(dve, squared, n + 1)
                        wait(dve, factor_ready, n - 1)
                        nc.vector.tensor_reduce(sums[:, c % 2, :], sq[:].rearrange("p (h d) -> p h d", h=LH),
                                                AX.X, ALU.add).then_inc(reduced, 1)
                        wait(dve, reduced, n + 1)
                        nc.vector.tensor_scalar(sums[:, c % 2, :], sums[:, c % 2, :], 1.0 / LD, 1e-16, ALU.mult,
                                                ALU.max).then_inc(sums_ready, 1)
                    if c >= 2:
                        dve.wait_ge(kn_turned, n0 + c - 1)
                        take(c - 2).then_inc(kT_b, 1)

            def turned_keys():
                return ps[:, Y_BANK + 1, :].rearrange("p (j r) -> p j r", j=PG)

            def maxima(b, p):
                n = PAIRS * b + p
                dve.wait_ge(scores_done, n + 1)
                wait(dve, exp_done, 2 * n)
                wait(dve, spare_set, n)
                nc.vector.memset(spare[:], 0.0).then_inc(spare_set, 1)
                nc.vector.tensor_tensor_reduce(
                    out=scores[:], in0=halves(ps[:, S_BANK:S_BANK + 2, :]), in1=mask[:], scale=-1.0,
                    scalar=lmin[:, p:p + 1], op0=ALU.add, op1=ALU.min, accum_out=top[:, p:p + 1]).then_inc(max_ready, 1)

            def normalize(b, p):
                n = PAIRS * b + p
                dve.wait_ge(exp_done, 2 * n + 2)
                link(nc.vector.tensor_tensor(total[:, p:p + 1], total[:, p:p + 1], tlat[:, p:p + 1], ALU.add))
                link(nc.vector.reciprocal(total[:, p:p + 1], total[:, p:p + 1]))
                link(nc.vector.tensor_scalar(plat[:, p, :], plat[:, p, :], total[:, p:p + 1], None, ALU.mult))
                nc.vector.tensor_scalar(probs[:, p % 2, :], probs[:, p % 2, :], total[:, p:p + 1], None, ALU.mult)\
                    .then_inc(probs_ready, 1)

            def rows_stats(i):
                for c in range(CC):
                    nc.vector.bn_stats(stats[:, c, :], xn[:, i, c, :]).then_inc(vstep, 1)
                    link.n += 1
                dve.wait_ge(vstep, link.base + link.n)
                nc.vector.memset(step[:], 0.0).then_inc(vstep, 1)
                link.n += 1
                for c in range(CC):
                    nc.vector.bn_aggr(mv[:, c, :], stats[:, c, :]).then_inc(vstep, 1)
                    link.n += 1
                dve.wait_ge(vstep, link.base + link.n)
                nc.vector.tensor_scalar(mv[:, :, 1], mv[:, :, 1], LN_EPS, None, ALU.add).then_inc(stats_ready, 1)

            def centre(i, c):
                nc.vector.tensor_scalar(xn[:, i, c, :], xn[:, i, c, :], mv[:, c, 0:1], rstd[:, c:c + 1],
                                        ALU.subtract, ALU.mult).then_inc(centred, 1)

            def take_y(b, g):
                dve.wait_ge(y_done, 4 * b + 2 * g + 2)
                nc.vector.tensor_copy(y[:, g, 1].rearrange("p h l -> p (h l)"), ps[:, Y_BANK + 1, :]).then_inc(y_taken, 1)

            def take_latents(b, i, g):
                dve.wait_ge(lat_turned, 2 * b + g + 1)
                nc.vector.tensor_copy(platT[i * SEQ:(i + 1) * SEQ, :], ps[0:SEQ, L_BANK, :]).then_inc(latT_ready, 1)

            PER_SAMPLE = 3 + 3 * PAIRS + 2 * CC

            def sample(b, i, last):
                link.restart(before + PER_SAMPLE * b)
                wait(dve, qbd_ready, b)
                nc.vector.tensor_tensor(
                    qbd[:], qT[:, :, bass.ds(b * SEQ, SEQ)].unsqueeze(2).broadcast_to([P, PAIRS, 2, SEQ]),
                    env.half_mask[:].unsqueeze(1).unsqueeze(3).broadcast_to([P, PAIRS, 2, SEQ]), ALU.mult)\
                    .then_inc(qbd_ready, 1)
                jobs(FIRST + JOBS * b, JOBS,
                     lambda c: nc.vector.tensor_copy(kT[:, PG:PAIRS, c * P:(c + 1) * P], turned_keys()))
                wait(dve, mask_in[i], 16 * (b // 2 + 1) if isinstance(b, int) else 8 * b + 16 - 8 * i)
                nc.vector.tensor_scalar(mask[:], mask8[:, i, :], -1.0, 1e30, ALU.add, ALU.mult).then_inc(mask_ready, 1)
                dve.wait_ge(slat_ready, b + 1)
                link(nc.vector.tensor_reduce(lmin[:], slat[:], AX.X, ALU.min))
                wait(dve, mask_ready, b + 1)
                maxima(b, 0)
                for p in range(PAIRS):
                    normalize(b, p)
                    if p + 1 < PAIRS:
                        maxima(b, p + 1)
                    if p == PG:
                        take_latents(b, i, 0)
                        take_y(b, 0)
                    dve.wait_ge(turned_b, PAIRS * b + p + 1)
                    nc.vector.tensor_copy(probsT[:, 4:8, p % PG, :],
                                          ps[:, T_BANK + 1, :].rearrange("p (c q) -> p c q", c=4)).then_inc(probsT_b, 1)
                    if not last:
                        if p == 1:
                            wait(dve, ctx_in[1 - i], 8 * b + 16 + 8 * i)
                            rows_stats(1 - i)
                        if p == 2:
                            dve.wait_ge(rstd_ready, b + 3)
                        if 2 <= p < 6:
                            centre(1 - i, 2 * (p - 2))
                            centre(1 - i, 2 * (p - 2) + 1)
                take_latents(b, i, 1)
                take_y(b, 1)
                dve.wait_ge(o_done, 2 * b + 2)
                nc.vector.memset(step[:], 0.0).then_inc(vstep, 1)
                link.n += 1
                nc.vector.tensor_copy(oT[:, :, bass.ds(b * SEQ, SEQ)],
                                      ps[:, O_BANK, :].rearrange("p (j l) -> p j l", j=PAIRS)).then_inc(o_ready, 1)

            for t in range(TT):
                link(nc.vector.bn_stats(stats[:, t, :], env.h[:, t, :]))
            for t in range(TT):
                link(nc.vector.bn_aggr(mv[:, t, :], stats[:, t, :]))
            nc.vector.tensor_scalar(mv[:, 0:TT, 1], mv[:, 0:TT, 1], LN_EPS, None, ALU.add).then_inc(stats_ready, 1)
            dve.wait_ge(rstd_ready, 1)
            dve.wait_ge(consts_in, 128)
            for t in range(TT):
                link(nc.vector.tensor_scalar(lat[:, t, :], env.h[:, t, :], mv[:, t, 0:1], rstd[:, t:t + 1],
                                             ALU.subtract, ALU.mult))
                link(nc.vector.tensor_tensor(lat[:, t, :], lat[:, t, :], lg[:], ALU.mult))
                nc.vector.tensor_tensor(lat[:, t, :], lat[:, t, :], lb[:], ALU.add).then_inc(lat_ready, 1)
            link(nc.vector.tensor_tensor(gains[:, 0:1], gains[:, 0:1], gains[:, 1:2], ALU.mult))
            link(nc.vector.tensor_scalar(gains[:, 0:1], gains[:, 0:1], LD ** -0.5, None, ALU.mult))
            nc.vector.engine_nop().then_inc(lat_normed, 1)
            dve.wait_ge(ctx_in0, 16)
            rows_stats(0)
            dve.wait_ge(rstd_ready, 2)
            for c in range(CC):
                centre(0, c)
            jobs(0, TT, lambda c: nc.vector.tensor_scalar(qT[:, PG:PAIRS, c * P:(c + 1) * P], turned_keys(),
                                                          gains[:, 0:1], None, ALU.mult))
            jobs(TT, TT, lambda c: nc.vector.tensor_copy(kTl[:, PG:PAIRS, c * P:(c + 1) * P], turned_keys()))
            dve.wait_ge(kT_a, 2 * TT)
            dve.wait_ge(kT_b, 2 * TT)
            before = link.n
            samples(dve, sample)
            add_out(nc, env, dve, out_done, x_added)


def gated_latent_attention(nc, env, ins):
    NH, NOPE, HALF = 16, 32, 32
    QK = NOPE + 2 * HALF
    RANK_Q, RANK_KV, VH = 96, 32, 32
    W = NH * NOPE
    KR, GATE = RANK_Q + RANK_KV, RANK_Q + RANK_KV + 2 * HALF
    MISC = GATE + 3
    K1, KS, KW, Q = range(4)
    RING, LAG = 4, 3
    T_BANK, O_BANK = 2, 7
    score_bank = lambda h: (0, 1, 4, 5)[h % RING]
    turn_order = [(a, g) for a in (KS, KW, Q, K1) for g in range(4)]
    with ExitStack() as mem, stage(
            nc, "consts_in", "wide_in", "zeroed", "hTt_ready", "misc_done", "misc_taken", "squared", "means_ready",
            "rs_ready", "normed", "nT_done", "nT_ready", "gate_sum", "gate_max", "gate_exp", "a_done", "act_took",
            "mults", "roped", "kr_ready", "kr_spread", "heads_turned", "turned_a", "turned_d", "scores_done",
            "max_ready", "exp_done", "factor_ready", "scaled", "turned", "probsT_ready", "pv_done", "o_ready",
            "out_done", "x_added", "vstep") as (
            block, consts_in, wide_in, zeroed, hTt_ready, misc_done, misc_taken, squared, means_ready,
            rs_ready, normed, nT_done, nT_ready, gate_sum, gate_max, gate_exp, a_done, act_took,
            mults, roped, kr_ready, kr_spread, heads_turned, turned_a, turned_d, scores_done,
            max_ready, exp_done, factor_ready, scaled, turned, probsT_ready, pv_done, o_ready,
            out_done, x_added, vstep):
        sb = allocator(nc, mem)
        ps = env.ps
        w_misc = sb("w_misc", [P, KD, MISC])
        w_sel, w_win = sb("w_sel", [P, KD, 4 * W]), sb("w_win", [P, KD, 4 * W])
        w_lat = sb("w_lat", [P, 5 * W])
        w_proj = sb("w_proj", [P, 4, D])
        gain, mean64 = sb("gain", [P, 1]), sb("mean64", [P, P])
        masks = sb("masks", [P, 2, P])
        cos, sin = sb("cos", [P, HALF]), sb("sin", [P, HALF])
        hTt = sb("hTt", [P, KD, P])
        misc, squares = sb("misc", [P, MISC]), sb("squares", [P, KR])
        ms, half_less = sb("ms", [P, 2]), sb("half_less", [P, 1])
        nr, nT = sb("nr", [P, P]), sb("nT", [P, P])
        gate, gtop, gtotal = sb("gate", [P, 3]), sb("gtop", [P, 1]), sb("gtotal", [P, 1])
        kt, kr, part = sb("kt", [P, 4, HALF]), sb("kr", [P, 2 * HALF]), sb("part", [P, NH])
        tmp = sb("rope_tmp", [P, 2, 4, W])
        tok, turn = sb("tok", [P, 4, NH, P]), sb("turn", [P, 4, NH, P])
        v = sb("v", [P, 3, W])
        neg, probs = sb("neg", [P, RING, 3, P]), sb("probs", [P, RING, 3, P])
        top, total, factor = sb("top", [P, RING, 3]), sb("total", [P, RING, 3]), sb("factor", [P, RING, 3])
        probsT = sb("probsT", [P, 2, 3, P])
        oT = sb("oT", [P, 4, T])
        step = sb("step", [P, 2])
        by_head = lambda ap: ap.rearrange("p (h d) -> p h d", h=NH)

        def tiles(eng, body):
            body(0)
            with eng.Fori(1, TT) as t:
                body(t)

        @block.sync
        def _(sp):
            sp.dma_start(w_misc[:], ins["L3_attn_misc"].rearrange("(k p) n -> p k n", p=P)).then_inc(consts_in, 16)
            for dst, src in ((gain, ins["L3_attn_gain"].unsqueeze(1)), (mean64, env.consts["mean64"]),
                             (masks, env.consts["masks"]), (cos, env.consts["cos64"]), (sin, env.consts["sin64"])):
                sp.dma_start(dst[:], src).then_inc(consts_in, 16)
            sp.dma_start(w_sel[:], ins["L3_attn_sel"].rearrange("(k p) n -> p k n", p=P)).then_inc(wide_in, 16)
            sp.dma_start(w_win[:], ins["L3_attn_win"].rearrange("(k p) n -> p k n", p=P)).then_inc(wide_in, 16)
            sp.dma_start(w_lat[:], ins["L3_attn_lat"]).then_inc(wide_in, 16)
            sp.dma_start(w_proj[:], ins["L3_attn_w_proj"].rearrange("(k p) n -> p k n", p=P)).then_inc(wide_in, 16)

        @block.tensor
        def _(pe):
            def wide(bank, weight, part):
                project(nc, ps[:, bank, :], lambda k: hTt[:, k, :], KD,
                        lambda k: weight[:, k, part * W:(part + 1) * W]).then_inc(a_done, 1)

            def low(bank, part):
                nc.tensor.matmul(ps[:, bank, :], nT[:], w_lat[:, part * W:(part + 1) * W], start=True, stop=True)\
                    .then_inc(a_done, 1)

            def tile(t):
                wait(pe, o_ready, t)
                pe.wait_ge(hTt_ready, t + 1)
                project(nc, ps[:, 0, 0:MISC], lambda k: hTt[:, k, :], KD, lambda k: w_misc[:, k, :]).then_inc(misc_done, 1)
                if isinstance(t, int):
                    pe.wait_ge(wide_in, 64)
                for part in range(4):
                    wide(1 + part, w_sel, part)
                pe.wait_ge(misc_taken, t + 1)
                nc.tensor.matmul(ps[:, 0, 0:3], mean64[:], misc[:, GATE:MISC], start=True, stop=True).then_inc(gate_sum, 1)
                for part in range(3):
                    wide(5 + part, w_win, part)
                pe.wait_ge(act_took, 7 * t + 1)
                wide(1, w_win, 3)
                pe.wait_ge(normed, 2 * t + 2)
                pe.wait_ge(gate_max, t + 1)
                nc.tensor.transpose(ps[:, 0, 0:P], nr[:], env.ident[:]).then_inc(nT_done, 1)
                pe.wait_ge(nT_ready, t + 1)
                pe.wait_ge(act_took, 7 * t + 2)
                low(4, 0)
                pe.wait_ge(mults, 12 * t + 4)
                low(2, 1)
                low(3, 2)
                pe.wait_ge(act_took, 7 * t + 4)
                low(5, 3)
                low(1, 4)
                pe.wait_ge(mults, 12 * t + 8)
                for m, (a, g) in enumerate(turn_order):
                    if g == 0:
                        pe.wait_ge(*((kr_spread, t + 1) if a == K1 else
                                     (roped, 6 * t + 2 * {KS: 1, KW: 2, Q: 3}[a])))
                        pe.wait_ge(act_took, 7 * t + 7)
                    if m >= 4:
                        done = turned_d if m % 2 else turned_a
                        pe.wait_ge(done, 8 * t + m // 2 - 1)
                    for j in range(4):
                        last = nc.tensor.transpose(ps[:, (6, 7, 0, 1)[m % 4], j * P:(j + 1) * P], tok[:, a, 4 * g + j, :],
                                                   env.ident[:])
                    last.then_inc(heads_turned, 1)
                pe.wait_ge(turned_a, 8 * t + 8)
                pe.wait_ge(turned_d, 8 * t + 8)
                pe.wait_ge(mults, 12 * t + 12)
                for m in range(NH + LAG + 1):
                    n = NH * t + m
                    if m < NH:
                        if m >= RING:
                            wait(pe, max_ready, 3 * (n - RING + 1))
                        for a in range(3):
                            last = nc.tensor.matmul(ps[:, score_bank(m), a * P:(a + 1) * P], turn[:, Q, m, :],
                                                    turn[:, a, m, :], start=True, stop=True)
                        last.then_inc(scores_done, 1)
                    if LAG <= m < NH + LAG:
                        h = m - LAG
                        wait(pe, scaled, n - LAG + 1)
                        wait(pe, probsT_ready, n - LAG - 1)
                        for a in range(3):
                            last = nc.tensor.transpose(ps[:, T_BANK + h % 2, a * P:(a + 1) * P], probs[:, h % RING, a, :],
                                                       env.ident[:])
                        last.then_inc(turned, 1)
                    if m > LAG:
                        h = m - LAG - 1
                        wait(pe, probsT_ready, n - LAG)
                        for a in range(3):
                            last = nc.tensor.matmul(ps[32 * (h % 4):32 * (h % 4) + 32, O_BANK, (h // 4) * P:(h // 4 + 1) * P],
                                                    v[:, a, h * VH:(h + 1) * VH], probsT[:, h % 2, a, :],
                                                    start=(a == 0), stop=(a == 2))
                        last.then_inc(pv_done, 1)

            pe.wait_ge(consts_in, 96)
            tiles(pe, tile)
            pe.wait_ge(o_ready, TT)
            project_out(nc, env, pe, oT, w_proj, 4, out_done)

        @block.scalar
        def _(act):
            def tile(t):
                act.wait_ge(misc_taken, t + 1)
                nc.scalar.activation(squares[:, 0:RANK_Q], misc[:, 0:RANK_Q], ACT.Square, accum_out=ms[:, 0:1])\
                    .then_inc(squared, 1)
                nc.scalar.activation(squares[:, RANK_Q:KR], misc[:, RANK_Q:KR], ACT.Square, accum_out=ms[:, 1:2])\
                    .then_inc(squared, 1)

                def take(unit, bank, dst):
                    act.wait_ge(a_done, 13 * t + unit)
                    nc.scalar.copy(dst, by_head(ps[:, bank, :])).then_inc(act_took, 1)

                nope = lambda a: tok[:, a, :, 0:NOPE]
                value = lambda a: by_head(v[:, a, :])
                take(1, 1, nope(KS))
                take(4, 4, value(KS))
                act.wait_ge(gate_max, t + 1)
                nc.scalar.activation(gate[:], gate[:], ACT.Exp, bias=gtop[:], accum_out=gtotal[:]).then_inc(gate_exp, 1)
                take(5, 5, nope(KW))
                take(8, 1, value(KW))
                act.wait_ge(nT_done, t + 1)
                nc.scalar.activation(nT[:], ps[:, 0, 0:P], ACT.Copy, scale=gain[:]).then_inc(nT_ready, 1)
                take(9, 4, nope(Q))
                take(12, 5, nope(K1))
                take(13, 1, value(K1))
                for m, (a, g) in enumerate(turn_order):
                    if m % 2 == 0:
                        act.wait_ge(heads_turned, 16 * t + m + 1)
                        nc.scalar.copy(turn[:, a, 4 * g:4 * g + 4, :].rearrange("p h n -> p (h n)"),
                                       ps[:, (6, 7, 0, 1)[m % 4], :]).then_inc(turned_a, 1)
                for m in range(NH + LAG):
                    n = NH * t + m
                    if m < NH:
                        wait(act, turned, n - RING + 1)
                        for a in range(3):
                            act.wait_ge(max_ready, 3 * n + a + 1)
                            nc.scalar.activation(probs[:, m % RING, a, :], neg[:, m % RING, a, :], ACT.Exp,
                                                 bias=top[:, m % RING, a:a + 1], scale=-1.0,
                                                 accum_out=total[:, m % RING, a:a + 1]).then_inc(exp_done, 1)
                    if m >= LAG:
                        h = m - LAG
                        wait(act, turned, n - LAG + 1)
                        wait(act, pv_done, n - LAG - 1)
                        nc.scalar.copy(probsT[:, h % 2].rearrange("p a n -> p (a n)"), ps[:, T_BANK + h % 2, 0:3 * P])\
                            .then_inc(probsT_ready, 1)

            act.wait_ge(zeroed, 3)
            tiles(act, tile)

        @block.gpsimd
        def _(pool):
            nc.gpsimd.memset(half_less[:], -0.5).then_inc(zeroed, 1)
            nc.gpsimd.memset(part[:], 1.0 / NH).then_inc(zeroed, 1)

            def rope(t, i, a):
                pool.wait_ge(mults, 12 * t + 4 * (i + 1))
                nc.gpsimd.tensor_tensor(tok[:, a, :, NOPE:NOPE + HALF], by_head(tmp[:, i % 2, 0]),
                                        by_head(tmp[:, i % 2, 1]), ALU.subtract).then_inc(roped, 1)
                nc.gpsimd.tensor_tensor(tok[:, a, :, NOPE + HALF:QK], by_head(tmp[:, i % 2, 2]),
                                        by_head(tmp[:, i % 2, 3]), ALU.add).then_inc(roped, 1)

            def tile(t):
                pool.wait_ge(means_ready, 2 * t + 2)
                nc.gpsimd.tensor_tensor(ms[:], ms[:], half_less[:].broadcast_to([P, 2]), ALU.pow).then_inc(rs_ready, 1)
                rope(t, 0, KS)
                pool.wait_ge(kr_ready, t + 1)
                nc.gpsimd.tensor_tensor(tok[:, K1, :, NOPE:QK], kr[:].unsqueeze(1).broadcast_to([P, NH, 2 * HALF]),
                                        part[:].unsqueeze(2).broadcast_to([P, NH, 2 * HALF]), ALU.mult)\
                    .then_inc(kr_spread, 1)
                rope(t, 1, KW)
                rope(t, 2, Q)
                for m in range(NH):
                    n = NH * t + m
                    pool.wait_ge(factor_ready, n + 1)
                    nc.gpsimd.tensor_tensor(probs[:, m % RING], probs[:, m % RING],
                                            factor[:, m % RING, :].unsqueeze(2).broadcast_to([P, 3, P]), ALU.mult)\
                        .then_inc(scaled, 1)

            pool.wait_ge(zeroed, 3)
            tiles(pool, tile)

        @block.vector
        def _(dve):
            link = Chain(dve, vstep)
            PER_TILE = 6 + 2 + NH * 2 + 1

            def carry(i):
                nc.vector.memset(step[:, i:i + 1], 0.0).then_inc(vstep, 1)
                link.n += 1

            def rope(t, i, unit, b1, b2):
                dve.wait_ge(a_done, 13 * t + unit)
                if i == 2:
                    dve.wait_ge(roped, 6 * t + 2)
                for n, (bank, table) in enumerate(((b1, cos), (b2, sin), (b1, sin), (b2, cos))):
                    nc.vector.tensor_tensor(by_head(tmp[:, i % 2, n]), by_head(ps[:, bank, :]),
                                            table[:].unsqueeze(1).broadcast_to([P, NH, HALF]), ALU.mult)\
                        .then_inc(mults, 1)

            def tile(t):
                link.restart(before + PER_TILE * t)
                nc.vector.tensor_copy(hTt[:], env.hT[:, :, bass.ds(t * P, P)]).then_inc(hTt_ready, 1)
                dve.wait_ge(misc_done, t + 1)
                nc.vector.tensor_copy(misc[:], ps[:, 0, 0:MISC]).then_inc(misc_taken, 1)
                for i, rank in ((0, RANK_Q), (1, RANK_KV)):
                    dve.wait_ge(squared, 2 * t + i + 1)
                    nc.vector.tensor_scalar(ms[:, i:i + 1], ms[:, i:i + 1], 1.0 / rank, 1e-6, ALU.mult, ALU.add)\
                        .then_inc(means_ready, 1)
                rope(t, 0, 3, 2, 3)
                dve.wait_ge(rs_ready, t + 1)
                for i, cols in ((0, slice(0, RANK_Q)), (1, slice(RANK_Q, KR))):
                    nc.vector.tensor_scalar(nr[:, cols], misc[:, cols], ms[:, i:i + 1], None, ALU.mult)\
                        .then_inc(normed, 1)
                dve.wait_ge(gate_sum, t + 1)
                link(nc.vector.tensor_copy(gate[:], ps[:, 0, 0:3]))
                nc.vector.tensor_reduce(gtop[:], gate[:], AX.X, ALU.max, negate=True).then_inc(gate_max, 1)
                for n, (x, table) in enumerate(((0, cos), (1, sin), (0, sin), (1, cos))):
                    nc.vector.tensor_tensor(kt[:, n], misc[:, KR + x * HALF:KR + (x + 1) * HALF], table[:], ALU.mult)\
                        .then_inc(vstep, 1)
                    link.n += 1
                dve.wait_ge(vstep, link.base + link.n)
                nc.vector.tensor_tensor(kr[:, 0:HALF], kt[:, 0], kt[:, 1], ALU.subtract).then_inc(vstep, 1)
                link.n += 1
                nc.vector.tensor_tensor(kr[:, HALF:], kt[:, 2], kt[:, 3], ALU.add).then_inc(kr_ready, 1)
                dve.wait_ge(gate_exp, t + 1)
                link(nc.vector.reciprocal(gtotal[:], gtotal[:]))
                link(nc.vector.tensor_scalar(gate[:], gate[:], gtotal[:], None, ALU.mult))
                rope(t, 1, 7, 6, 7)
                rope(t, 2, 11, 2, 3)
                for m, (a, g) in enumerate(turn_order):
                    if m % 2 == 1:
                        dve.wait_ge(heads_turned, 16 * t + m + 1)
                        nc.vector.tensor_copy(turn[:, a, 4 * g:4 * g + 4, :].rearrange("p h n -> p (h n)"),
                                              ps[:, (6, 7, 0, 1)[m % 4], :]).then_inc(turned_d, 1)
                for m in range(NH + 1):
                    n = NH * t + m
                    if m < NH:
                        dve.wait_ge(scores_done, n + 1)
                        wait(dve, exp_done, 3 * (n - RING + 1))
                        carry(m % 2)
                        for a in range(3):
                            nc.vector.tensor_tensor_reduce(
                                out=neg[:, m % RING, a, :], in0=ps[:, score_bank(m), a * P:(a + 1) * P],
                                in1=masks[:, a % 2, :], scale=-1.0, scalar=3e38, op0=ALU.add, op1=ALU.min,
                                accum_out=top[:, m % RING, a:a + 1]).then_inc(max_ready, 1)
                    if m >= 1:
                        i = (m - 1) % RING
                        dve.wait_ge(exp_done, 3 * n)
                        link(nc.vector.reciprocal(total[:, i], total[:, i]))
                        nc.vector.tensor_tensor(factor[:, i], total[:, i], gate[:], ALU.mult).then_inc(factor_ready, 1)
                dve.wait_ge(pv_done, NH * (t + 1))
                carry(0)
                nc.vector.tensor_copy(oT[:, :, bass.ds(t * P, P)], ps[:, O_BANK, :].rearrange("p (g n) -> p g n", g=4))\
                    .then_inc(o_ready, 1)

            dve.wait_ge(consts_in, 96)
            link(nc.vector.tensor_scalar(gain[0:RANK_Q], gain[0:RANK_Q], QK ** -0.5, None, ALU.mult))
            nc.vector.memset(tok[:].rearrange("p a h n -> p (a h) n")[:, :, QK:], 0.0).then_inc(zeroed, 1)
            before = link.n
            tiles(dve, tile)
            add_out(nc, env, dve, out_done, x_added)


def build(nc, ins, consts, out):
    env = Env()
    nc.stage_sem_base = min(nc.free_semaphores)
    with ExitStack() as mem:
        sb = lambda name, shape: mem.enter_context(nc.sbuf_tensor(name, shape, F32))
        env.ps = mem.enter_context(nc.psum_tensor("psum", [P, 8, BANK], F32))
        env.x, env.h, env.hT = sb("x", [P, TT, D]), sb("h", [P, TT, D]), sb("hT", [P, KD, T])
        env.ident, env.head_mask = sb("ident", [P, P]), sb("head_mask", [P, HG])
        env.pair_mask, env.same_sample = sb("pair_mask", [P, 2]), sb("same_sample", [P, P])
        env.half_mask = sb("half_mask", [P, 2])
        env.consts = consts
        env.eps, env.ones = sb("eps", [P, 4]), sb("ones", [P, BANK])

        with stage(nc, "loaded", "filled") as (block, loaded, filled):
            @block.sync
            def _(sp):
                sp.dma_start(env.x[:], ins["x"].rearrange("(t p) d -> p t d", p=P)).then_inc(loaded, 16)
                sp.dma_start(env.ident[:], consts["ident"]).then_inc(loaded, 16)
                sp.dma_start(env.head_mask[:], consts["head_mask"]).then_inc(loaded, 16)
                sp.dma_start(env.pair_mask[:], consts["pair_mask"]).then_inc(loaded, 16)
                sp.dma_start(env.same_sample[:], consts["same_sample"]).then_inc(loaded, 16)
                sp.dma_start(env.half_mask[:], consts["half_mask"]).then_inc(loaded, 16)
                sp.wait_ge(loaded, 96)

            @block.vector
            def _(dve):
                for i, e in enumerate((1e-5, 1e-6, 1.0, 0.0)):
                    nc.vector.memset(env.eps[:, i:i + 1], e).then_inc(filled, 1)
                nc.vector.memset(env.ones[:], 1.0).then_inc(filled, 1)
                dve.wait_ge(filled, 5)

        for n in ONLY:
            layernorm(nc, env, ins["L1_attn_pe"] if n == 4 else None)
            LAYERS[n](nc, env, ins)

        with stage(nc, "stored") as (block, stored):
            @block.sync
            def _(sp):
                sp.dma_start(out.rearrange("(t p) d -> p t d", p=P), env.x[:]).then_inc(stored, 16)
                sp.wait_ge(stored, 16)


LAYERS = {
    0: lambda nc, env, ins: sigmoid_cross_attention(
        nc, env, {n: ins["L0_xattn_" + n] for n in ("WqT", "WkT", "WvT", "WoT")}, ins["ctxT"]),
    1: selective_scan,
    2: moe_top2,
    3: latent_cross_attention,
    4: self_attention,
    6: context_fusion,
    7: rotary_attention,
    9: softmax_cross_attention,
    5: ternary_mlp,
    8: binary_mlp,
    10: gated_latent_attention,
    11: grouped_moe,
}


def constants():
    p = np.arange(P)
    same = p[:, None] // SEQ == p[None, :] // SEQ
    theta = np.power(np.float32(10000.0), np.float32(-2.0) * (np.arange(D // 2, dtype=np.float32) - 1) / D)
    angle = (theta[:, None] * np.arange(SEQ, dtype=np.float32)[None, :]).astype(np.float32)
    freq = (1.0 / np.float32(10000.0) ** (np.arange(0, 64, 2, dtype=np.float32) / np.float32(64))).astype(np.float32)
    angle64 = np.outer((p % SEQ).astype(np.float32), freq).astype(np.float32)
    causal = same & (p[None, :] <= p[:, None])
    return {
        "cos64": np.cos(angle64), "sin64": np.sin(angle64), "mean64": same.astype(np.float32) / SEQ,
        "masks": np.where(np.stack([causal, same], axis=1), 0, -1e30).astype(np.float32),
        "pair_mask": (p[:, None] % 32 // HD == np.arange(2)[None, :]).astype(np.float32),
        "half_mask": (p[:, None] // SEQ == np.arange(2)[None, :]).astype(np.float32),
        "same": same.astype(np.float32),
        "same_sample": np.where(same, 0, -1e30).astype(np.float32),
        "cos256": np.cos(angle), "sin256": np.sin(angle),
        "pick": np.eye(P, dtype=np.float32)[:, 16:48],
        "ident": np.eye(P, dtype=np.float32),
        "head_mask": (p[:, None] // HD == np.arange(HG)[None, :]).astype(np.float32),
    }


def layout(inputs):
    a = {k: np.asarray(v) for k, v in inputs.items()}
    ctx = a["ctx_1024"]
    out = {"x": a["x"].reshape(T, D), "ctx": ctx, "ctxT": ctx.transpose(0, 2, 1)}
    for n in ("Wq", "Wk", "Wv", "Wo"):
        out[f"L0_xattn_{n}T"] = a[f"L0_xattn_{n}"].T
    for n in ("wq", "wk", "wv", "wo"):
        out[f"L3_xattn_{n}"] = a[f"L3_xattn_{n}"]
    out["mask"] = a["mask_1x1xSxS2_ff0"][0, 0]
    w_kv = a["L1_xattn_Wkv"]
    out["L1_xattn_Wk"], out["L1_xattn_Wv"] = w_kv[:, :D * 4], w_kv[:, D * 4:]
    for n in ("Wq", "Wout", "bout", "ln_x_g", "ln_x_b", "ln_l_g", "ln_l_b"):
        out[f"L1_xattn_{n}"] = a[f"L1_xattn_{n}"]
    out["L1_xattn_gains"] = np.stack([np.tile(a[f"L1_xattn_{n}"], 2) for n in ("qn_g", "kn_g")], axis=1)
    out["mask_ctx"] = a["mask_BxS2_bf1"].view(np.uint8)
    out["L1_attn_pe"] = a["L1_attn_pe"][0, :SEQ]
    for n in ("wq", "wk", "wv", "wo", "bv", "bo", "gamma", "beta"):
        out[f"L1_attn_{n}"] = a[f"L1_attn_{n}"]
    for n in ("bq", "bk"):
        out[f"L1_attn_{n}"] = a[f"L1_attn_{n}"].reshape(KD, P).T
    for n in ("W_in", "W_x", "W_dt", "W_out"):
        out[f"L0_attn_{n}T"] = a[f"L0_attn_{n}"].T
    for n in ("b_x", "b_out", "A_log"):
        out[f"L0_attn_{n}"] = a[f"L0_attn_{n}"]
    for n in ("b_in", "b_dt", "D"):
        out[f"L0_attn_{n}"] = a[f"L0_attn_{n}"].reshape(-1, P).T
    w_sim = a["L2_xattn_w_sim"].reshape(3, D)
    out["L2_xattn_w1"] = w_sim[0]
    out["L2_xattn_w23"] = w_sim[1:].reshape(2, KD, P).transpose(2, 0, 1)
    for n in ("b_sim", "W_qv", "b_qv"):
        out[f"L2_xattn_{n}"] = a[f"L2_xattn_{n}"]
    for n in ("wq", "wk"):
        out[f"L2_attn_{n}T"] = a[f"L2_attn_{n}"].reshape(D // 2, 2, D).transpose(2, 1, 0).reshape(D, D)
    out["L2_attn_wvT"] = a["L2_attn_wv"].T
    columns = lambda v: v.reshape(v.shape[:-1] + (-1, P))
    for n in ("W1", "W2", "b2", "gate_W", "shared_W", "shared_b", "gamma", "beta"):
        out[f"L0_ffn_{n}"] = a[f"L0_ffn_{n}"]
    out["L0_ffn_b1"] = columns(a["L0_ffn_b1"]).transpose(2, 0, 1)
    blocks = lambda w: w.reshape(w.shape[0] // P, P, -1, P).transpose(0, 3, 2, 1)
    for n in ("w1", "w2", "h1", "h2"):
        out[f"L1_ffn_{n}"] = blocks(a[f"L1_ffn_{n}_w"])
    out["L1_ffn_w3T"] = a["L1_ffn_w3_w"].T
    out["L1_ffn_w3_s"] = a["L1_ffn_w3_s"]
    out["L1_ffn_scales"] = np.stack([columns(a[f"L1_ffn_{n}_s"]) for n in ("w1", "w2", "h1", "h2")]).transpose(2, 0, 1)
    for n in ("w1", "w2", "b2"):
        out[f"L2_ffn_{n}"] = a[f"L2_ffn_{n}"]
    out["L2_ffn_b1"] = columns(a["L2_ffn_b1"]).T
    out["L3_ffn_gate_wT"] = a["L3_ffn_gate_w"].T
    out["L3_ffn_gate_bias"] = a["L3_ffn_gate_bias"]
    for n in ("gate", "up"):
        shared = a[f"L3_ffn_shared_{n}"].reshape(2, P, D)
        out[f"L3_ffn_{n}T"] = np.concatenate([a[f"L3_ffn_expert_{n}"], shared]).transpose(0, 2, 1)
    shared = a["L3_ffn_shared_down"].T.reshape(2, P, D)
    out["L3_ffn_downT"] = np.concatenate([a["L3_ffn_expert_down"].transpose(0, 2, 1), shared])
    g = lambda n: a["L3_attn_" + n]
    out["L3_attn_misc"] = np.concatenate([g("w_cq"), g("w_ckv"), g("w_krope"), g("w_gate")], axis=1)
    out["L3_attn_gain"] = np.concatenate([g("g_qnorm"), g("g_kvnorm")])
    parts = lambda w: w.reshape(w.shape[0], 16, 3, 32).transpose(0, 2, 1, 3).reshape(w.shape[0], -1)
    out["L3_attn_sel"] = np.concatenate([parts(g("w_selk")), g("w_selv")], axis=1)
    out["L3_attn_win"] = np.concatenate([parts(g("w_wink")), g("w_winv")], axis=1)
    halves = g("w_dq_rope").reshape(96, 16, 2, 32).transpose(0, 2, 1, 3).reshape(96, -1)
    lat = np.zeros((P, 5 * 512), np.float32)
    lat[:96, :1536] = np.concatenate([g("w_dq_nope"), halves], axis=1)
    lat[96:, 1536:] = np.concatenate([g("w_dk_nope"), g("w_dv")], axis=1)
    out["L3_attn_lat"] = lat
    out["L3_attn_w_proj"] = g("w_proj")
    return {k: np.ascontiguousarray(v) for k, v in out.items()}


def kernel(**inputs):
    import concourse.bacc as bacc
    from concourse.bass_utils import run_bass_kernel_spmd

    nc = bacc.Bacc("TRN2", target_bir_lowering=False, num_devices=1)
    arrays, aps = {}, ({}, {})
    for which, group in enumerate((layout(inputs), constants())):
        for name, a in group.items():
            full = f"in_{name}_dram"
            arrays[full] = a
            aps[which][name] = nc.dram_tensor(full, a.shape, mybir.dt.from_np(a.dtype), kind="ExternalInput").ap()
    out = nc.dram_tensor("out_0_dram", (T, D), F32, kind="ExternalOutput").ap()
    build(nc, aps[0], aps[1], out)
    r = run_bass_kernel_spmd(nc, [arrays], core_ids=[0])
    return r.results[0]["out_0_dram"].reshape(BATCH, SEQ, D)
```

```python
from contextlib import ExitStack, contextmanager

import numpy as np

import concourse.bass as bass
from concourse import mybir

F32 = mybir.dt.float32
F32R = mybir.dt.float32r
ALU = mybir.AluOpType
ACT = mybir.ActivationFunctionType
AX = mybir.AxisListType

P = 128
BATCH, SEQ, D = 8, 64, 256
CTX = 1024
T = BATCH * SEQ
TT = T // P
KD = D // P
BANK = 512
LN_EPS = 1e-5

ONLY = list(range(12))


class Env:
    pass


@contextmanager
def layer_stage(nc, env, mem, *names):
    with stage(nc, *names, *Norm.NAMES) as (block, *sems):
        env.norm = Norm(nc, env, mem, sems[len(names):])
        yield (block, *sems[:len(names)])


@contextmanager
def stage(nc, *names):
    first = nc.stage_sem_base
    sems = [nc.alloc_semaphore(n, num=first + i) for i, n in enumerate(names)]
    with nc.Block() as block:
        yield (block, *sems)
    nc.all_engine_barrier(sems_to_clear=range(first, first + len(sems)))
    for s in sems:
        nc.release_semaphore(s)


def wait(eng, sem, value):
    if not isinstance(value, int) or value > 0:
        eng.wait_ge(sem, value)


class Chain:

    def __init__(self, eng, sem):
        self.eng, self.sem, self.base, self.n = eng, sem, 0, 0

    def restart(self, base):
        self.base, self.n = base, 0

    def __call__(self, ins):
        ins.then_inc(self.sem, 1)
        self.n += 1
        self.eng.wait_ge(self.sem, self.base + self.n)


def project(nc, out, weight, chunks, moving, **kw):
    for k in range(chunks):
        last = nc.tensor.matmul(out, weight(k), moving(k), start=(k == 0), stop=(k == chunks - 1), **kw)
    return last


def split_product(nc, out, stationary, moving, first=True, last=True):
    (sh, sl), (mh, ml) = stationary, moving
    nc.tensor.matmul(out, sh, mh, start=first, stop=False)
    nc.tensor.matmul(out, sh, ml, start=False, stop=False)
    return nc.tensor.matmul(out, sl, mh, start=False, stop=last)


def project_split(nc, out, weight, chunks, moving):
    for k in range(chunks):
        last = split_product(nc, out, weight(k), moving(k), k == 0, k == chunks - 1)
    return last


class Norm:

    NAMES = ("ln_pe_in", "ln_stats_done", "ln_moments_done", "ln_var_ready", "ln_rstd_ready", "ln_normed",
             "ln_h_ready", "ln_transposed", "ln_hT_ready")

    def __init__(self, nc, env, mem, sems):
        self.nc, self.env = nc, env
        (self.pe_in, self.stats_done, self.moments_done, self.var_ready, self.rstd_ready, self.normed, self.h_ready,
         self.transposed, self.hT_ready) = sems
        sb = lambda name, shape: mem.enter_context(nc.sbuf_tensor(name, shape, F32, allow_name_mangling=True))
        self.stats, self.mv, self.rstd = sb("ln_stats", [P, TT, 6]), sb("ln_mv", [P, TT, 2]), sb("ln_rstd", [P, TT])
        self.pos = None if env.positions is None else sb("ln_pos", [P, D])

    def sync(self, sp):
        if self.pos is not None:
            for i in range(2):
                sp.dma_start(self.pos[i * SEQ:(i + 1) * SEQ, :], self.env.positions).then_inc(self.pe_in, 16)

    def vector(self, dve):
        nc, env, stats, mv = self.nc, self.env, self.stats, self.mv
        for t in range(TT):
            nc.vector.bn_stats(stats[:, t, :], env.x[:, t, :]).then_inc(self.stats_done, 1)
        for t in range(TT):
            dve.wait_ge(self.stats_done, t + 1)
            nc.vector.bn_aggr(mv[:, t, :], stats[:, t, :]).then_inc(self.moments_done, 1)
        dve.wait_ge(self.moments_done, TT)
        nc.vector.tensor_scalar(mv[:, :, 1], mv[:, :, 1], LN_EPS, None, ALU.add).then_inc(self.var_ready, 1)
        dve.wait_ge(self.rstd_ready, 1)
        for t in range(TT):
            nc.vector.tensor_scalar(env.h[:, t, :], env.x[:, t, :], mv[:, t, 0:1], self.rstd[:, t:t + 1],
                                    ALU.subtract, ALU.mult).then_inc(self.h_ready if self.pos is None else self.normed, 1)
            if self.pos is not None:
                dve.wait_ge(self.pe_in, 32)
                dve.wait_ge(self.normed, t + 1)
                nc.vector.tensor_tensor(env.h[:, t, :], env.h[:, t, :], self.pos[:], ALU.add).then_inc(self.h_ready, 1)
        dve.wait_ge(self.transposed, 2)
        nc.vector.tensor_copy(env.hT[:, 1, :], env.ps[:, 1, :]).then_inc(self.hT_ready, 1)
        dve.wait_ge(self.hT_ready, 2)

    def gpsimd(self, pool):
        pool.wait_ge(self.var_ready, 1)
        self.nc.gpsimd.tensor_tensor(self.rstd[:], self.mv[:, :, 1], self.env.half_less[:].broadcast_to([P, TT]), ALU.pow)\
            .then_inc(self.rstd_ready, 1)

    def scalar(self, act):
        act.wait_ge(self.transposed, 1)
        self.nc.scalar.copy(self.env.hT[:, 0, :], self.env.ps[:, 0, :]).then_inc(self.hT_ready, 1)
        act.wait_ge(self.hT_ready, 2)

    def tensor(self, pe):
        nc, env = self.nc, self.env
        for t in range(TT):
            pe.wait_ge(self.h_ready, t + 1)
            for k in range(KD):
                turned = nc.tensor.transpose(env.ps[:, k, t * P:(t + 1) * P], env.h[:, t, k * P:(k + 1) * P],
                                             env.ident[:])
                if t == TT - 1:
                    turned.then_inc(self.transposed, 1)
        pe.wait_ge(self.hT_ready, 2)


HEADS, HD = 16, 16
HG = 8
GROUPS = HEADS // HG
CC = CTX // P


def sigmoid_cross_attention(nc, env, w, ctxT):
    UNITS = 8
    STEPS = CC * GROUPS
    LAG = 2
    RING = 4
    with ExitStack() as mem, layer_stage(
            nc, env, mem, "weights_in", "ctx_in", "q_done", "q_ready", "unit_done", "k_taken", "v_taken", "qbd_ready",
            "scores_done", "probs_ready", "pv_done", "masked", "o_ready", "out_done", "x_added",
            "w_high", "w_split", "ctx_high", "ctx_split", "k_high", "q_low") as (
            block, weights_in, ctx_in, q_done, q_ready, unit_done, k_taken, v_taken, qbd_ready,
            scores_done, probs_ready, pv_done, masked, o_ready, out_done, x_added,
            w_high, w_split, ctx_high, ctx_split, k_high, q_low):
        sb = lambda name, shape: mem.enter_context(nc.sbuf_tensor(name, shape, F32, allow_name_mangling=True))
        wq, wk, wv, wo = (sb(n, [P, KD, D]) for n in ("wq", "wk", "wv", "wo"))
        cT = sb("ctxT", [P, KD, CTX])
        high = lambda name, shape: mem.enter_context(nc.sbuf_tensor(name, shape, F32R, allow_name_mangling=True))
        wkh, wvh, cTh = high("wk_high", [P, KD, D]), high("wv_high", [P, KD, D]), high("ctxT_high", [P, 2, KD, CTX])
        wkl, wvl, cTl = high("wk_low", [P, KD, D]), high("wv_low", [P, KD, D]), high("ctxT_low", [P, 2, KD, CTX])
        kTh, kTl = high("kT_high", [P, 2, GROUPS, CTX]), high("kT_low", [P, 2, GROUPS, CTX])
        qTh, qTl = high("qT_high", [P, GROUPS, T]), high("qT_low", [P, GROUPS, T])
        v = sb("v", [P, 2, CC, D])
        qbdh, qbdl = high("qbd_high", [P, 2, GROUPS, HG, SEQ]), high("qbd_low", [P, 2, GROUPS, HG, SEQ])
        probs = sb("probs", [P, RING, BANK])
        prod = sb("prod", [P, GROUPS, 2, SEQ])
        oT = sb("oT", [P, GROUPS, T])
        ps = env.ps
        O_BANK = 6

        def pairs(body, lead):
            body(0, False)
            with body.eng.Fori(1, BATCH // 2 - 1) as j:
                body(j, False)
            body(BATCH // 2 - 1, True)

        @block.sync
        def _(sp):
            env.norm.sync(sp)
            for dst, src in ((wq, w["WqT"]), (wk, w["WkT"]), (wv, w["WvT"]), (wo, w["WoT"])):
                sp.dma_start(dst[:], src.rearrange("(k p) n -> p k n", p=P)).then_inc(weights_in, 16)
            for b in range(BATCH):
                wait(sp, ctx_split, b)
                sp.dma_start(cT[:], ctxT[b].rearrange("(k p) s -> p k s", p=P)).then_inc(ctx_in, 16)

        @block.tensor
        def _(pe):
            env.norm.tensor(pe)
            def proj(b, i):
                wait(pe, ctx_split, b + 1)
                for u in range(UNITS):
                    if 2 <= u < 6:
                        wait(pe, k_taken, 4 * b + u - 1)
                    else:
                        wait(pe, v_taken, 4 * b + (u - 5 if u >= 6 else u - 1))
                    bank = u % 2
                    if u < 4:
                        g, half = u // 2, u % 2
                        weights, keys = slice(g * P, (g + 1) * P), slice(half * BANK, (half + 1) * BANK)
                        last = project_split(nc, ps[:, bank, :], lambda k: (wkh[:, k, weights], wkl[:, k, weights]),
                                             KD, lambda k: (cTh[:, i, k, keys], cTl[:, i, k, keys]))
                    else:
                        for cc in range(2):
                            c = 2 * (u - 4) + cc
                            keys = slice(c * P, (c + 1) * P)
                            last = project_split(nc, ps[:, bank, cc * D:(cc + 1) * D],
                                                 lambda k: (cTh[:, i, k, keys], cTl[:, i, k, keys]), KD,
                                                 lambda k: (wvh[:, k, :], wvl[:, k, :]))
                    last.then_inc(unit_done, 1)

            def attend(b, i):
                pe.wait_ge(qbd_ready, 2 * GROUPS * (b + 1))
                wait(pe, k_taken, 4 * (b + 1))
                wait(pe, v_taken, 4 * (b + 1))
                for m in range(STEPS + LAG):
                    if m < STEPS:
                        c, g = m // GROUPS, m % GROUPS
                        wait(pe, probs_ready, STEPS * b + m - RING + 1)
                        keys = slice(c * P, (c + 1) * P)
                        split_product(nc, ps[:, 2 + m % RING, :], (kTh[:, i, g, keys], kTl[:, i, g, keys]),
                                      tuple(q[:, i, g].rearrange("p h l -> p (h l)") for q in (qbdh, qbdl)))\
                            .then_inc(scores_done, 1)
                    if m >= LAG:
                        n = m - LAG
                        c, g = n // GROUPS, n % GROUPS
                        pe.wait_ge(probs_ready, STEPS * b + n + 1)
                        if c == 0 and g == 0:
                            wait(pe, masked, GROUPS * b)
                        for j in range(4):
                            first = g * P + 2 * HD * j
                            last = nc.tensor.matmul(ps[32 * j:32 * j + 32, O_BANK + g, 0:P],
                                                    v[:, i, c, first:first + 2 * HD],
                                                    probs[:, n % RING, j * P:(j + 1) * P],
                                                    start=(c == 0), stop=(c == CC - 1))
                        last.then_inc(pv_done, 1)

            pe.wait_ge(weights_in, 64)
            for g in range(GROUPS):
                project(nc, ps[:, 2 + g, :], lambda k: wq[:, k, g * P:(g + 1) * P], KD,
                        lambda k: env.hT[:, k, :]).then_inc(q_done, 1)
            pe.wait_ge(w_split, 2)
            proj(0, 0)
            pe.wait_ge(q_low, GROUPS)

            def pair(j, last):
                proj(2 * j + 1, 1)
                attend(2 * j, 0)
                if not last:
                    proj(2 * j + 2, 0)
                attend(2 * j + 1, 1)

            pair(0, False)
            with pe.Fori(1, BATCH // 2 - 1) as j:
                pair(j, False)
            pair(BATCH // 2 - 1, True)

            for t in range(TT):
                if t == 0:
                    pe.wait_ge(o_ready, GROUPS * BATCH)
                project(nc, ps[:, t, 0:D], lambda k: oT[:, k, t * P:(t + 1) * P], KD,
                        lambda k: wo[:, k, :]).then_inc(out_done, 1)

        @block.scalar
        def _(act):
            env.norm.scalar(act)
            def split_ctx(b, i):
                act.wait_ge(ctx_in, 16 * (b + 1))
                wait(act, unit_done, UNITS * (b - 1))
                nc.scalar.copy(cTh[:, i], cT[:]).then_inc(ctx_high, 1)

            split_ctx(0, 0)
            act.wait_ge(weights_in, 64)
            nc.scalar.copy(wkh[:], wk[:]).then_inc(w_high, 1)
            nc.scalar.copy(wvh[:], wv[:]).then_inc(w_high, 1)
            for g in range(GROUPS):
                act.wait_ge(q_done, g + 1)
                nc.scalar.mul(qTh[:, g, :], ps[:, 2 + g, :], HD ** -0.5).then_inc(q_ready, 1)
            split_ctx(1, 1)

            def sample(b, i, last):
                for m in range(STEPS):
                    act.wait_ge(scores_done, STEPS * b + m + 1)
                    wait(act, pv_done, STEPS * b + m - RING + 1)
                    nc.scalar.activation(probs[:, m % RING, :], ps[:, 2 + m % RING, :],
                                         ACT.Sigmoid).then_inc(probs_ready, 1)
                    if m == STEPS // 2 and not last:
                        split_ctx(b + 2, i)

            def take(b, i):
                for u in range(UNITS):
                    act.wait_ge(unit_done, UNITS * b + u + 1)
                    if u < 4:
                        nc.scalar.copy(kTh[:, i, u // 2, (u % 2) * BANK:(u % 2 + 1) * BANK], ps[:, u % 2, :])\
                            .then_inc(k_high, 1)
                    else:
                        nc.scalar.copy(v[:, i, 2 * (u - 4):2 * (u - 4) + 2, :].rearrange("p c n -> p (c n)"),
                                       ps[:, u % 2, :]).then_inc(v_taken, 1)

            def pair(j, last):
                take(2 * j + 1, 1)
                sample(2 * j, 0, last)
                if not last:
                    take(2 * j + 2, 0)
                sample(2 * j + 1, 1, last)

            take(0, 0)
            pair(0, False)
            with act.Fori(1, BATCH // 2 - 1) as j:
                pair(j, False)
            pair(BATCH // 2 - 1, True)

        @block.gpsimd
        def _(pool):
            env.norm.gpsimd(pool)

            def split_ctx(b, i):
                pool.wait_ge(ctx_high, b + 1)
                nc.gpsimd.tensor_tensor(cTl[:, i], cT[:], cTh[:, i], ALU.subtract).then_inc(ctx_split, 1)

            split_ctx(0, 0)
            split_ctx(1, 1)
            with pool.Fori(1, BATCH // 2) as j:
                split_ctx(2 * j, 0)
                split_ctx(2 * j + 1, 1)

        @block.vector
        def _(dve):
            env.norm.vector(dve)
            def take(b, i):
                for u in range(4):
                    keys = slice((u % 2) * BANK, (u % 2 + 1) * BANK)
                    dve.wait_ge(k_high, 4 * b + u + 1)
                    nc.vector.tensor_tensor(kTl[:, i, u // 2, keys], ps[:, u % 2, :], kTh[:, i, u // 2, keys],
                                            ALU.subtract).then_inc(k_taken, 1)
                for q, qbd in ((qTh, qbdh), (qTl, qbdl)):
                    for g in range(GROUPS):
                        nc.vector.tensor_tensor(
                            qbd[:, i, g], q[:, g, bass.ds(b * SEQ, SEQ)].unsqueeze(1).broadcast_to([P, HG, SEQ]),
                            env.head_mask[:].unsqueeze(2).broadcast_to([P, HG, SEQ]), ALU.mult).then_inc(qbd_ready, 1)

            def extract(b):
                dve.wait_ge(pv_done, STEPS * (b + 1))
                for g in range(GROUPS):
                    wait(dve, o_ready, GROUPS * b)
                    nc.vector.tensor_tensor(prod[:, g], ps[:, O_BANK + g, 0:P].rearrange("p (h l) -> p h l", h=2),
                                            env.pair_mask[:].unsqueeze(2).broadcast_to([P, 2, SEQ]),
                                            ALU.mult).then_inc(masked, 1)
                for g in range(GROUPS):
                    dve.wait_ge(masked, GROUPS * b + g + 1)
                    nc.vector.tensor_tensor(oT[:, g, bass.ds(b * SEQ, SEQ)], prod[:, g, 0, :], prod[:, g, 1, :],
                                            ALU.add).then_inc(o_ready, 1)

            def pair(j, last):
                take(2 * j + 1, 1)
                extract(2 * j)
                if not last:
                    take(2 * j + 2, 0)
                extract(2 * j + 1)

            for i, (w, wh, wl) in enumerate(((wk, wkh, wkl), (wv, wvh, wvl))):
                dve.wait_ge(w_high, i + 1)
                nc.vector.tensor_tensor(wl[:], w[:], wh[:], ALU.subtract).then_inc(w_split, 1)
            for g in range(GROUPS):
                dve.wait_ge(q_ready, g + 1)
                nc.vector.scalar_tensor_tensor(out=qTl[:, g, :], in0=ps[:, 2 + g, :], scalar=HD ** -0.5,
                                               in1=qTh[:, g, :], op0=ALU.mult, op1=ALU.subtract).then_inc(q_low, 1)
            dve.wait_ge(q_low, GROUPS)
            take(0, 0)
            pair(0, False)
            with dve.Fori(1, BATCH // 2 - 1) as j:
                pair(j, False)
            pair(BATCH // 2 - 1, True)
            for t in range(TT):
                dve.wait_ge(out_done, t + 1)
                nc.vector.tensor_tensor(env.x[:, t, :], env.x[:, t, :], ps[:, t, 0:D],
                                        ALU.add).then_inc(x_added, 1)


def project_out(nc, env, pe, oT, wo, chunks, out_done, bias=None):
    for t in range(TT):
        if bias is not None:
            nc.tensor.matmul(env.ps[:, t, 0:D], env.ones[0:1, 0:P], bias, start=True, stop=False)
        for k in range(chunks):
            last = nc.tensor.matmul(env.ps[:, t, 0:D], oT[:, k, t * P:(t + 1) * P], wo[:, k, :],
                                    start=(k == 0 and bias is None), stop=(k == chunks - 1))
        last.then_inc(out_done, 1)


def add_out(nc, env, dve, out_done, x_added):
    for t in range(TT):
        dve.wait_ge(out_done, t + 1)
        nc.vector.tensor_tensor(env.x[:, t, :], env.x[:, t, :], env.ps[:, t, 0:D], ALU.add).then_inc(x_added, 1)


def allocator(nc, mem):
    return lambda name, shape: mem.enter_context(nc.sbuf_tensor(name, shape, F32, allow_name_mangling=True))


def rows_of(ap, n=P):
    return ap.partition_broadcast(n)


def normalize_rows(nc, env, link, src, dst, stats, mv, std, moments_done, std_done, dve,
                   gamma=None, beta=None):
    for t in range(TT):
        link(nc.vector.bn_stats(stats[:, t, :], src[:, t, :]))
    for t in range(TT):
        nc.vector.bn_aggr(mv[:, t, :], stats[:, t, :]).then_inc(moments_done, 1)
    dve.wait_ge(std_done, 1)
    link(nc.vector.reciprocal(std[:], std[:]))
    for t in range(TT):
        link(nc.vector.tensor_scalar(dst[:, t, :], src[:, t, :], mv[:, t, 0:1], std[:, t:t + 1],
                                     ALU.subtract, ALU.mult))
        if gamma is not None:
            link(nc.vector.tensor_tensor(dst[:, t, :], dst[:, t, :], gamma, ALU.mult))
            link(nc.vector.tensor_tensor(dst[:, t, :], dst[:, t, :], beta, ALU.add))


def moe_top2(nc, env, ins):
    E, HID = 8, 1024
    HC = HID // P
    PAD = 6
    with ExitStack() as mem, layer_stage(
            nc, env, mem, "consts_in", "norm_in", "w1_in0", "w1_in1", "w2_in0", "w2_in1", "gate_done", "exp_done", "vstep", "combine_ready",
            "shared_done", "shared_gelu", "up_done", "gelu_done", "down_done", "down_taken", "moments_done",
            "std_done", "astep") as (
            block, consts_in, norm_in, w1_in0, w1_in1, w2_in0, w2_in1, gate_done, exp_done, vstep, combine_ready,
            shared_done, shared_gelu, up_done, gelu_done, down_done, down_taken, moments_done, std_done, astep):
        sb = allocator(nc, mem)
        ps = env.ps
        w1 = sb("w1", [P, 2, KD, HID])
        w2 = sb("w2", [P, 2, HC, D])
        b1, b2 = sb("b1", [P, E, HC]), sb("b2", [1, E, D])
        hid = sb("hid", [P, 2, HC, T])
        gw, ws, bs = sb("gate_w", [P, KD, E]), sb("shared_w", [P, KD, D]), sb("shared_b", [1, D])
        gamma, beta = sb("gamma", [P, D]), sb("beta", [P, D])
        acc = sb("acc", [P, TT, D])
        probs = sb("probs", [P, TT, E + PAD])
        top, rest = sb("top", [P, TT, 8]), sb("rest", [P, TT, E + PAD])
        neg_max, total, combine = sb("neg_max", [P, TT]), sb("total", [P, TT]), sb("combine", [P, TT, E])
        stats, mv, std = sb("stats", [P, TT, 6]), sb("mv", [P, TT, 2]), sb("std", [P, TT])
        w1_in, w2_in = (w1_in0, w1_in1), (w2_in0, w2_in1)

        @block.sync
        def _(sp):
            env.norm.sync(sp)
            sp.dma_start(gw[:], ins["L0_ffn_gate_W"].rearrange("(k p) e -> p k e", p=P)).then_inc(consts_in, 16)
            sp.dma_start(ws[:], ins["L0_ffn_shared_W"].rearrange("(k p) n -> p k n", p=P)).then_inc(consts_in, 16)
            sp.dma_start(bs[:], ins["L0_ffn_shared_b"].unsqueeze(0)).then_inc(consts_in, 16)
            sp.dma_start(b1[:], ins["L0_ffn_b1"]).then_inc(consts_in, 16)
            sp.dma_start(b2[:], ins["L0_ffn_b2"].unsqueeze(0)).then_inc(consts_in, 16)
            for e in range(E):
                wait(sp, up_done, HC * (e - 1))
                sp.dma_start(w1[:, e % 2], ins["L0_ffn_W1"][e].rearrange("(k p) n -> p k n", p=P))\
                    .then_inc(w1_in[e % 2], 16)
                wait(sp, down_done, TT * (e - 1))
                sp.dma_start(w2[:, e % 2], ins["L0_ffn_W2"][e].rearrange("(k p) n -> p k n", p=P))\
                    .then_inc(w2_in[e % 2], 16)
                if e == 1:
                    sp.dma_start(gamma[:], rows_of(ins["L0_ffn_gamma"])).then_inc(norm_in, 16)
                    sp.dma_start(beta[:], rows_of(ins["L0_ffn_beta"])).then_inc(norm_in, 16)

        @block.tensor
        def _(pe):
            env.norm.tensor(pe)
            pe.wait_ge(consts_in, 80)
            for t in range(TT):
                last = project(nc, ps[:, 4, t * E:(t + 1) * E], lambda k: env.hT[:, k, t * P:(t + 1) * P], KD,
                               lambda k: gw[:, k, :])
            last.then_inc(gate_done, 1)
            for t in range(TT):
                nc.tensor.matmul(ps[:, t, 0:D], env.ones[0:1, 0:P], bs[:], start=True, stop=False)
                for k in range(KD):
                    last = nc.tensor.matmul(ps[:, t, 0:D], env.hT[:, k, t * P:(t + 1) * P], ws[:, k, :],
                                            start=False, stop=(k == KD - 1))
                last.then_inc(shared_done, 1)
            pe.wait_ge(shared_gelu, TT)

            def up(e, i):
                pe.wait_ge(w1_in[i], 8 * e + 16 - 8 * i)
                for u in range(HC):
                    wait(pe, gelu_done, HC * e + u - 3)
                    project(nc, ps[:, u % 4, :], lambda k: w1[:, i, k, u * P:(u + 1) * P], KD,
                            lambda k: env.hT[:, k, :]).then_inc(up_done, 1)

            def down(e, i):
                pe.wait_ge(w2_in[i], 8 * e + 16 - 8 * i)
                wait(pe, gelu_done, HC * (e + 1))
                for t in range(TT):
                    wait(pe, down_taken, TT * e + t - 3)
                    for k in range(HC):
                        nc.tensor.matmul(ps[:, 4 + t, 0:D], hid[:, i, k, t * P:(t + 1) * P], w2[:, i, k, :],
                                         start=(k == 0), stop=False)
                    last = nc.tensor.matmul(ps[:, 4 + t, 0:D], env.ones[0:1, 0:P], b2[0:1, bass.ds(e, 1), :].rearrange(
                        "p e n -> p (e n)"), start=False, stop=True)
                    last.then_inc(down_done, 1)

            def pair(j, last):
                up(2 * j + 1, 1)
                down(2 * j, 0)
                if not last:
                    up(2 * j + 2, 0)
                down(2 * j + 1, 1)

            up(0, 0)
            pe.wait_ge(combine_ready, 1)
            pair(0, False)
            with pe.Fori(1, E // 2 - 1) as j:
                pair(j, False)
            pair(E // 2 - 1, True)

        @block.scalar
        def _(act):
            env.norm.scalar(act)
            act.wait_ge(vstep, 1)
            for t in range(TT):
                nc.scalar.activation(probs[:, t, 0:E], ps[:, 4, t * E:(t + 1) * E], ACT.Exp,
                                     bias=neg_max[:, t:t + 1]).then_inc(exp_done, 1)
            for t in range(TT):
                act.wait_ge(shared_done, t + 1)
                nc.scalar.activation(acc[:, t, :], ps[:, t, 0:D], ACT.Gelu).then_inc(shared_gelu, 1)

            def gelus(e, i):
                for u in range(HC):
                    act.wait_ge(up_done, HC * e + u + 1)
                    nc.scalar.activation(hid[:, i, u, :], ps[:, u % 4, :], ACT.Gelu,
                                         bias=b1[:, bass.ds(e, 1), u:u + 1].rearrange("p e u -> p (e u)"))\
                        .then_inc(gelu_done, 1)

            gelus(0, 0)
            with act.Fori(0, E // 2 - 1) as j:
                gelus(2 * j + 1, 1)
                gelus(2 * j + 2, 0)
            gelus(E - 1, 1)
            act.wait_ge(moments_done, TT)
            nc.scalar.activation(std[:], mv[:, :, 1], ACT.Sqrt, bias=env.eps[:, 0:1]).then_inc(std_done, 1)

        @block.gpsimd
        def _(pool):
            env.norm.gpsimd(pool)

        @block.vector
        def _(dve):
            env.norm.vector(dve)
            link = Chain(dve, vstep)
            dve.wait_ge(gate_done, 1)
            link(nc.vector.tensor_reduce(neg_max[:], ps[:, 4, 0:TT * E].rearrange("p (t e) -> p t e", t=TT),
                                         AX.X, ALU.max, negate=True))
            link(nc.vector.memset(probs[:, :, E:], -1.0))
            dve.wait_ge(exp_done, TT)
            for t in range(TT):
                link(nc.vector.max(top[:, t, :], probs[:, t, :]))
            link(nc.vector.memset(top[:, :, 2:8], -1.0))
            for t in range(TT):
                link(nc.vector.match_replace(rest[:, t, :], top[:, t, :], probs[:, t, :], -2.0))
            link(nc.vector.tensor_tensor(total[:], top[:, :, 0], top[:, :, 1], ALU.add))
            link(nc.vector.reciprocal(total[:], total[:]))
            link(nc.vector.tensor_scalar(rest[:, :, 0:E], rest[:, :, 0:E], -1.5, None, ALU.is_lt))
            link(nc.vector.tensor_tensor(combine[:], rest[:, :, 0:E], probs[:, :, 0:E], ALU.mult))
            link(nc.vector.tensor_tensor(combine[:], combine[:], total[:].unsqueeze(2).broadcast_to([P, TT, E]),
                                         ALU.mult))
            dve.wait_ge(shared_gelu, TT)
            link(nc.vector.tensor_scalar(acc[:], acc[:], 0.5, None, ALU.mult))
            nc.vector.engine_nop().then_inc(combine_ready, 1)

            def take(e):
                for t in range(TT):
                    dve.wait_ge(down_done, TT * e + t + 1)
                    wait(dve, down_taken, TT * e + t - 3)
                    nc.vector.scalar_tensor_tensor(out=acc[:, t, :], in0=ps[:, 4 + t, 0:D],
                                                   scalar=combine[:, t, bass.ds(e, 1)], in1=acc[:, t, :],
                                                   op0=ALU.mult, op1=ALU.add).then_inc(down_taken, 1)

            take(0)
            with dve.Fori(1, E) as e:
                take(e)
            dve.wait_ge(down_taken, TT * E)
            dve.wait_ge(norm_in, 32)
            normalize_rows(nc, env, link, acc, acc, stats, mv, std, moments_done, std_done, dve,
                           gamma[:], beta[:])
            link(nc.vector.tensor_tensor(env.x[:], env.x[:], acc[:], ALU.add))


def grouped_moe(nc, env, ins):
    E, GR, HID = 32, 4, 128
    ALL = E + 2
    EG = E // GR
    PAD = 6
    NONE = -1e30
    with ExitStack() as mem, layer_stage(
            nc, env, mem, "consts_in", "up_in0", "up_in1", "down_in0", "down_in1", "gate_done", "scores_ready", "vstep", "combine_ready",
            "up_done", "silu_done", "hid_ready", "down_done", "down_taken", "weights_used") as (
            block, consts_in, up_in0, up_in1, down_in0, down_in1, gate_done, scores_ready, vstep, combine_ready,
            up_done, silu_done, hid_ready, down_done, down_taken, weights_used):
        sb = allocator(nc, mem)
        ps = env.ps
        wgu, wd = sb("wgu", [P, 2, KD, 2, HID]), sb("wd", [P, 2, D])
        gw, bias = sb("gate_w", [P, KD, E]), sb("gate_bias", [P, E])
        silu, hid = sb("silu", [P, 2, T]), sb("hid", [P, 2, T])
        scores, choice, rest = sb("scores", [P, TT, E]), sb("choice", [P, TT, E]), sb("rest", [P, TT, E])
        top = sb("top", [P, TT, GR, 8])
        group, gtop, grest = sb("group", [P, TT, GR + PAD]), sb("gtop", [P, TT, 8]), sb("grest", [P, TT, GR + PAD])
        total, combine = sb("total", [P, TT]), sb("combine", [P, TT, ALL])
        up_in, down_in = (up_in0, up_in1), (down_in0, down_in1)

        @block.sync
        def _(sp):
            env.norm.sync(sp)
            sp.dma_start(gw[:], ins["L3_ffn_gate_wT"].rearrange("(k p) e -> p k e", p=P)).then_inc(consts_in, 16)
            sp.dma_start(bias[:], rows_of(ins["L3_ffn_gate_bias"])).then_inc(consts_in, 16)

            def load(e, i):
                wait(sp, up_done, 2 * (e - 1))
                sp.dma_start(wgu[:, i].rearrange("p k s n -> p (k s n)"),
                             ins["L3_ffn_gate_up"][bass.ds(e, 1)].rearrange("e p n -> p (e n)")).then_inc(up_in[i], 16)
                wait(sp, down_done, TT * (e - 1))
                sp.dma_start(wd[:, i], ins["L3_ffn_downT"][bass.ds(e, 1)].rearrange("e p n -> p (e n)"))\
                    .then_inc(down_in[i], 16)

            load(0, 0)
            load(1, 1)
            with sp.Fori(1, ALL // 2) as j:
                load(2 * j, 0)
                load(2 * j + 1, 1)

        @block.tensor
        def _(pe):
            env.norm.tensor(pe)
            pe.wait_ge(consts_in, 32)
            for t in range(TT):
                last = project(nc, ps[:, 4, t * E:(t + 1) * E], lambda k: env.hT[:, k, t * P:(t + 1) * P], KD,
                               lambda k: gw[:, k, :])
            last.then_inc(gate_done, 1)

            def up(e, i):
                pe.wait_ge(up_in[i], 8 * e + 16 - 8 * i)
                wait(pe, hid_ready, e - 1)
                project(nc, ps[:, 2 * i, :], lambda k: wgu[:, i, k, 0, :], KD, lambda k: env.hT[:, k, :])\
                    .then_inc(up_done, 1)
                project(nc, ps[:, 2 * i + 1, :], lambda k: wgu[:, i, k, 1, :], KD, lambda k: env.hT[:, k, :])\
                    .then_inc(up_done, 1)

            def down(e, i):
                pe.wait_ge(down_in[i], 8 * e + 16 - 8 * i)
                wait(pe, hid_ready, e + 1)
                for t in range(TT):
                    wait(pe, down_taken, TT * e + t - 3)
                    nc.tensor.matmul(ps[:, 4 + t, 0:D], hid[:, i, t * P:(t + 1) * P], wd[:, i, :],
                                     start=True, stop=True).then_inc(down_done, 1)

            def pair(j, last):
                up(2 * j + 1, 1)
                down(2 * j, 0)
                if not last:
                    up(2 * j + 2, 0)
                down(2 * j + 1, 1)

            up(0, 0)
            pe.wait_ge(combine_ready, 1)
            pair(0, False)
            with pe.Fori(1, ALL // 2 - 1) as j:
                pair(j, False)
            pair(ALL // 2 - 1, True)

        @block.scalar
        def _(act):
            env.norm.scalar(act)
            act.wait_ge(gate_done, 1)
            nc.scalar.activation(scores[:], ps[:, 4, 0:TT * E].rearrange("p (t e) -> p t e", t=TT),
                                 ACT.Sigmoid).then_inc(scores_ready, 1)

            def silus(e, i):
                act.wait_ge(up_done, 2 * e + 1)
                wait(act, hid_ready, e - 1)
                nc.scalar.activation(silu[:, i, :], ps[:, 2 * i, :], ACT.Silu).then_inc(silu_done, 1)

            silus(0, 0)
            silus(1, 1)
            with act.Fori(1, ALL // 2) as j:
                silus(2 * j, 0)
                silus(2 * j + 1, 1)

        @block.gpsimd
        def _(pool):
            env.norm.gpsimd(pool)

        @block.vector
        def _(dve):
            env.norm.vector(dve)
            link = Chain(dve, vstep)

            def gating():
                dve.wait_ge(scores_ready, 1)
                dve.wait_ge(consts_in, 32)
                link(nc.vector.memset(group[:, :, GR:], NONE))
                link(nc.vector.tensor_tensor(choice[:], scores[:], bias[:].unsqueeze(1).broadcast_to([P, TT, E]),
                                             ALU.add))
                for t in range(TT):
                    for g in range(GR):
                        ins_ = nc.vector.max(top[:, t, g, :], choice[:, t, g * EG:(g + 1) * EG])
                        if t < TT - 1 or g < GR - 1:
                            ins_.then_inc(vstep, 1)
                            link.n += 1
                        else:
                            link(ins_)
                link(nc.vector.tensor_tensor(group[:, :, 0:GR], top[:, :, :, 0], top[:, :, :, 1], ALU.add))
                for t in range(TT):
                    link(nc.vector.max(gtop[:, t, :], group[:, t, :]))
                link(nc.vector.memset(gtop[:, :, 2:8], NONE))
                for t in range(TT):
                    link(nc.vector.match_replace(grest[:, t, :], gtop[:, t, :], group[:, t, :], 2 * NONE))
                link(nc.vector.tensor_scalar(grest[:, :, 0:GR], grest[:, :, 0:GR], 1.5 * NONE, None, ALU.is_lt))
                link(nc.vector.tensor_tensor(
                    choice[:].rearrange("p t (g e) -> p t g e", g=GR), choice[:].rearrange("p t (g e) -> p t g e", g=GR),
                    grest[:, :, 0:GR].unsqueeze(3).broadcast_to([P, TT, GR, EG]), ALU.mult))
                for t in range(TT):
                    link(nc.vector.max(gtop[:, t, :], choice[:, t, :]))
                    link(nc.vector.match_replace(rest[:, t, :], gtop[:, t, :], choice[:, t, :], NONE))
                link(nc.vector.tensor_scalar(rest[:], rest[:], 0.5 * NONE, None, ALU.is_lt))
                link(nc.vector.tensor_tensor(scores[:], scores[:], rest[:], ALU.mult))
                link(nc.vector.tensor_reduce(total[:], scores[:], AX.X, ALU.add))
                link(nc.vector.tensor_scalar(total[:], total[:], 1e-20, None, ALU.add))
                link(nc.vector.reciprocal(total[:], total[:]))
                link(nc.vector.tensor_tensor(combine[:, :, 0:E], scores[:],
                                             total[:].unsqueeze(2).broadcast_to([P, TT, E]), ALU.mult))
                link(nc.vector.tensor_scalar(combine[:, :, 0:E], combine[:, :, 0:E], 2.5, None, ALU.mult))
                nc.vector.memset(combine[:, :, E:ALL], 1.0).then_inc(combine_ready, 1)
                dve.wait_ge(combine_ready, 1)

            def hidden(e, i):
                dve.wait_ge(silu_done, e + 1)
                dve.wait_ge(up_done, 2 * e + 2)
                wait(dve, down_done, TT * e - TT)
                nc.vector.tensor_tensor(hid[:, i, :], ps[:, 2 * i + 1, :], silu[:, i, :], ALU.mult)\
                    .then_inc(hid_ready, 1)

            def take(e):
                for t in range(TT):
                    dve.wait_ge(down_done, TT * e + t + 1)
                    wait(dve, down_taken, TT * e + t - 3)
                    nc.vector.scalar_tensor_tensor(out=env.x[:, t, :], in0=ps[:, 4 + t, 0:D],
                                                   scalar=combine[:, t, bass.ds(e, 1)], in1=env.x[:, t, :],
                                                   op0=ALU.mult, op1=ALU.add).then_inc(down_taken, 1)

            def pair(j, last):
                hidden(2 * j + 1, 1)
                take(2 * j)
                if not last:
                    hidden(2 * j + 2, 0)
                take(2 * j + 1)

            gating()
            hidden(0, 0)
            pair(0, False)
            with dve.Fori(1, ALL // 2 - 1) as j:
                pair(j, False)
            pair(ALL // 2 - 1, True)


def ternary_mlp(nc, env, ins):
    HID = 1024
    HC = HID // P
    with ExitStack() as mem, layer_stage(
            nc, env, mem, "scales_in", "w12_in", "h1_in", "h2_in", "w3_in", "up_done", "silu_done", "a_ready", "h1_done",
            "b_ready", "h2_done", "c_ready", "out_done", "scaled", "x_added") as (
            block, scales_in, w12_in, h1_in, h2_in, w3_in, up_done, silu_done, a_ready, h1_done,
            b_ready, h2_done, c_ready, out_done, scaled, x_added):
        sb = allocator(nc, mem)
        ps = env.ps
        w1, w2 = sb("w1", [P, HC, KD, P]), sb("w2", [P, HC, KD, P])
        h1, h2 = sb("h1", [P, HC, HC, P]), sb("h2", [P, HC, HC, P])
        w3 = sb("w3", [P, HC, D])
        scales, s3 = sb("scales", [P, 4, HC]), sb("s3", [P, D])
        silu = sb("silu", [P, 2, T])
        a, b = sb("a", [P, HC, T]), sb("b", [P, HC, T])
        tmp = sb("tmp", [P, TT, D])

        @block.sync
        def _(sp):
            env.norm.sync(sp)
            sp.dma_start(scales[:], ins["L1_ffn_scales"]).then_inc(scales_in, 16)
            sp.dma_start(s3[:], rows_of(ins["L1_ffn_w3_s"])).then_inc(scales_in, 16)
            for o in range(HC):
                sp.dma_start(w1[:, o], ins["L1_ffn_w1"][o]).then_inc(w12_in, 16)
                sp.dma_start(w2[:, o], ins["L1_ffn_w2"][o]).then_inc(w12_in, 16)
            for o in range(HC):
                sp.dma_start(h1[:, o], ins["L1_ffn_h1"][o]).then_inc(h1_in, 16)
            for o in range(HC):
                sp.dma_start(h2[:, o], ins["L1_ffn_h2"][o]).then_inc(h2_in, 16)
            sp.dma_start(w3[:], ins["L1_ffn_w3T"].rearrange("(k p) n -> p k n", p=P)).then_inc(w3_in, 16)

        @block.tensor
        def _(pe):
            env.norm.tensor(pe)
            pe.wait_ge(w12_in, 32 * HC)
            for o in range(HC):
                wait(pe, a_ready, o - 1)
                for s, w in enumerate((w1, w2)):
                    project(nc, ps[:, 2 * (o % 2) + s, :], lambda k: w[:, o, k, :], KD, lambda k: env.hT[:, k, :])\
                        .then_inc(up_done, 1)
            for base, w, w_in, src, ready, done, taken in ((4, h1, h1_in, a, a_ready, h1_done, b_ready),
                                                           (0, h2, h2_in, b, b_ready, h2_done, c_ready)):
                pe.wait_ge(w_in, 16 * HC)
                pe.wait_ge(ready, HC)
                for o in range(HC):
                    wait(pe, taken, o - 3)
                    project(nc, ps[:, base + o % 4, :], lambda k: w[:, o, k, :], HC, lambda k: src[:, k, :])\
                        .then_inc(done, 1)
            pe.wait_ge(w3_in, 16)
            pe.wait_ge(c_ready, HC)
            project_out(nc, env, pe, a, w3, HC, out_done)

        @block.scalar
        def _(act):
            env.norm.scalar(act)
            act.wait_ge(scales_in, 32)
            for o in range(HC):
                act.wait_ge(up_done, 2 * o + 1)
                wait(act, a_ready, o - 1)
                nc.scalar.activation(silu[:, o % 2, :], ps[:, 2 * (o % 2), :], ACT.Silu,
                                     scale=scales[:, 0, o:o + 1]).then_inc(silu_done, 1)
            for base, s, dst, done, ready in ((4, 2, b, h1_done, b_ready), (0, 3, a, h2_done, c_ready)):
                for o in range(HC):
                    act.wait_ge(done, o + 1)
                    if s == 3 and o == 0:
                        act.wait_ge(h1_done, HC)
                    nc.scalar.activation(dst[:, o, :], ps[:, base + o % 4, :], ACT.Gelu,
                                         scale=scales[:, s, o:o + 1]).then_inc(ready, 1)

        @block.gpsimd
        def _(pool):
            env.norm.gpsimd(pool)

        @block.vector
        def _(dve):
            env.norm.vector(dve)
            dve.wait_ge(scales_in, 32)
            for o in range(HC):
                dve.wait_ge(silu_done, o + 1)
                dve.wait_ge(up_done, 2 * o + 2)
                nc.vector.scalar_tensor_tensor(out=a[:, o, :], in0=ps[:, 2 * (o % 2) + 1, :],
                                               scalar=scales[:, 1, o:o + 1], in1=silu[:, o % 2, :],
                                               op0=ALU.mult, op1=ALU.mult).then_inc(a_ready, 1)
            for t in range(TT):
                dve.wait_ge(out_done, t + 1)
                nc.vector.tensor_tensor(tmp[:, t, :], ps[:, t, 0:D], s3[:], ALU.mult).then_inc(scaled, 1)
                dve.wait_ge(scaled, t + 1)
                nc.vector.tensor_tensor(env.x[:, t, :], env.x[:, t, :], tmp[:, t, :], ALU.add).then_inc(x_added, 1)


def binary_mlp(nc, env, ins):
    HID = 1024
    HC = HID // P
    with ExitStack() as mem, layer_stage(
            nc, env, mem, "w1_in", "w2_in", "vstep", "signed1", "signed2", "bw1_ready", "bw2_ready", "turned1", "turned2",
            "w1T_ready", "w2T_ready", "up_done", "gelu_done", "out_done", "x_added", "vstep2") as (
            block, w1_in, w2_in, vstep, signed1, signed2, bw1_ready, bw2_ready, turned1, turned2,
            w1T_ready, w2T_ready, up_done, gelu_done, out_done, x_added, vstep2):
        sb = allocator(nc, mem)
        ps = env.ps
        w1, sg1 = sb("w1", [P, HC, D]), sb("sg1", [P, HC, D])
        w2, sg2 = sb("w2", [P, KD, HID]), sb("sg2", [P, KD, HID])
        w1T, w2T = sb("w1T", [P, KD, HID]), sb("w2T", [P, HC, D])
        b1, b2 = sb("b1", [P, HC]), sb("b2", [1, D])
        alpha1, alpha2 = sb("alpha1", [P, HC]), sb("alpha2", [P, KD])
        hid = sb("hid", [P, HC, T])

        @block.sync
        def _(sp):
            env.norm.sync(sp)
            sp.dma_start(w1[:], ins["L2_ffn_w1"].rearrange("(o p) n -> p o n", p=P)).then_inc(w1_in, 16)
            sp.dma_start(w2[:], ins["L2_ffn_w2"].rearrange("(o p) n -> p o n", p=P)).then_inc(w2_in, 16)
            sp.dma_start(b1[:], ins["L2_ffn_b1"]).then_inc(w2_in, 16)
            sp.dma_start(b2[:], ins["L2_ffn_b2"].unsqueeze(0)).then_inc(w2_in, 16)

        @block.scalar
        def _(act):
            env.norm.scalar(act)
            act.wait_ge(w1_in, 16)
            nc.scalar.activation(sg1[:], w1[:], ACT.Sign).then_inc(signed1, 1)
            act.wait_ge(w2_in, 48)
            nc.scalar.activation(sg2[:], w2[:], ACT.Sign).then_inc(signed2, 1)
            for n in range(4):
                act.wait_ge(turned1, n + 1)
                nc.scalar.copy(w1T[:, n // 2, (n % 2) * BANK:(n % 2 + 1) * BANK], ps[:, n, :]).then_inc(w1T_ready, 1)
            for o in range(HC):
                act.wait_ge(up_done, o + 1)
                nc.scalar.activation(hid[:, o, :], ps[:, o % 4, :], ACT.Gelu, bias=b1[:, o:o + 1])\
                    .then_inc(gelu_done, 1)

        @block.gpsimd
        def _(pool):
            env.norm.gpsimd(pool)

        @block.vector
        def _(dve):
            env.norm.vector(dve)
            link = Chain(dve, vstep)
            for w, sg, alpha, rows, cols, w_in, n_in, signed, ready in (
                    (w1, sg1, alpha1, HC, D, w1_in, 16, signed1, bw1_ready),
                    (w2, sg2, alpha2, KD, HID, w2_in, 48, signed2, bw2_ready)):
                dve.wait_ge(w_in, n_in)
                link(nc.vector.tensor_reduce(alpha[:], w[:], AX.X, ALU.add, apply_absolute_value=True))
                link(nc.vector.tensor_scalar(alpha[:], alpha[:], 1.0 / cols, None, ALU.mult))
                dve.wait_ge(signed, 1)
                for r in range(rows):
                    link(nc.vector.scalar_tensor_tensor(out=sg[:, r, :], in0=sg[:, r, :], scalar=alpha[:, r:r + 1],
                                                        in1=w[:, r, :], op0=ALU.mult, op1=ALU.subtract))
                    nc.vector.tensor_tensor(w[:, r, :], w[:, r, :], sg[:, r, :], ALU.add).then_inc(ready, 1)
            for n in range(4):
                dve.wait_ge(turned2, n + 1)
                nc.vector.tensor_copy(w2T[:, 2 * n:2 * n + 2, :].rearrange("p c n -> p (c n)"), ps[:, 4 + n, :])\
                    .then_inc(w2T_ready, 1)
            add_out(nc, env, dve, out_done, x_added)

        @block.tensor
        def _(pe):
            env.norm.tensor(pe)
            pe.wait_ge(bw1_ready, HC)
            for n in range(4):
                k, half = n // 2, n % 2
                for o in range(4):
                    last = nc.tensor.transpose(ps[:, n, o * P:(o + 1) * P], w1[:, 4 * half + o, k * P:(k + 1) * P],
                                               env.ident[:])
                last.then_inc(turned1, 1)
            pe.wait_ge(bw2_ready, KD)
            for n in range(4):
                for c in range(2):
                    for r in range(KD):
                        last = nc.tensor.transpose(ps[:, 4 + n, c * D + r * P:c * D + (r + 1) * P],
                                                   w2[:, r, (2 * n + c) * P:(2 * n + c + 1) * P], env.ident[:])
                last.then_inc(turned2, 1)
            pe.wait_ge(w1T_ready, 4)
            for o in range(HC):
                wait(pe, gelu_done, o - 3)
                project(nc, ps[:, o % 4, :], lambda k: w1T[:, k, o * P:(o + 1) * P], KD, lambda k: env.hT[:, k, :])\
                    .then_inc(up_done, 1)
            pe.wait_ge(w2T_ready, 4)
            pe.wait_ge(gelu_done, HC)
            project_out(nc, env, pe, hid, w2T, HC, out_done, b2[:])


def selective_scan(nc, env, ins):
    INNER, STATES, RANK = 512, 16, 16
    IC = INNER // P
    R = RANK + 2 * STATES
    PT = SEQ + 1
    with ExitStack() as mem, layer_stage(
            nc, env, mem, "consts_in", "w_in_in", "proj_done", "x_ready", "z_ready", "dbc_done", "dbc_ready", "dt_done",
            "astep", "dstep", "A_ready", "delta_ready", "dtx_ready", "row_ready", "spread_done", "B_ready", "dA_ready",
            "u_ready", "scanned", "prod_ready", "y_done", "y_ready", "out_done", "x_added", "pads_set") as (
            block, consts_in, w_in_in, proj_done, x_ready, z_ready, dbc_done, dbc_ready, dt_done,
            astep, dstep, A_ready, delta_ready, dtx_ready, row_ready, spread_done, B_ready, dA_ready,
            u_ready, scanned, prod_ready, y_done, y_ready, out_done, x_added, pads_set):
        sb = allocator(nc, mem)
        ps = env.ps
        w_in, b_in = sb("w_in", [P, KD, 2 * INNER]), sb("b_in", [P, 2 * IC])
        w_x, b_x = sb("w_x", [P, IC, R]), sb("b_x", [R, 1])
        w_dt, b_dt = sb("w_dt", [RANK, INNER]), sb("b_dt", [P, IC])
        A, Dskip = sb("A", [P, IC, STATES]), sb("Dskip", [P, IC])
        w_out, b_out = sb("w_out", [P, IC, D]), sb("b_out", [1, D])
        pick = sb("pick", [P, 2 * STATES])
        xT, zT = sb("xT", [P, IC, T]), sb("zT", [P, IC, T])
        dbc = sb("dbc", [P, T])
        mag, delta, dtx = sb("mag", [P, IC, T]), sb("delta", [P, IC, T]), sb("dtx", [P, IC, T])
        row = sb("row", [P, 2, 2, T])
        B_all = sb("B_all", [P, 2, T])
        dA, u = sb("dA", [P, 2, IC, BATCH, PT]), sb("u", [P, 2, IC, BATCH, PT])
        state = sb("state", [P, IC, BATCH, PT])
        prod = sb("prod", [P, 2, IC, T])
        by_sample = lambda ap: ap.rearrange("p (b t) -> p b t", b=BATCH)
        flat = lambda ap: ap.rearrange("p b t -> p (b t)")

        @block.sync
        def _(sp):
            env.norm.sync(sp)
            sp.dma_start(w_in[:], ins["L0_attn_W_inT"].rearrange("(k p) n -> p k n", p=P)).then_inc(w_in_in, 16)
            sp.dma_start(b_in[:], ins["L0_attn_b_in"]).then_inc(w_in_in, 16)
            for dst, src in ((w_x, ins["L0_attn_W_xT"].rearrange("(k p) n -> p k n", p=P)),
                             (b_x, ins["L0_attn_b_x"].unsqueeze(1)), (w_dt, ins["L0_attn_W_dtT"]),
                             (b_dt, ins["L0_attn_b_dt"]), (A, ins["L0_attn_A_log"].rearrange("(k p) n -> p k n", p=P)),
                             (Dskip, ins["L0_attn_D"]),
                             (w_out, ins["L0_attn_W_outT"].rearrange("(k p) n -> p k n", p=P)),
                             (b_out, ins["L0_attn_b_out"].unsqueeze(0)), (pick, env.consts["pick"])):
                sp.dma_start(dst[:], src).then_inc(consts_in, 16)

        @block.tensor
        def _(pe):
            env.norm.tensor(pe)
            pe.wait_ge(w_in_in, 32)
            for o in range(2 * IC):
                project(nc, ps[:, o, :], lambda k: w_in[:, k, o * P:(o + 1) * P], KD, lambda k: env.hT[:, k, :])\
                    .then_inc(proj_done, 1)
            pe.wait_ge(consts_in, 144)
            pe.wait_ge(x_ready, IC)
            project(nc, ps[0:R, 0, :], lambda k: w_x[:, k, :], IC, lambda k: xT[:, k, :]).then_inc(dbc_done, 1)
            pe.wait_ge(dbc_ready, 1)
            pe.wait_ge(z_ready, IC)
            for c in range(IC):
                nc.tensor.matmul(ps[:, 4 + c, :], w_dt[:, c * P:(c + 1) * P], dbc[0:RANK, :],
                                 start=True, stop=True).then_inc(dt_done, 1)

            def state_step(n, i, first=False, last=False):
                for s in range(2):
                    pe.wait_ge(row_ready, 2 * n + s + 1)
                    if s == 0:
                        wait(pe, B_ready, n - 1)
                    else:
                        wait(pe, prod_ready, IC * (n - 1))
                    nc.tensor.matmul(ps[:, 2 * s + i, :], env.ones[:, 0:P], row[:, i, s, :],
                                     start=True, stop=True).then_inc(spread_done, 1)

            def sum_step(n, i, first=False, last=False):
                for c in range(IC):
                    pe.wait_ge(prod_ready, IC * n + c + 1)
                    nc.tensor.matmul(ps[:, 4 + c, :], env.ident[:], prod[:, i, c, :], start=first, stop=last,
                                     skip_group_check=True).then_inc(y_done, 1)

            pe.wait_ge(delta_ready, IC)
            state_step(0, 0)
            state_step(1, 1)
            sum_step(0, 0, first=True)
            with pe.Fori(1, STATES // 2) as j:
                state_step(2 * j, 0)
                sum_step(2 * j - 1, 1)
                state_step(2 * j + 1, 1)
                sum_step(2 * j, 0)
            sum_step(STATES - 1, 1, last=True)
            pe.wait_ge(y_ready, IC)
            project_out(nc, env, pe, xT, w_out, IC, out_done, b_out[:])

        @block.scalar
        def _(act):
            env.norm.scalar(act)
            link = Chain(act, astep)
            act.wait_ge(w_in_in, 32)
            for c in range(IC):
                act.wait_ge(proj_done, c + 1)
                nc.scalar.activation(xT[:, c, :], ps[:, c, :], ACT.Identity, bias=b_in[:, c:c + 1]).then_inc(x_ready, 1)
            for c in range(IC):
                act.wait_ge(proj_done, IC + c + 1)
                nc.scalar.activation(zT[:, c, :], ps[:, IC + c, :], ACT.Silu,
                                     bias=b_in[:, IC + c:IC + c + 1]).then_inc(z_ready, 1)
            act.wait_ge(consts_in, 144)
            act.wait_ge(dbc_done, 1)
            act.wait_ge(pads_set, 4)
            nc.scalar.activation(dbc[0:R, :], ps[0:R, 0, :], ACT.Identity, bias=b_x[:]).then_inc(dbc_ready, 1)
            nc.scalar.activation(A[:], A[:], ACT.Exp).then_inc(A_ready, 1)
            for c in range(IC):
                act.wait_ge(dt_done, c + 1)
                nc.scalar.activation(delta[:, c, :], ps[:, 4 + c, :], ACT.Relu, bias=b_dt[:, c:c + 1])\
                    .then_inc(astep, 1)
                link.n += 1
                link(nc.scalar.activation(mag[:, c, :], ps[:, 4 + c, :], ACT.Abs, bias=b_dt[:, c:c + 1]))
            link(nc.scalar.activation(mag[:], mag[:], ACT.Exp, scale=-1.0))
            link(nc.scalar.activation(mag[:], mag[:], ACT.Ln, bias=env.eps[:, 2:3]))

            def state_step(n, i):
                act.wait_ge(spread_done, 2 * n + 1)
                wait(act, u_ready, IC * (n - 1))
                nc.scalar.copy(B_all[:, i, :], ps[:, i, :]).then_inc(B_ready, 1)
                for c in range(IC):
                    wait(act, scanned, IC * (n - 2) + c + 1)
                    nc.scalar.activation(dA[:, i, c, :, 1:], by_sample(delta[:, c, :]), ACT.Exp,
                                         scale=A[:, c, bass.ds(n, 1)]).then_inc(dA_ready, 1)

            act.wait_ge(delta_ready, IC)
            act.wait_ge(dtx_ready, 1)
            act.wait_ge(pads_set, 4)
            state_step(0, 0)
            state_step(1, 1)
            with act.Fori(1, STATES // 2) as j:
                state_step(2 * j, 0)
                state_step(2 * j + 1, 1)

        @block.gpsimd
        def _(pool):
            env.norm.gpsimd(pool)
            nc.gpsimd.memset(dA[:, :, :, :, 0:1].rearrange("p i c b o -> p (i c b) o"), 0.0).then_inc(pads_set, 1)
            nc.gpsimd.memset(u[:, :, :, :, 0:1].rearrange("p i c b o -> p (i c b) o"), 0.0).then_inc(pads_set, 1)

            def inputs(n, i):
                pool.wait_ge(B_ready, n + 1)
                for c in range(IC):
                    wait(pool, scanned, IC * (n - 2) + c + 1)
                    nc.gpsimd.tensor_tensor(u[:, i, c, :, 1:], by_sample(dtx[:, c, :]), by_sample(B_all[:, i, :]),
                                            ALU.mult).then_inc(u_ready, 1)

            pool.wait_ge(pads_set, 4)
            pool.wait_ge(dtx_ready, 1)
            inputs(0, 0)
            inputs(1, 1)
            with pool.Fori(1, STATES // 2) as j:
                inputs(2 * j, 0)
                inputs(2 * j + 1, 1)

        @block.vector
        def _(dve):
            env.norm.vector(dve)
            nc.vector.memset(dbc[32:64, :], 0.0).then_inc(pads_set, 1)
            nc.vector.memset(dbc[64:P, :], 0.0).then_inc(pads_set, 1)
            dve.wait_ge(A_ready, 1)
            nc.vector.tensor_scalar(A[:], A[:], -1.0, None, ALU.mult).then_inc(dstep, 1)
            dve.wait_ge(astep, 2 * IC + 2)
            for c in range(IC):
                nc.vector.tensor_tensor(delta[:, c, :], delta[:, c, :], mag[:, c, :], ALU.add).then_inc(delta_ready, 1)
            dve.wait_ge(delta_ready, IC)
            dve.wait_ge(dstep, 1)
            dve.wait_ge(x_ready, IC)
            nc.vector.tensor_tensor(dtx[:], delta[:], xT[:], ALU.mult).then_inc(dtx_ready, 1)

            def pick_rows(n, i):
                wait(dve, spread_done, 2 * n - 2)
                for s in range(2):
                    nc.vector.tensor_scalar(row[:, i, s, :], dbc[:], pick[:, bass.ds(n + s * STATES, 1)], None,
                                            ALU.mult).then_inc(row_ready, 1)

            def state_step(n, i):
                dve.wait_ge(spread_done, 2 * n + 2)
                for c in range(IC):
                    dve.wait_ge(dA_ready, IC * n + c + 1)
                    dve.wait_ge(u_ready, IC * n + c + 1)
                    wait(dve, prod_ready, IC * (n - 1) + c + 1)
                    nc.vector.tensor_tensor_scan(flat(state[:, c]), flat(dA[:, i, c]), flat(u[:, i, c]), 0.0,
                                                 ALU.mult, ALU.add).then_inc(scanned, 1)
                for c in range(IC):
                    dve.wait_ge(scanned, IC * n + c + 1)
                    wait(dve, y_done, IC * (n - 2) + c + 1)
                    nc.vector.tensor_tensor(by_sample(prod[:, i, c, :]), state[:, c, :, 1:],
                                            by_sample(ps[:, 2 + i, :]), ALU.mult).then_inc(prod_ready, 1)

            dve.wait_ge(dbc_ready, 1)
            pick_rows(0, 0)
            pick_rows(1, 1)
            state_step(0, 0)
            pick_rows(2, 0)
            state_step(1, 1)
            with dve.Fori(1, STATES // 2 - 1) as j:
                pick_rows(2 * j + 1, 1)
                state_step(2 * j, 0)
                pick_rows(2 * j + 2, 0)
                state_step(2 * j + 1, 1)
            pick_rows(STATES - 1, 1)
            state_step(STATES - 2, 0)
            state_step(STATES - 1, 1)
            for c in range(IC):
                dve.wait_ge(y_done, IC * (STATES - 1) + c + 1)
                nc.vector.scalar_tensor_tensor(out=xT[:, c, :], in0=xT[:, c, :], scalar=Dskip[:, c:c + 1],
                                               in1=ps[:, 4 + c, :], op0=ALU.mult, op1=ALU.add).then_inc(dstep, 1)
                dve.wait_ge(dstep, 2 + c)
                nc.vector.tensor_tensor(xT[:, c, :], xT[:, c, :], zT[:, c, :], ALU.mult).then_inc(y_ready, 1)
            add_out(nc, env, dve, out_done, x_added)


def self_attention(nc, env, ins):
    W = HG * P
    with ExitStack() as mem, layer_stage(
            nc, env, mem, "weights_in", "qkv_done", "qT_ready", "kT_ready", "kbd_ready", "v_ready", "scores_done", "max_ready",
            "probs_ready", "factor_ready", "normed", "turned", "probsT_ready", "pv_done", "masked", "oT_ready", "out_done",
            "vstep", "moments_done", "std_done") as (
            block, weights_in, qkv_done, qT_ready, kT_ready, kbd_ready, v_ready, scores_done, max_ready,
            probs_ready, factor_ready, normed, turned, probsT_ready, pv_done, masked, oT_ready, out_done,
            vstep, moments_done, std_done):
        sb = allocator(nc, mem)
        ps = env.ps
        wq, wk, wv, wo = (sb(n, [P, KD, D]) for n in ("wq", "wk", "wv", "wo"))
        bq, bk = sb("bq", [P, KD]), sb("bk", [P, KD])
        bv, bo = sb("bv", [1, D]), sb("bo", [1, D])
        gamma, beta = sb("gamma", [P, D]), sb("beta", [P, D])
        qT, kT = sb("qT", [P, GROUPS, T]), sb("kT", [P, GROUPS, T])
        kbd = sb("kbd", [P, 2, HG, P])
        v = sb("v", [P, TT, D])
        scores = sb("scores", [P, 2, HG, P])
        probs = sb("probs", [P, 2, HG, P])
        probsT = sb("probsT", [P, 2, HG, P])
        top, total = sb("top", [P, TT * HEADS]), sb("total", [P, TT * HEADS])
        prod = sb("prod", [P, 2, 2, P])
        oT = sb("oT", [P, GROUPS, T])
        acc = sb("acc", [P, TT, D])
        stats, mv, std = sb("stats", [P, TT, 6]), sb("mv", [P, TT, 2]), sb("std", [P, TT])
        STEPS = TT * GROUPS
        score_bank = lambda s: 0 if s % 2 == 0 else 6

        @block.sync
        def _(sp):
            env.norm.sync(sp)
            for n, dst in (("wq", wq), ("wk", wk), ("wv", wv), ("wo", wo)):
                sp.dma_start(dst[:], ins["L1_attn_" + n].rearrange("(k p) n -> p k n", p=P)).then_inc(weights_in, 16)
            sp.dma_start(bq[:], ins["L1_attn_bq"]).then_inc(weights_in, 16)
            sp.dma_start(bk[:], ins["L1_attn_bk"]).then_inc(weights_in, 16)
            sp.dma_start(bv[:], ins["L1_attn_bv"].unsqueeze(0)).then_inc(weights_in, 16)
            sp.dma_start(bo[:], ins["L1_attn_bo"].unsqueeze(0)).then_inc(weights_in, 16)
            sp.dma_start(gamma[:], rows_of(ins["L1_attn_gamma"])).then_inc(weights_in, 16)
            sp.dma_start(beta[:], rows_of(ins["L1_attn_beta"])).then_inc(weights_in, 16)

        @block.tensor
        def _(pe):
            env.norm.tensor(pe)
            pe.wait_ge(weights_in, 160)
            for s, w in ((0, wk), (2, wq)):
                for g in range(GROUPS):
                    project(nc, ps[:, s + g, :], lambda k: w[:, k, g * P:(g + 1) * P], KD,
                            lambda k: env.hT[:, k, :]).then_inc(qkv_done, 1)
            for t in range(TT):
                nc.tensor.matmul(ps[:, 4 + t, 0:D], env.ones[0:1, 0:P], bv[:], start=True, stop=False)
                for k in range(KD):
                    last = nc.tensor.matmul(ps[:, 4 + t, 0:D], env.hT[:, k, t * P:(t + 1) * P], wv[:, k, :],
                                            start=False, stop=(k == KD - 1))
                last.then_inc(qkv_done, 1)

            def score(s):
                t, g = s // GROUPS, s % GROUPS
                pe.wait_ge(kbd_ready, s + 1)
                if s == 0:
                    pe.wait_ge(qT_ready, GROUPS)
                wait(pe, max_ready, HG * (s - 1))
                for half in range(2):
                    last = nc.tensor.matmul(ps[:, score_bank(s) + half, :], qT[:, g, t * P:(t + 1) * P],
                                            kbd[:, s % 2, 4 * half:4 * half + 4, :].rearrange("p h k -> p (h k)"),
                                            start=True, stop=True)
                last.then_inc(scores_done, 1)

            def turn(s):
                pe.wait_ge(normed, s + 1)
                wait(pe, probsT_ready, s)
                for h in range(HG):
                    last = nc.tensor.transpose(ps[:, 2 + h // 4, (h % 4) * P:(h % 4 + 1) * P], probs[:, s % 2, h, :],
                                               env.ident[:])
                last.then_inc(turned, 1)

            def values(s):
                g = s % GROUPS
                pe.wait_ge(probsT_ready, s + 1)
                wait(pe, masked, s - 1)
                for j in range(4):
                    c = (4 * g + j) * 2 * HD
                    last = nc.tensor.matmul(ps[32 * j:32 * j + 32, 4 + s % 2, 0:2 * P], v[:, s // GROUPS, c:c + 2 * HD],
                                            probsT[:, s % 2, 2 * j:2 * j + 2, :].rearrange("p h q -> p (h q)"),
                                            start=True, stop=True)
                last.then_inc(pv_done, 1)

            score(0)
            pe.wait_ge(v_ready, TT)
            score(1)
            for s in range(STEPS):
                if s + 2 < STEPS:
                    score(s + 2)
                turn(s)
                if s >= 1:
                    values(s - 1)
            values(STEPS - 1)
            pe.wait_ge(oT_ready, STEPS)
            pe.wait_ge(v_ready, TT)
            project_out(nc, env, pe, oT, wo, KD, out_done, bo[:])

        @block.scalar
        def _(act):
            env.norm.scalar(act)
            act.wait_ge(weights_in, 160)
            for t in range(TT):
                act.wait_ge(qkv_done, 2 * GROUPS + t + 1)
                nc.scalar.copy(v[:, t, :], ps[:, 4 + t, 0:D]).then_inc(v_ready, 1)

            def take_turned(s):
                act.wait_ge(turned, s + 1)
                wait(act, pv_done, s - 1)
                nc.scalar.copy(probsT[:, s % 2].rearrange("p h q -> p (h q)"), ps[:, 2:4, :].rearrange("p b n -> p (b n)"))\
                    .then_inc(probsT_ready, 1)

            for s in range(STEPS):
                act.wait_ge(max_ready, HG * (s + 1))
                wait(act, turned, s - 1)
                for h in range(HG):
                    i = HG * s + h
                    nc.scalar.activation(probs[:, s % 2, h, :], scores[:, s % 2, h, :], ACT.Exp, bias=top[:, i:i + 1],
                                         scale=-1.0, accum_out=total[:, i:i + 1]).then_inc(probs_ready, 1)
                if s >= 1:
                    take_turned(s - 1)
            take_turned(STEPS - 1)
            act.wait_ge(moments_done, TT)
            nc.scalar.activation(std[:], mv[:, :, 1], ACT.Sqrt, bias=env.eps[:, 0:1]).then_inc(std_done, 1)

        @block.gpsimd
        def _(pool):
            env.norm.gpsimd(pool)
            for s in range(STEPS):
                pool.wait_ge(factor_ready, s + 1)
                nc.gpsimd.tensor_tensor(probs[:, s % 2], probs[:, s % 2],
                                        total[:, HG * s:HG * (s + 1)].unsqueeze(2).broadcast_to([P, HG, P]),
                                        ALU.mult).then_inc(normed, 1)

        @block.vector
        def _(dve):
            env.norm.vector(dve)
            link = Chain(dve, vstep)
            dve.wait_ge(weights_in, 160)
            for g in range(GROUPS):
                dve.wait_ge(qkv_done, g + 1)
                nc.vector.tensor_scalar(kT[:, g, :], ps[:, g, :], bk[:, g:g + 1], None, ALU.add).then_inc(kT_ready, 1)
            for g in range(GROUPS):
                dve.wait_ge(qkv_done, GROUPS + g + 1)
                nc.vector.tensor_scalar(qT[:, g, :], ps[:, 2 + g, :], bq[:, g:g + 1], HD ** -0.5, ALU.add, ALU.mult)\
                    .then_inc(qT_ready, 1)
            dve.wait_ge(kT_ready, GROUPS)

            def spread(s):
                t, g = s // GROUPS, s % GROUPS
                wait(dve, scores_done, s - 1)
                nc.vector.tensor_tensor(kbd[:, s % 2], kT[:, g, t * P:(t + 1) * P].unsqueeze(1).broadcast_to([P, HG, P]),
                                        env.head_mask[:].unsqueeze(2).broadcast_to([P, HG, P]),
                                        ALU.mult).then_inc(kbd_ready, 1)

            def softmax(s):
                dve.wait_ge(scores_done, s + 1)
                wait(dve, probs_ready, HG * (s - 1))
                for h in range(HG):
                    i = HG * s + h
                    nc.vector.tensor_tensor_reduce(
                        out=scores[:, s % 2, h, :], in0=ps[:, score_bank(s) + h // 4, (h % 4) * P:(h % 4 + 1) * P],
                        in1=env.same_sample[:], scale=-1.0, scalar=3e38, op0=ALU.add, op1=ALU.min,
                        accum_out=top[:, i:i + 1]).then_inc(max_ready, 1)

            def norm(s):
                dve.wait_ge(probs_ready, HG * (s + 1))
                nc.vector.reciprocal(total[:, HG * s:HG * (s + 1)], total[:, HG * s:HG * (s + 1)])\
                    .then_inc(factor_ready, 1)

            def extract(s):
                t, g = s // GROUPS, s % GROUPS
                dve.wait_ge(pv_done, s + 1)
                wait(dve, oT_ready, s - 1)
                nc.vector.tensor_tensor(prod[:, s % 2], ps[:, 4 + s % 2, 0:2 * P].rearrange("p (h q) -> p h q", h=2),
                                        env.pair_mask[:].unsqueeze(2).broadcast_to([P, 2, P]), ALU.mult)\
                    .then_inc(masked, 1)
                dve.wait_ge(masked, s + 1)
                nc.vector.tensor_tensor(oT[:, g, t * P:(t + 1) * P], prod[:, s % 2, 0, :], prod[:, s % 2, 1, :], ALU.add)\
                    .then_inc(oT_ready, 1)

            spread(0)
            spread(1)
            softmax(0)
            for s in range(STEPS):
                if s + 2 < STEPS:
                    spread(s + 2)
                if s + 1 < STEPS:
                    softmax(s + 1)
                norm(s)
                if s >= 2:
                    extract(s - 2)
            extract(STEPS - 2)
            extract(STEPS - 1)
            for t in range(TT):
                dve.wait_ge(out_done, t + 1)
                link(nc.vector.tensor_tensor(acc[:, t, :], env.h[:, t, :], ps[:, t, 0:D], ALU.add))
            normalize_rows(nc, env, link, acc, acc, stats, mv, std, moments_done, std_done, dve, gamma[:], beta[:])
            link(nc.vector.tensor_tensor(env.x[:], env.x[:], acc[:], ALU.add))


def rotary_attention(nc, env, ins):
    with ExitStack() as mem, layer_stage(
            nc, env, mem, "weights_in", "proj_done", "vstep", "rotated", "v_ready", "scores_done", "max_ready", "probs_ready",
            "turned", "probsT_ready", "out_done", "x_added") as (
            block, weights_in, proj_done, vstep, rotated, v_ready, scores_done, max_ready, probs_ready,
            turned, probsT_ready, out_done, x_added):
        sb = allocator(nc, mem)
        ps = env.ps
        wq, wk, wv = (sb(n, [P, KD, D]) for n in ("wq", "wk", "wv"))
        cos, sin = sb("cos", [P, SEQ]), sb("sin", [P, SEQ])
        rot = sb("rot", [P, 2, KD, T])
        tmp = sb("tmp", [P, 2, T])
        v = sb("v", [P, TT, D])
        scores, probs, probsT = sb("scores", [P, TT, P]), sb("probs", [P, TT, P]), sb("probsT", [P, TT, P])
        top, total = sb("top", [P, TT]), sb("total", [P, TT])

        @block.sync
        def _(sp):
            env.norm.sync(sp)
            for n, dst in (("wqT", wq), ("wkT", wk), ("wvT", wv)):
                sp.dma_start(dst[:], ins["L2_attn_" + n].rearrange("(k p) n -> p k n", p=P)).then_inc(weights_in, 16)
            sp.dma_start(cos[:], env.consts["cos256"]).then_inc(weights_in, 16)
            sp.dma_start(sin[:], env.consts["sin256"]).then_inc(weights_in, 16)

        @block.tensor
        def _(pe):
            env.norm.tensor(pe)
            pe.wait_ge(weights_in, 80)
            for s, w in ((0, wq), (2, wk)):
                for c in range(KD):
                    project(nc, ps[:, s + c, :], lambda k: w[:, k, c * P:(c + 1) * P], KD, lambda k: env.hT[:, k, :])\
                        .then_inc(proj_done, 1)
            for t in range(TT):
                project(nc, ps[:, 4 + t, 0:D], lambda k: env.hT[:, k, t * P:(t + 1) * P], KD, lambda k: wv[:, k, :])\
                    .then_inc(proj_done, 1)
            pe.wait_ge(rotated, 4)
            for t in range(TT):
                project(nc, ps[:, t, 0:P], lambda k: rot[:, 0, k, t * P:(t + 1) * P], KD,
                        lambda k: rot[:, 1, k, t * P:(t + 1) * P]).then_inc(scores_done, 1)
            pe.wait_ge(v_ready, TT)
            for t in range(TT):
                pe.wait_ge(probs_ready, t + 1)
                nc.tensor.transpose(ps[:, 4 + t, 0:P], probs[:, t, :], env.ident[:]).then_inc(turned, 1)
            for t in range(TT):
                pe.wait_ge(probsT_ready, t + 1)
                nc.tensor.matmul(ps[:, t, 0:D], probsT[:, t, :], v[:, t, :], start=True, stop=True)\
                    .then_inc(out_done, 1)

        @block.scalar
        def _(act):
            env.norm.scalar(act)
            for t in range(TT):
                act.wait_ge(proj_done, 4 + t + 1)
                nc.scalar.copy(v[:, t, :], ps[:, 4 + t, 0:D]).then_inc(v_ready, 1)
            for t in range(TT):
                act.wait_ge(max_ready, t + 1)
                nc.scalar.activation(probs[:, t, :], scores[:, t, :], ACT.Exp, bias=top[:, t:t + 1],
                                     scale=-1.0, accum_out=total[:, t:t + 1]).then_inc(probs_ready, 1)
            for t in range(TT):
                act.wait_ge(turned, t + 1)
                nc.scalar.copy(probsT[:, t, :], ps[:, 4 + t, 0:P]).then_inc(probsT_ready, 1)

        @block.gpsimd
        def _(pool):
            env.norm.gpsimd(pool)

        @block.vector
        def _(dve):
            env.norm.vector(dve)
            link = Chain(dve, vstep)
            dve.wait_ge(weights_in, 80)
            table = lambda tab: tab[:].unsqueeze(1).broadcast_to([P, BATCH, SEQ])
            wide = lambda ap: ap.rearrange("p (b t) -> p b t", b=BATCH)
            for s in range(2):
                dve.wait_ge(proj_done, 2 * s + 2)
                even, odd = ps[:, 2 * s, :], ps[:, 2 * s + 1, :]
                for c, a, b, op in ((0, even, odd, ALU.add), (1, odd, even, ALU.subtract)):
                    nc.vector.tensor_tensor(wide(tmp[:, 0, :]), wide(a), table(cos), ALU.mult).then_inc(vstep, 1)
                    link.n += 1
                    link(nc.vector.tensor_tensor(wide(tmp[:, 1, :]), wide(b), table(sin), ALU.mult))
                    nc.vector.tensor_tensor(rot[:, s, c, :], tmp[:, 0, :], tmp[:, 1, :], op).then_inc(rotated, 1)
                    dve.wait_ge(rotated, 2 * s + c + 1)
                if s == 0:
                    link(nc.vector.tensor_scalar(rot[:, 0], rot[:, 0], D ** -0.5, None, ALU.mult))
            for t in range(TT):
                dve.wait_ge(scores_done, t + 1)
                nc.vector.tensor_tensor_reduce(out=scores[:, t, :], in0=ps[:, t, 0:P], in1=env.same_sample[:],
                                               scale=-1.0, scalar=3e38, op0=ALU.add, op1=ALU.min,
                                               accum_out=top[:, t:t + 1]).then_inc(max_ready, 1)
            dve.wait_ge(probs_ready, TT)
            link(nc.vector.reciprocal(total[:], total[:]))
            for t in range(TT):
                dve.wait_ge(out_done, t + 1)
                nc.vector.scalar_tensor_tensor(out=env.x[:, t, :], in0=ps[:, t, 0:D], scalar=total[:, t:t + 1],
                                               in1=env.x[:, t, :], op0=ALU.mult, op1=ALU.add).then_inc(x_added, 1)


def context_fusion(nc, env, ins):
    FEATS = 4 * KD
    with ExitStack() as mem, layer_stage(
            nc, env, mem, "consts_in", "ctxT_in0", "ctxT_in1", "ctx_in0", "ctx_in1", "qw_ready", "scores_done", "max_ready", "probs_ready", "turned",
            "probsT_ready", "pv_done", "hq_ready", "vstep", "wqv_in", "own_ready", "line_ready", "exp_done", "sums_turned", "weights_ready", "weights_turned",
            "spread_ready", "mix_done", "feats_ready", "feats_turned", "featsT_ready", "out_done", "x_added") as (
            block, consts_in, ctxT_in0, ctxT_in1, ctx_in0, ctx_in1, qw_ready, scores_done, max_ready, probs_ready, turned,
            probsT_ready, pv_done, hq_ready, vstep, wqv_in, own_ready, line_ready, exp_done, sums_turned, weights_ready, weights_turned,
            spread_ready, mix_done, feats_ready, feats_turned, featsT_ready, out_done, x_added):
        sb = allocator(nc, mem)
        ps = env.ps
        w23, w1, b_sim = sb("w23", [P, 2, KD]), sb("w1", [P, D]), sb("b_sim", [P, 1])
        wqv, bqv = sb("wqv", [P, FEATS, D]), sb("bqv", [1, D])
        same = sb("same", [P, P])
        cT, ctx = sb("ctxT", [P, 2, 2, KD, CTX]), sb("ctx", [P, 2, 2, CC, D])
        qw = sb("qw", [P, KD, T])
        probs, probsT = sb("probs", [P, 2, CTX]), sb("probsT", [P, 2, CC, P])
        top, total, own = sb("top", [P, TT]), sb("total", [P, TT]), sb("own", [P, TT])
        junk = sb("junk", [P, D])
        line, peak, norm = sb("line", [TT, P]), sb("peak", [TT, 2]), sb("norm", [TT, 2])
        weights, spread = sb("weights", [P, TT]), sb("spread", [P, TT, P])
        feats = sb("feats", [P, 3, TT, D])
        featsT = sb("featsT", [P, 3 * KD, T])
        ctxT_in, ctx_in = (ctxT_in0, ctxT_in1), (ctx_in0, ctx_in1)
        split = lambda ap: ap.rearrange("p (b i) -> p b i", b=2)

        @block.sync
        def _(sp):
            env.norm.sync(sp)
            for dst, src in ((w23, ins["L2_xattn_w23"]), (w1, rows_of(ins["L2_xattn_w1"])),
                             (b_sim, rows_of(ins["L2_xattn_b_sim"])), (same, env.consts["same"])):
                sp.dma_start(dst[:], src).then_inc(consts_in, 16)
            for t in range(TT):
                wait(sp, scores_done, t - 1)
                for i in range(2):
                    sp.dma_start(cT[:, t % 2, i], ins["ctxT"][2 * t + i].rearrange("(k p) s -> p k s", p=P))\
                        .then_inc(ctxT_in[t % 2], 16)
                wait(sp, pv_done, t - 1)
                for i in range(2):
                    sp.dma_start(ctx[:, t % 2, i], ins["ctx"][2 * t + i].rearrange("(c p) d -> p c d", p=P))\
                        .then_inc(ctx_in[t % 2], 16)
            sp.dma_start(wqv[:], ins["L2_xattn_W_qv"].rearrange("(f p) n -> p f n", p=P)).then_inc(wqv_in, 16)
            sp.dma_start(bqv[:], ins["L2_xattn_b_qv"].unsqueeze(0)).then_inc(wqv_in, 16)

        @block.tensor
        def _(pe):
            env.norm.tensor(pe)
            def score(t):
                pe.wait_ge(ctxT_in[t % 2], 32 * (t // 2 + 1))
                pe.wait_ge(qw_ready, KD)
                wait(pe, probs_ready, t - 1)
                for half in range(2):
                    for k in range(KD):
                        for i in range(2):
                            last = nc.tensor.matmul(
                                ps[SEQ * i:SEQ * (i + 1), 2 * (t % 2) + half, :],
                                qw[:, k, (2 * t + i) * SEQ:(2 * t + i + 1) * SEQ],
                                cT[:, t % 2, i, k, half * BANK:(half + 1) * BANK], start=(k == 0), stop=(k == KD - 1))
                last.then_inc(scores_done, 1)

            def attend(t):
                pe.wait_ge(probs_ready, t + 1)
                wait(pe, probsT_ready, 2 * t)
                for half in range(2):
                    for c in range(4):
                        last = nc.tensor.transpose(ps[:, 4 + half, c * P:(c + 1) * P],
                                                   probs[:, t % 2, (4 * half + c) * P:(4 * half + c + 1) * P],
                                                   env.ident[:])
                    last.then_inc(turned, 1)
                pe.wait_ge(probsT_ready, 2 * t + 2)
                wait(pe, hq_ready, t - 1)
                pe.wait_ge(ctx_in[t % 2], 32 * (t // 2 + 1))
                for c in range(CC):
                    for i in range(2):
                        last = nc.tensor.matmul(ps[SEQ * i:SEQ * (i + 1), 6 + t % 2, 0:D],
                                                probsT[:, t % 2, c, SEQ * i:SEQ * (i + 1)], ctx[:, t % 2, i, c, :],
                                                start=(c == 0), stop=(c == CC - 1))
                last.then_inc(pv_done, 1)

            score(0)
            for t in range(TT):
                if t + 1 < TT:
                    score(t + 1)
                attend(t)
            pe.wait_ge(own_ready, 1)
            nc.tensor.transpose(ps[0:TT, 0, 0:P], own[:], env.ident[:]).then_inc(sums_turned, 1)
            pe.wait_ge(weights_ready, 1)
            nc.tensor.transpose(ps[:, 1, 0:TT], line[:], env.ident[0:TT, 0:TT]).then_inc(weights_turned, 1)
            for t in range(TT):
                pe.wait_ge(spread_ready, t + 1)
                nc.tensor.matmul(ps[:, 2 + t, 0:D], spread[:, t, :], env.h[:, t, :], start=True, stop=True)\
                    .then_inc(mix_done, 1)
            for n in range(3 * KD):
                pe.wait_ge(feats_ready, (n // KD + 1) * TT)
                wait(pe, featsT_ready, n - 3)
                for t in range(TT):
                    last = nc.tensor.transpose(ps[:, (0, 1, 6, 7)[n % 4], t * P:(t + 1) * P],
                                               feats[:, n // KD, t, (n % KD) * P:(n % KD + 1) * P], env.ident[:])
                last.then_inc(feats_turned, 1)
            pe.wait_ge(featsT_ready, 3 * KD)
            pe.wait_ge(wqv_in, 32)
            for t in range(TT):
                nc.tensor.matmul(ps[:, t, 0:D], env.ones[0:1, 0:P], bqv[:], start=True, stop=False)
                for f in range(FEATS):
                    src = env.hT[:, f, t * P:(t + 1) * P] if f < KD else featsT[:, f - KD, t * P:(t + 1) * P]
                    last = nc.tensor.matmul(ps[:, t, 0:D], src, wqv[:, f, :], start=False, stop=(f == FEATS - 1))
                last.then_inc(out_done, 1)

        @block.scalar
        def _(act):
            env.norm.scalar(act)
            for t in range(TT):
                act.wait_ge(max_ready, t + 1)
                wait(act, turned, 2 * (t - 1))
                nc.scalar.activation(probs[:, t % 2, :], ps[:, 2 * (t % 2):2 * (t % 2) + 2, :].rearrange(
                    "p b n -> p (b n)"), ACT.Exp, bias=top[:, t:t + 1], accum_out=total[:, t:t + 1])\
                    .then_inc(probs_ready, 1)
                act.wait_ge(turned, 2 * t + 1)
                nc.scalar.copy(probsT[:, t % 2, 0:4, :].rearrange("p c q -> p (c q)"), ps[:, 4, :])\
                    .then_inc(probsT_ready, 1)
            act.wait_ge(line_ready, 1)
            nc.scalar.activation(line[:], line[:], ACT.Exp).then_inc(exp_done, 1)

        @block.gpsimd
        def _(pool):
            env.norm.gpsimd(pool)

        @block.vector
        def _(dve):
            env.norm.vector(dve)
            link = Chain(dve, vstep)
            dve.wait_ge(consts_in, 64)
            for k in range(KD):
                nc.vector.tensor_scalar(qw[:, k, :], env.hT[:, k, :], w23[:, 1, k:k + 1], w23[:, 0, k:k + 1],
                                        ALU.mult, ALU.add).then_inc(qw_ready, 1)
            for t in range(TT):
                link(nc.vector.tensor_tensor_reduce(out=junk[:], in0=env.h[:, t, :], in1=w1[:], scale=1.0, scalar=0.0,
                                                    op0=ALU.mult, op1=ALU.add, accum_out=own[:, t:t + 1]))
            for t in range(TT):
                dve.wait_ge(scores_done, t + 1)
                nc.vector.tensor_reduce(top[:, t:t + 1], ps[:, 2 * (t % 2):2 * (t % 2) + 2, :].rearrange(
                    "p b n -> p (b n)"), AX.X, ALU.max, negate=True).then_inc(max_ready, 1)
                dve.wait_ge(turned, 2 * t + 2)
                nc.vector.tensor_copy(probsT[:, t % 2, 4:8, :].rearrange("p c q -> p (c q)"), ps[:, 5, :])\
                    .then_inc(probsT_ready, 1)
                link(nc.vector.reciprocal(total[:, t:t + 1], total[:, t:t + 1]))
                dve.wait_ge(pv_done, t + 1)
                nc.vector.tensor_scalar(feats[:, 0, t, :], ps[:, 6 + t % 2, 0:D], total[:, t:t + 1], None, ALU.mult)\
                    .then_inc(hq_ready, 1)
            dve.wait_ge(max_ready, TT)
            nc.vector.scalar_tensor_tensor(out=own[:], in0=own[:], scalar=b_sim[:], in1=top[:],
                                           op0=ALU.add, op1=ALU.subtract).then_inc(own_ready, 1)
            dve.wait_ge(sums_turned, 1)
            link(nc.vector.tensor_reduce(peak[:], split(ps[0:TT, 0, 0:P]), AX.X, ALU.max))
            nc.vector.tensor_tensor(split(line[:]), split(ps[0:TT, 0, 0:P]),
                                    peak[:].unsqueeze(2).broadcast_to([TT, 2, SEQ]), ALU.subtract)\
                .then_inc(line_ready, 1)
            dve.wait_ge(hq_ready, TT)
            for t in range(TT):
                nc.vector.engine_nop().then_inc(feats_ready, 1)
            for t in range(TT):
                nc.vector.tensor_tensor(feats[:, 1, t, :], feats[:, 0, t, :], env.h[:, t, :], ALU.mult)\
                    .then_inc(feats_ready, 1)
            dve.wait_ge(exp_done, 1)
            link(nc.vector.tensor_reduce(norm[:], split(line[:]), AX.X, ALU.add))
            link(nc.vector.reciprocal(norm[:], norm[:]))
            nc.vector.tensor_tensor(split(line[:]), split(line[:]), norm[:].unsqueeze(2).broadcast_to([TT, 2, SEQ]),
                                    ALU.mult).then_inc(weights_ready, 1)
            dve.wait_ge(weights_turned, 1)
            link(nc.vector.tensor_copy(weights[:], ps[:, 1, 0:TT]))
            for t in range(TT):
                nc.vector.tensor_scalar(spread[:, t, :], same[:], weights[:, t:t + 1], None, ALU.mult)\
                    .then_inc(spread_ready, 1)
            for t in range(TT):
                dve.wait_ge(mix_done, t + 1)
                nc.vector.tensor_tensor(feats[:, 2, t, :], ps[:, 2 + t, 0:D], env.h[:, t, :], ALU.mult)\
                    .then_inc(feats_ready, 1)
            for n in range(3 * KD):
                dve.wait_ge(feats_turned, n + 1)
                nc.vector.tensor_copy(featsT[:, n, :], ps[:, (0, 1, 6, 7)[n % 4], :]).then_inc(featsT_ready, 1)
            add_out(nc, env, dve, out_done, x_added)


def softmax_cross_attention(nc, env, ins):
    PAIRS = HEADS // 2
    PG = PAIRS // GROUPS
    K_UNITS, UNITS = 4, 8
    with ExitStack() as mem, layer_stage(
            nc, env, mem, "weights_in", "mask_in", "ctx_in", "q_done", "q_ready", "unit_done", "k_taken", "v_taken",
            "qbd_ready", "scores_done", "max_ready", "exp_done", "probs_ready", "turned_a", "turned_b", "probsT_a",
            "probsT_b", "pv_done", "masked", "o_ready", "out_done", "x_added", "total_ready", "spare_set",
            "w_high", "w_split", "ctx_high", "ctx_split", "k_high", "q_low") as (
            block, weights_in, mask_in, ctx_in, q_done, q_ready, unit_done, k_taken, v_taken,
            qbd_ready, scores_done, max_ready, exp_done, probs_ready, turned_a, turned_b, probsT_a,
            probsT_b, pv_done, masked, o_ready, out_done, x_added, total_ready, spare_set,
            w_high, w_split, ctx_high, ctx_split, k_high, q_low):
        sb = allocator(nc, mem)
        ps = env.ps
        wq, wk, wv, wo = (sb(n, [P, KD, D]) for n in ("wq", "wk", "wv", "wo"))
        mask = sb("mask", [P, CTX])
        cT = sb("ctxT", [P, KD, CTX])
        v = sb("v", [P, 2, CC, D])
        high = lambda name, shape: mem.enter_context(nc.sbuf_tensor(name, shape, F32R, allow_name_mangling=True))
        wkh, wvh, cTh = high("wk_high", [P, KD, D]), high("wv_high", [P, KD, D]), high("ctxT_high", [P, 2, KD, CTX])
        wkl, wvl, cTl = high("wk_low", [P, KD, D]), high("wv_low", [P, KD, D]), high("ctxT_low", [P, 2, KD, CTX])
        kTh, kTl = high("kT_high", [P, 2, GROUPS, CTX]), high("kT_low", [P, 2, GROUPS, CTX])
        qTh, qTl = high("qT_high", [P, GROUPS, T]), high("qT_low", [P, GROUPS, T])
        qbdh, qbdl = high("qbd_high", [P, 2, GROUPS, HG, SEQ]), high("qbd_low", [P, 2, GROUPS, HG, SEQ])
        scores, probs = sb("scores", [P, 2, CTX]), sb("probs", [P, 2, CTX])
        probsT = sb("probsT", [P, GROUPS, CC, PG, P])
        spare = sb("spare", [P, 1])
        top, total = sb("top", [P, PAIRS]), sb("total", [P, PAIRS])
        prod, oT = sb("prod", [P, GROUPS, 2, SEQ]), sb("oT", [P, GROUPS, T])
        UNIT_BANK, O_BANK, S_BANK, T_BANK = 0, 1, 2, 6
        halves = lambda ap: ap.rearrange("p b n -> p (b n)")

        def samples(eng, body):
            body(0, 0, False)
            with eng.Fori(0, BATCH // 2 - 1) as j:
                body(2 * j + 1, 1, False)
                body(2 * j + 2, 0, False)
            body(BATCH - 1, 1, True)

        @block.sync
        def _(sp):
            env.norm.sync(sp)
            for n, dst in (("wq", wq), ("wk", wk), ("wv", wv), ("wo", wo)):
                sp.dma_start(dst[:], ins["L3_xattn_" + n].rearrange("(k p) n -> p k n", p=P)).then_inc(weights_in, 16)
            for b in range(BATCH):
                wait(sp, ctx_split, b)
                sp.dma_start(cT[:], ins["ctxT"][b].rearrange("(k p) s -> p k s", p=P))\
                    .then_inc(ctx_in, 16)
                if b == 0:
                    for i in range(2):
                        sp.dma_start(mask[i * SEQ:(i + 1) * SEQ, :], ins["mask"]).then_inc(mask_in, 16)

        @block.tensor
        def _(pe):
            env.norm.tensor(pe)
            def unit(b, i, u):
                if u == 0:
                    pe.wait_ge(ctx_split, b + 1)
                first = isinstance(b, int) and b == 0
                bank = UNIT_BANK + (u % 2 if first else 0)
                back = u - (2 if first else 1)
                if back >= K_UNITS:
                    wait(pe, v_taken, 4 * b + back - K_UNITS + 1)
                elif back >= 0:
                    wait(pe, k_taken, 4 * b + back + 1)
                elif not first:
                    wait(pe, v_taken, 4 * b)
                if u < K_UNITS:
                    g, half = u // 2, u % 2
                    weights, keys = slice(g * P, (g + 1) * P), slice(half * BANK, (half + 1) * BANK)
                    last = project_split(nc, ps[:, bank, :], lambda k: (wkh[:, k, weights], wkl[:, k, weights]), KD,
                                         lambda k: (cTh[:, i, k, keys], cTl[:, i, k, keys]))
                else:
                    for cc in range(2):
                        c = 2 * (u - K_UNITS) + cc
                        keys = slice(c * P, (c + 1) * P)
                        last = project_split(nc, ps[:, bank, cc * D:(cc + 1) * D],
                                             lambda k: (cTh[:, i, k, keys], cTl[:, i, k, keys]), KD,
                                             lambda k: (wvh[:, k, :], wvl[:, k, :]))
                last.then_inc(unit_done, 1)

            def score(b, i, p):
                g, j = p // PG, p % PG
                if p == 0:
                    pe.wait_ge(qbd_ready, 2 * GROUPS * (b + 1))
                    wait(pe, k_taken, 4 * (b + 1))
                wait(pe, max_ready, PAIRS * b + p - 1)
                for half in range(2):
                    keys = slice(half * BANK, (half + 1) * BANK)
                    last = split_product(nc, ps[:, S_BANK + 2 * (p % 2) + half, :],
                                         tuple(q[:, i, g, 2 * j:2 * j + 2, :].rearrange("p h l -> p (h l)")
                                               for q in (qbdh, qbdl)), (kTh[:, i, g, keys], kTl[:, i, g, keys]))
                last.then_inc(scores_done, 1)

            def turn(b, p):
                wait(pe, probs_ready, PAIRS * b + p + 1)
                for half, taken, done in ((0, probsT_a, turned_a), (1, probsT_b, turned_b)):
                    wait(pe, taken, PAIRS * b + p)
                    for c in range(4):
                        last = nc.tensor.transpose(ps[:, T_BANK + half, c * P:(c + 1) * P],
                                                   probs[:, p % 2, (4 * half + c) * P:(4 * half + c + 1) * P],
                                                   env.ident[:])
                    last.then_inc(done, 1)

            def values(b, i, g):
                pe.wait_ge(probsT_a, PAIRS * b + PG * (g + 1))
                pe.wait_ge(probsT_b, PAIRS * b + PG * (g + 1))
                if g == 0:
                    wait(pe, masked, GROUPS * b)
                    wait(pe, v_taken, 4 * (b + 1))
                for c in range(CC):
                    for j in range(PG):
                        first = g * P + 2 * HD * j
                        last = nc.tensor.matmul(ps[32 * j:32 * j + 32, O_BANK, g * P:(g + 1) * P],
                                                v[:, i, c, first:first + 2 * HD], probsT[:, g, c, j, :],
                                                start=(c == 0), stop=(c == CC - 1))
                last.then_inc(pv_done, 1)

            def sample(b, i, last):
                for p in range(PAIRS):
                    if not last:
                        unit(b + 1, 1 - i, p)
                    if p == 0 and not (isinstance(b, int) and b == 0):
                        values(b - 1, 1 - i, 1)
                    if p == PG:
                        values(b, i, 0)
                    turn(b, p)
                    if p + 2 < PAIRS:
                        score(b, i, p + 2)
                    elif not last:
                        score(b + 1, 1 - i, p + 2 - PAIRS)
                if last:
                    values(b, i, 1)

            pe.wait_ge(weights_in, 64)
            for g in range(GROUPS):
                project(nc, ps[:, S_BANK + g, :], lambda k: wq[:, k, g * P:(g + 1) * P], KD,
                        lambda k: env.hT[:, k, :]).then_inc(q_done, 1)
            pe.wait_ge(w_split, 2)
            for u in range(UNITS):
                unit(0, 0, u)
            pe.wait_ge(q_low, GROUPS)
            score(0, 0, 0)
            score(0, 0, 1)
            samples(pe, sample)
            pe.wait_ge(o_ready, GROUPS * BATCH)
            project_out(nc, env, pe, oT, wo, KD, out_done)

        @block.scalar
        def _(act):
            env.norm.scalar(act)
            def split_ctx(b, i):
                act.wait_ge(ctx_in, 16 * (b + 1))
                wait(act, unit_done, UNITS * (b - 1))
                nc.scalar.copy(cTh[:, i], cT[:]).then_inc(ctx_high, 1)

            def take(b, i, u):
                act.wait_ge(unit_done, UNITS * b + u + 1)
                bank = UNIT_BANK + (u % 2 if isinstance(b, int) and b == 0 else 0)
                if u < K_UNITS:
                    nc.scalar.copy(kTh[:, i, u // 2, (u % 2) * BANK:(u % 2 + 1) * BANK], ps[:, bank, :]).then_inc(k_high, 1)
                else:
                    nc.scalar.copy(v[:, i, 2 * (u - K_UNITS):2 * (u - K_UNITS) + 2, :].rearrange("p c n -> p (c n)"),
                                   ps[:, bank, :]).then_inc(v_taken, 1)

            split_ctx(0, 0)
            act.wait_ge(weights_in, 64)
            nc.scalar.copy(wkh[:], wk[:]).then_inc(w_high, 1)
            nc.scalar.copy(wvh[:], wv[:]).then_inc(w_high, 1)
            for g in range(GROUPS):
                act.wait_ge(q_done, g + 1)
                nc.scalar.mul(qTh[:, g, :], ps[:, S_BANK + g, :], HD ** -0.5).then_inc(q_ready, 1)
            split_ctx(1, 1)
            for u in range(UNITS):
                take(0, 0, u)

            def exponentials(b, p):
                n = PAIRS * b + p
                act.wait_ge(max_ready, n + 1)
                wait(act, turned_b, n - 1)
                nc.scalar.activation(probs[:, p % 2, :], scores[:, p % 2, :], ACT.Exp, bias=top[:, p:p + 1],
                                     scale=-1.0, accum_out=total[:, p:p + 1]).then_inc(exp_done, 1)

            def sample(b, i, last, ahead=True):
                for p in range(PAIRS):
                    if p == 2 and ahead:
                        split_ctx(b + 2, i)
                    if not last:
                        take(b + 1, 1 - i, p)
                    if p + 1 < PAIRS:
                        exponentials(b, p + 1)
                    elif not last:
                        exponentials(b + 1, 0)
                    act.wait_ge(turned_a, PAIRS * b + p + 1)
                    if p == 0:
                        wait(act, pv_done, GROUPS * b - 1)
                    if p == PG:
                        wait(act, pv_done, GROUPS * b)
                    nc.scalar.copy(probsT[:, p // PG, 0:4, p % PG, :],
                                   ps[:, T_BANK, :].rearrange("p (c q) -> p c q", c=4)).then_inc(probsT_a, 1)

            exponentials(0, 0)
            sample(0, 0, False)
            with act.Fori(0, BATCH // 2 - 2) as j:
                sample(2 * j + 1, 1, False)
                sample(2 * j + 2, 0, False)
            sample(BATCH - 3, 1, False)
            sample(BATCH - 2, 0, False, ahead=False)
            sample(BATCH - 1, 1, True, ahead=False)

        @block.gpsimd
        def _(pool):
            env.norm.gpsimd(pool)

            def split_ctx(b, i):
                pool.wait_ge(ctx_high, b + 1)
                nc.gpsimd.tensor_tensor(cTl[:, i], cT[:], cTh[:, i], ALU.subtract).then_inc(ctx_split, 1)

            split_ctx(0, 0)
            split_ctx(1, 1)
            with pool.Fori(1, BATCH // 2) as j:
                split_ctx(2 * j, 0)
                split_ctx(2 * j + 1, 1)

        @block.vector
        def _(dve):
            env.norm.vector(dve)
            def spread(b, i):
                for q, qbd in ((qTh, qbdh), (qTl, qbdl)):
                    for g in range(GROUPS):
                        nc.vector.tensor_tensor(
                            qbd[:, i, g], q[:, g, bass.ds(b * SEQ, SEQ)].unsqueeze(1).broadcast_to([P, HG, SEQ]),
                            env.head_mask[:].unsqueeze(2).broadcast_to([P, HG, SEQ]), ALU.mult).then_inc(qbd_ready, 1)

            def take(b, i, u):
                keys = slice((u % 2) * BANK, (u % 2 + 1) * BANK)
                bank = UNIT_BANK + (u % 2 if isinstance(b, int) and b == 0 else 0)
                dve.wait_ge(k_high, 4 * b + u + 1)
                nc.vector.tensor_tensor(kTl[:, i, u // 2, keys], ps[:, bank, :], kTh[:, i, u // 2, keys], ALU.subtract)\
                    .then_inc(k_taken, 1)

            def maxima(b, p):
                n = PAIRS * b + p
                dve.wait_ge(scores_done, n + 1)
                wait(dve, exp_done, n - 1)
                wait(dve, spare_set, n)
                nc.vector.memset(spare[:], 0.0).then_inc(spare_set, 1)
                nc.vector.tensor_tensor_reduce(
                    out=scores[:, p % 2, :], in0=halves(ps[:, S_BANK + 2 * (p % 2):S_BANK + 2 * (p % 2) + 2, :]),
                    in1=mask[:], scale=-1.0, scalar=3e38, op0=ALU.add, op1=ALU.min,
                    accum_out=top[:, p:p + 1]).then_inc(max_ready, 1)

            def normalize(b, p):
                n = PAIRS * b + p
                dve.wait_ge(exp_done, n + 1)
                nc.vector.reciprocal(total[:, p:p + 1], total[:, p:p + 1]).then_inc(total_ready, 1)
                dve.wait_ge(total_ready, n + 1)
                nc.vector.tensor_scalar(probs[:, p % 2, :], probs[:, p % 2, :], total[:, p:p + 1], None, ALU.mult)\
                    .then_inc(probs_ready, 1)

            def extract(b):
                dve.wait_ge(pv_done, GROUPS * b + GROUPS)
                for g in range(GROUPS):
                    wait(dve, o_ready, GROUPS * b)
                    nc.vector.tensor_tensor(
                        prod[:, g], ps[:, O_BANK, g * P:(g + 1) * P].rearrange("p (h l) -> p h l", h=2),
                        env.pair_mask[:].unsqueeze(2).broadcast_to([P, 2, SEQ]), ALU.mult).then_inc(masked, 1)
                for g in range(GROUPS):
                    dve.wait_ge(masked, GROUPS * b + g + 1)
                    nc.vector.tensor_tensor(oT[:, g, bass.ds(b * SEQ, SEQ)], prod[:, g, 0, :], prod[:, g, 1, :],
                                            ALU.add).then_inc(o_ready, 1)

            def sample(b, i, last):
                for p in range(PAIRS):
                    if not last and p == K_UNITS:
                        spread(b + 1, 1 - i)
                    dve.wait_ge(turned_b, PAIRS * b + p + 1)
                    nc.vector.tensor_copy(probsT[:, p // PG, 4:8, p % PG, :],
                                          ps[:, T_BANK + 1, :].rearrange("p (c q) -> p c q", c=4)).then_inc(probsT_b, 1)
                    if not last and p < K_UNITS:
                        take(b + 1, 1 - i, p)
                    if p + 1 < PAIRS:
                        normalize(b, p + 1)
                    elif not last:
                        normalize(b + 1, 0)
                    if p + 2 < PAIRS:
                        maxima(b, p + 2)
                    elif not last:
                        maxima(b + 1, p + 2 - PAIRS)
                    if p == 1 and not (isinstance(b, int) and b == 0):
                        extract(b - 1)
                if last:
                    extract(b)

            for i, (w, wh, wl) in enumerate(((wk, wkh, wkl), (wv, wvh, wvl))):
                dve.wait_ge(w_high, i + 1)
                nc.vector.tensor_tensor(wl[:], w[:], wh[:], ALU.subtract).then_inc(w_split, 1)
            for g in range(GROUPS):
                dve.wait_ge(q_ready, g + 1)
                nc.vector.scalar_tensor_tensor(out=qTl[:, g, :], in0=ps[:, S_BANK + g, :], scalar=HD ** -0.5,
                                               in1=qTh[:, g, :], op0=ALU.mult, op1=ALU.subtract).then_inc(q_low, 1)
            for u in range(K_UNITS):
                take(0, 0, u)
            dve.wait_ge(q_low, GROUPS)
            spread(0, 0)
            dve.wait_ge(mask_in, 32)
            maxima(0, 0)
            maxima(0, 1)
            normalize(0, 0)
            samples(dve, sample)
            add_out(nc, env, dve, out_done, x_added)


def latent_cross_attention(nc, env, ins):
    LH, LD = 16, 64
    INNER = LH * LD
    PAIRS = LH // 2
    PG = 4
    JOBS = CC
    FIRST = 2 * TT
    RING, LAG = 4, 3
    with ExitStack() as mem, layer_stage(
            nc, env, mem, "consts_in", "wq_in", "wout_in", "ctx_in0", "ctx_in1", "mask_in0", "mask_in1", "vstep", "pstep",
            "lat_normed", "lat_ready", "stats_ready", "rstd_ready", "centred", "xn_ready", "rows_turned", "xnT_ready",
            "k_done", "k_taken", "squared", "sums_ready", "factor_ready", "kn_ready", "kn_turned", "kT_a", "kT_b", "qbd_ready",
            "mask_ready", "slat_done", "slat_ready", "scores_done", "max_ready", "exp_done", "probs_ready",
            "turned_a", "turned_b", "probsT_a", "probsT_b", "lat_turned", "latT_ready", "y_done", "y_taken",
            "o_done", "o_ready", "out_done", "x_added", "spare_set", "latb_ready", "reduced", "scaled") as (
            block, consts_in, wq_in, wout_in, ctx_in0, ctx_in1, mask_in0, mask_in1, vstep, pstep,
            lat_normed, lat_ready, stats_ready, rstd_ready, centred, xn_ready, rows_turned, xnT_ready,
            k_done, k_taken, squared, sums_ready, factor_ready, kn_ready, kn_turned, kT_a, kT_b, qbd_ready,
            mask_ready, slat_done, slat_ready, scores_done, max_ready, exp_done, probs_ready,
            turned_a, turned_b, probsT_a, probsT_b, lat_turned, latT_ready, y_done, y_taken,
            o_done, o_ready, out_done, x_added, spare_set, latb_ready, reduced, scaled):
        sb = allocator(nc, mem)
        ps = env.ps
        wqo = sb("wqo", [P, 8 * D])
        wq = wqo[:].rearrange("p (k n) -> p k n", k=KD)
        wout = wqo[:].rearrange("p (k n) -> p k n", k=INNER // P)
        wk, wv = sb("wk", [P, KD, INNER]), sb("wv", [P, KD, INNER])
        bout = sb("bout", [1, D])
        xg, xb, lg, lb = (sb(n, [P, D]) for n in ("xg", "xb", "lg", "lb"))
        gains = sb("gains", [P, 2])
        lat = sb("lat", [P, TT, D])
        latb = sb("latb", [P, D])
        xn = sb("xn", [P, 2, CC, D])
        mv = sb("mv", [P, CC, 2])
        stats = sb("stats", [P, CC, 6])
        rstd = sb("rstd", [P, CC])
        xnT = sb("xnT", [P, 2, KD, P])
        sums, factor = sb("sums", [P, RING, LH]), sb("factor", [P, RING, LH])
        half_less = sb("half_less", [P, 1])
        qT, kTl = sb("qT", [P, PAIRS, T]), sb("kT_lat", [P, PAIRS, T])
        kT = sb("kT", [P, PAIRS, CTX])
        qbd = sb("qbd", [P, PAIRS, 2, SEQ])
        mask8, mask = mem.enter_context(nc.sbuf_tensor("mask8", [P, 2, CTX], mybir.dt.uint8)), sb("mask", [P, CTX])
        slat, lmin = sb("slat", [P, PAIRS, SEQ]), sb("lmin", [P, PAIRS])
        scores, probs = sb("scores", [P, 2, CTX]), sb("probs", [P, RING, CTX])
        kn, sq = probs, scores[:, 0, :]
        plat = sb("plat", [P, PAIRS, SEQ])
        top, total, tlat = sb("top", [P, PAIRS]), sb("total", [P, PAIRS]), sb("tlat", [P, PAIRS])
        probsT, platT = sb("probsT", [P, CC, PG, P]), sb("platT", [P, PG * P])
        y = sb("y", [P, 2, KD, HG, SEQ])
        oT = qT
        spare, step = sb("spare", [P, 1]), sb("step", [P, 1])
        ctx_in, mask_in = (ctx_in0, ctx_in1), (mask_in0, mask_in1)
        halves = lambda ap: ap.rearrange("p b n -> p (b n)")
        Y_BANK, O_BANK, L_BANK, T_BANK = 4, 7, 0, 6
        score_banks = lambda p: slice(2, 4) if p % 2 == 0 else slice(0, 2)

        def samples(eng, body):
            body(0, 0, False)
            with eng.Fori(0, BATCH // 2 - 1) as j:
                body(2 * j + 1, 1, False)
                body(2 * j + 2, 0, False)
            body(BATCH - 1, 1, True)

        @block.sync
        def _(sp):
            env.norm.sync(sp)
            sp.dma_start(wq, ins["L1_xattn_Wq"].rearrange("(k p) n -> p k n", p=P)).then_inc(wq_in, 16)
            for dst, src in ((wk, ins["L1_xattn_Wk"].rearrange("(k p) n -> p k n", p=P)),
                             (wv, ins["L1_xattn_Wv"].rearrange("(k p) n -> p k n", p=P)),
                             (lg, rows_of(ins["L1_xattn_ln_l_g"])), (lb, rows_of(ins["L1_xattn_ln_l_b"])),
                             (xg, rows_of(ins["L1_xattn_ln_x_g"])), (xb, rows_of(ins["L1_xattn_ln_x_b"])),
                             (gains, ins["L1_xattn_gains"]), (bout, ins["L1_xattn_bout"].unsqueeze(0))):
                sp.dma_start(dst[:], src).then_inc(consts_in, 16)
            for b in range(BATCH):
                wait(sp, y_done, 4 * (b - 1))
                wait(sp, mask_ready, b - 1)
                sp.dma_start(xn[:, b % 2], ins["ctx"][b].rearrange("(c p) d -> p c d", p=P)).then_inc(ctx_in[b % 2], 16)
                sp.dma_start(mask8[:, b % 2, :], rows_of(ins["mask_ctx"][b])).then_inc(mask_in[b % 2], 16)
                if b == 2:
                    sp.wait_ge(k_done, TT)
                    sp.dma_start(wout, ins["L1_xattn_Wout"].rearrange("(k p) n -> p k n", p=P)).then_inc(wout_in, 16)

        @block.tensor
        def _(pe):
            env.norm.tensor(pe)
            def jobs(n0, count, source, ready, weight, between=None):
                def turn_rows(c):
                    wait(pe, ready, c + 1 if isinstance(n0, int) and n0 < FIRST else n0 - FIRST + c + 1)
                    wait(pe, xnT_ready, n0 + c)
                    for k in range(KD):
                        last = nc.tensor.transpose(ps[:, T_BANK, k * P:(k + 1) * P], source(c)[:, k * P:(k + 1) * P],
                                                   env.ident[:])
                    last.then_inc(rows_turned, 1)

                def product(c):
                    wait(pe, xnT_ready, n0 + c + 1)
                    wait(pe, k_taken, n0 + c - 1)
                    for half in range(2):
                        last = project(nc, ps[:, 2 * (c % 2) + half, :], lambda k: xnT[:, c % 2, k, :], KD,
                                       lambda k: weight[:, k, half * BANK:(half + 1) * BANK])
                    last.then_inc(k_done, 1)

                def turn_k(c):
                    wait(pe, kn_ready, n0 + c + 1)
                    wait(pe, kT_a, n0 + c)
                    wait(pe, kT_b, n0 + c)
                    for p in range(PAIRS):
                        last = nc.tensor.transpose(ps[:, Y_BANK + p // PG, (p % PG) * P:(p % PG + 1) * P],
                                                   kn[:, c % RING, p * P:(p + 1) * P], env.ident[:])
                    last.then_inc(kn_turned, 1)

                turn_rows(0)
                for c in range(count + LAG):
                    if c + 1 < count:
                        turn_rows(c + 1)
                    if c < count:
                        product(c)
                    if c >= LAG:
                        turn_k(c - LAG)
                    if between and count <= c < count + 2:
                        between[c - count]()

            def score(b, p):
                wait(pe, max_ready, PAIRS * b + p - 1)
                for half in range(2):
                    last = nc.tensor.matmul(ps[:, score_banks(p).start + half, :], qbd[:, p].rearrange("p h l -> p (h l)"),
                                            kT[:, p, half * BANK:(half + 1) * BANK], start=True, stop=True)
                last.then_inc(scores_done, 1)

            def turn(b, p):
                wait(pe, probs_ready, PAIRS * b + p + 1)
                if p == 0:
                    wait(pe, o_ready, b)
                elif p == PG:
                    wait(pe, latT_ready, 4 * b + 2)
                for half, taken, done in ((0, probsT_a, turned_a), (1, probsT_b, turned_b)):
                    wait(pe, taken, PAIRS * b + p)
                    for c in range(4):
                        last = nc.tensor.transpose(ps[:, T_BANK + half, c * P:(c + 1) * P],
                                                   probs[:, p % RING, (4 * half + c) * P:(4 * half + c + 1) * P],
                                                   env.ident[:])
                    last.then_inc(done, 1)

            def values(b, i, g):
                wait(pe, probsT_a, PAIRS * b + PG * (g + 1))
                wait(pe, probsT_b, PAIRS * b + PG * (g + 1))
                for m in range(PG // 2):
                    last = nc.tensor.transpose(ps[:, T_BANK, m * P:(m + 1) * P],
                                               plat[:, PG * g + 2 * m:PG * g + 2 * m + 2, :].rearrange("p j l -> p (j l)"),
                                               env.ident[:])
                last.then_inc(lat_turned, 1)
                wait(pe, latb_ready, b + 2 - i)
                for k in range(KD):
                    wait(pe, y_taken, 4 * b + 2 * g + k - 1)
                    for c in range(CC):
                        nc.tensor.matmul(ps[:, Y_BANK + k, :], xn[:, i, c, k * P:(k + 1) * P],
                                         probsT[:, c].rearrange("p j q -> p (j q)"), start=(c == 0), stop=False)
                    if k == 0:
                        wait(pe, latT_ready, 4 * b + 2 * g + 2)
                    rows = slice(i * SEQ, (i + 1) * SEQ)
                    nc.tensor.matmul(ps[:, Y_BANK + k, :], latb[rows, k * P:(k + 1) * P], platT[rows, :],
                                     start=False, stop=True).then_inc(y_done, 1)

            def outputs(b, g):
                wait(pe, y_taken, 4 * b + 2 * g + 2)
                for j in range(PG):
                    for k in range(KD):
                        for s in range(2):
                            head = HG * g + 2 * j + s
                            last = nc.tensor.matmul(ps[s * LD:(s + 1) * LD, O_BANK, (PG * g + j) * SEQ:(PG * g + j + 1) * SEQ],
                                                    wv[:, k, head * LD:(head + 1) * LD], y[:, g, k, 2 * j + s, :],
                                                    start=(k == 0), stop=(k == KD - 1))
                last.then_inc(o_done, 1)

            def sample(b, i, last):
                first = isinstance(b, int) and b == 0

                def latent_scores():
                    wait(pe, qbd_ready, b + 1)
                    wait(pe, k_taken, FIRST + JOBS * (b + 1) - 1)
                    for p in range(PAIRS):
                        ins_ = nc.tensor.matmul(ps[:, L_BANK, p * SEQ:(p + 1) * SEQ],
                                                qbd[:, p].rearrange("p h l -> p (h l)"),
                                                kTl[:, p, bass.ds(b * SEQ, SEQ)], start=True, stop=True)
                    ins_.then_inc(slat_done, 1)

                def last_outputs():
                    latent_scores()
                    if not first:
                        outputs(b - 1, 0)

                jobs(FIRST + JOBS * b, JOBS, lambda c: xn[:, i, c, :], xn_ready, wk,
                     (last_outputs, lambda: None if first else outputs(b - 1, 1)))
                wait(pe, kT_a, FIRST + JOBS * (b + 1))
                wait(pe, kT_b, FIRST + JOBS * (b + 1))
                score(b, 0)
                wait(pe, slat_ready, b + 1)
                score(b, 1)
                for p in range(PAIRS + 1):
                    if p >= 1 and p != PG + 1:
                        turn(b, p - 1)
                    if p + 2 < PAIRS:
                        score(b, p + 2)
                    if p == PG + 1:
                        values(b, i, 0)
                        turn(b, p - 1)
                values(b, i, 1)
                if last:
                    outputs(b, 0)
                    outputs(b, 1)

            pe.wait_ge(wq_in, 16)
            jobs(0, TT, lambda c: lat[:, c, :], lat_ready, wq)
            pe.wait_ge(consts_in, 128)
            jobs(TT, TT, lambda c: lat[:, c, :], lat_ready, wk)
            samples(pe, sample)
            pe.wait_ge(o_ready, BATCH)
            pe.wait_ge(wout_in, 16)
            project_out(nc, env, pe, oT, wout, INNER // P, out_done, bout[:])

        @block.scalar
        def _(act):
            env.norm.scalar(act)
            def jobs(n0, count, take):
                def take_rows(c):
                    act.wait_ge(rows_turned, n0 + c + 1)
                    wait(act, k_done, n0 + c - 1)
                    nc.scalar.copy(xnT[:, c % 2].rearrange("p k n -> p (k n)"), ps[:, T_BANK, 0:D])\
                        .then_inc(xnT_ready, 1)

                take_rows(0)
                for c in range(count + LAG):
                    if c + 1 < count:
                        take_rows(c + 1)
                    if c < count:
                        act.wait_ge(k_done, n0 + c + 1)
                        wait(act, kn_turned, n0 + c - RING + 1)
                        nc.scalar.copy(kn[:, c % RING], halves(ps[:, 2 * (c % 2):2 * (c % 2) + 2, :])).then_inc(k_taken, 1)
                        act.wait_ge(k_taken, n0 + c + 1)
                        wait(act, reduced, n0 + c)
                        nc.scalar.activation(sq, kn[:, c % RING], ACT.Square).then_inc(squared, 1)
                    if c >= LAG:
                        act.wait_ge(kn_turned, n0 + c - LAG + 1)
                        take(c - LAG).then_inc(kT_a, 1)

            def turned_keys():
                return ps[:, Y_BANK, :].rearrange("p (j r) -> p j r", j=PG)

            def exponentials(b, p):
                act.wait_ge(max_ready, PAIRS * b + p + 1)
                wait(act, turned_b, PAIRS * b + p - RING + 1)
                nc.scalar.activation(probs[:, p % RING, :], scores[:, p % 2, :], ACT.Exp, bias=top[:, p:p + 1], scale=-1.0,
                                     accum_out=total[:, p:p + 1]).then_inc(exp_done, 1)
                nc.scalar.activation(plat[:, p, :], slat[:, p, :], ACT.Exp, bias=top[:, p:p + 1], scale=-1.0,
                                     accum_out=tlat[:, p:p + 1]).then_inc(exp_done, 1)

            def take_y(b, g):
                act.wait_ge(y_done, 4 * b + 2 * g + 1)
                nc.scalar.copy(y[:, g, 0].rearrange("p h l -> p (h l)"), ps[:, Y_BANK, :]).then_inc(y_taken, 1)

            def sample(b, i, last):
                jobs(FIRST + JOBS * b, JOBS,
                     lambda c: nc.scalar.copy(kT[:, 0:PG, c * P:(c + 1) * P], turned_keys()))
                act.wait_ge(slat_done, b + 1)
                nc.scalar.activation(slat[:], ps[:, L_BANK, :].rearrange("p (j l) -> p j l", j=PAIRS), ACT.Copy,
                                     scale=-1.0).then_inc(slat_ready, 1)
                exponentials(b, 0)
                for p in range(PAIRS + 1):
                    if p + 1 < PAIRS and p != PG + 2:
                        exponentials(b, p + 1)
                    if p == PG + 1:
                        exponentials(b, p + 2)
                        take_y(b, 0)
                    if p >= 1:
                        act.wait_ge(turned_a, PAIRS * b + p)
                        nc.scalar.copy(probsT[:, 0:4, (p - 1) % PG, :],
                                       ps[:, T_BANK, :].rearrange("p (c q) -> p c q", c=4)).then_inc(probsT_a, 1)
                take_y(b, 1)

            act.wait_ge(lat_normed, 1)
            gained = lambda dst: nc.scalar.activation(dst, turned_keys(), ACT.Copy, scale=gains[:, 0:1])
            jobs(0, TT, lambda c: gained(qT[:, 0:PG, c * P:(c + 1) * P]))
            jobs(TT, TT, lambda c: nc.scalar.copy(kTl[:, 0:PG, c * P:(c + 1) * P], turned_keys()))
            samples(act, sample)

        @block.gpsimd
        def _(pool):
            env.norm.gpsimd(pool)
            def power(dst, src, done):
                return nc.gpsimd.tensor_tensor(dst, src, half_less[:].broadcast_to(list(src.shape)), ALU.pow)\
                    .then_inc(done, 1)

            def affine(buf, c, index):
                wait(pool, centred, index + 1)
                nc.gpsimd.tensor_tensor(buf[:, c, :], buf[:, c, :], xg[:], ALU.mult).then_inc(scaled, 1)
                wait(pool, scaled, index + 1)
                nc.gpsimd.tensor_tensor(buf[:, c, :], buf[:, c, :], xb[:], ALU.add).then_inc(xn_ready, 1)

            def factors(n0, count):
                for c in range(count):
                    wait(pool, sums_ready, n0 + c + 1)
                    power(factor[:, c % RING, :], sums[:, c % RING, :], factor_ready)

            def rows(b, i):
                wait(pool, stats_ready, b + 2)
                power(rstd[:], mv[:, :, 1], rstd_ready)
                for c in range(CC):
                    affine(xn[:, i], c, JOBS * b + c)

            nc.gpsimd.memset(half_less[:], -0.5).then_inc(pstep, 1)
            pool.wait_ge(pstep, 1)
            pool.wait_ge(stats_ready, 1)
            power(rstd[:, 0:TT], mv[:, 0:TT, 1], rstd_ready)
            pool.wait_ge(consts_in, 128)
            rows(0, 0)
            factors(0, TT)
            factors(TT, TT)

            def paired(j):
                pool.wait_ge(lat_ready, TT)
                wait(pool, y_done, 8 * j)
                nc.gpsimd.tensor_copy(latb[:], lat[:, j, :] if isinstance(j, int) else
                                      lat[:, bass.ds(j, 1), :].rearrange("p t d -> p (t d)")).then_inc(latb_ready, 2)

            def body(b, i, last):
                factors(FIRST + JOBS * b, JOBS)
                if not last:
                    rows(b + 1, 1 - i)

            paired(0)
            body(0, 0, False)
            with pool.Fori(0, BATCH // 2 - 1) as j:
                body(2 * j + 1, 1, False)
                paired(j + 1)
                body(2 * j + 2, 0, False)
            body(BATCH - 1, 1, True)

        @block.vector
        def _(dve):
            env.norm.vector(dve)
            link = Chain(dve, vstep)

            def jobs(n0, count, take):
                for c in range(count + LAG):
                    if c >= LAG:
                        dve.wait_ge(kn_turned, n0 + c - LAG + 1)
                        take(c - LAG).then_inc(kT_b, 1)
                    if 2 <= c < count + 2:
                        n = n0 + c - 2
                        wait(dve, factor_ready, n + 1)
                        nc.vector.tensor_tensor(
                            kn[:, (c - 2) % RING].rearrange("p (h d) -> p h d", h=LH),
                            kn[:, (c - 2) % RING].rearrange("p (h d) -> p h d", h=LH),
                            factor[:, (c - 2) % RING, :].unsqueeze(2).broadcast_to([P, LH, LD]), ALU.mult)\
                            .then_inc(kn_ready, 1)
                    if c < count:
                        n = n0 + c
                        wait(dve, squared, n + 1)
                        wait(dve, factor_ready, n - RING + 1)
                        nc.vector.tensor_reduce(sums[:, c % RING, :], sq.rearrange("p (h d) -> p h d", h=LH),
                                                AX.X, ALU.add).then_inc(reduced, 1)
                        wait(dve, reduced, n + 1)
                        nc.vector.tensor_scalar(sums[:, c % RING, :], sums[:, c % RING, :], 1.0 / LD, 1e-16, ALU.mult,
                                                ALU.max).then_inc(sums_ready, 1)

            def turned_keys():
                return ps[:, Y_BANK + 1, :].rearrange("p (j r) -> p j r", j=PG)

            def maxima(b, p):
                n = PAIRS * b + p
                dve.wait_ge(scores_done, n + 1)
                wait(dve, exp_done, 2 * (n - 1))
                wait(dve, spare_set, n)
                nc.vector.memset(spare[:], 0.0).then_inc(spare_set, 1)
                nc.vector.tensor_tensor_reduce(
                    out=scores[:, p % 2, :], in0=halves(ps[:, score_banks(p), :]), in1=mask[:], scale=-1.0,
                    scalar=lmin[:, p:p + 1], op0=ALU.add, op1=ALU.min, accum_out=top[:, p:p + 1]).then_inc(max_ready, 1)

            def normalize(b, p):
                n = PAIRS * b + p
                dve.wait_ge(exp_done, 2 * n + 2)
                link(nc.vector.tensor_tensor(total[:, p:p + 1], total[:, p:p + 1], tlat[:, p:p + 1], ALU.add))
                link(nc.vector.reciprocal(total[:, p:p + 1], total[:, p:p + 1]))
                link(nc.vector.tensor_scalar(plat[:, p, :], plat[:, p, :], total[:, p:p + 1], None, ALU.mult))
                nc.vector.tensor_scalar(probs[:, p % RING, :], probs[:, p % RING, :], total[:, p:p + 1], None, ALU.mult)\
                    .then_inc(probs_ready, 1)

            def rows_stats(i):
                for c in range(CC):
                    nc.vector.bn_stats(stats[:, c, :], xn[:, i, c, :]).then_inc(vstep, 1)
                    link.n += 1
                dve.wait_ge(vstep, link.base + link.n)
                nc.vector.memset(step[:], 0.0).then_inc(vstep, 1)
                link.n += 1
                for c in range(CC):
                    nc.vector.bn_aggr(mv[:, c, :], stats[:, c, :]).then_inc(vstep, 1)
                    link.n += 1
                dve.wait_ge(vstep, link.base + link.n)
                nc.vector.tensor_scalar(mv[:, :, 1], mv[:, :, 1], LN_EPS, None, ALU.add).then_inc(stats_ready, 1)

            def centre(i, c):
                nc.vector.tensor_scalar(xn[:, i, c, :], xn[:, i, c, :], mv[:, c, 0:1], rstd[:, c:c + 1],
                                        ALU.subtract, ALU.mult).then_inc(centred, 1)

            def take_y(b, g):
                dve.wait_ge(y_done, 4 * b + 2 * g + 2)
                nc.vector.tensor_copy(y[:, g, 1].rearrange("p h l -> p (h l)"), ps[:, Y_BANK + 1, :]).then_inc(y_taken, 1)

            def take_latents(b, i, g):
                dve.wait_ge(lat_turned, 2 * b + g + 1)
                for s in range(2):
                    nc.vector.tensor_copy(
                        platT[i * SEQ:(i + 1) * SEQ, :].rearrange("p (m s q) -> p m s q", m=PG // 2, s=2)[:, :, s, :],
                        ps[s * SEQ:(s + 1) * SEQ, T_BANK, 0:2 * P].rearrange("p (m q) -> p m q", m=PG // 2))\
                        .then_inc(latT_ready, 1)

            PER_SAMPLE = 3 + 3 * PAIRS + 2 * CC

            def sample(b, i, last):
                link.restart(before + PER_SAMPLE * b)
                wait(dve, qbd_ready, b)
                nc.vector.tensor_tensor(
                    qbd[:], qT[:, :, bass.ds(b * SEQ, SEQ)].unsqueeze(2).broadcast_to([P, PAIRS, 2, SEQ]),
                    env.half_mask[:].unsqueeze(1).unsqueeze(3).broadcast_to([P, PAIRS, 2, SEQ]), ALU.mult)\
                    .then_inc(qbd_ready, 1)
                jobs(FIRST + JOBS * b, JOBS,
                     lambda c: nc.vector.tensor_copy(kT[:, PG:PAIRS, c * P:(c + 1) * P], turned_keys()))
                wait(dve, o_done, 2 * b)
                nc.vector.memset(step[:], 0.0).then_inc(vstep, 1)
                link.n += 1
                if not (isinstance(b, int) and b == 0):
                    take_outputs(b - 1)
                wait(dve, mask_in[i], 16 * (b // 2 + 1) if isinstance(b, int) else 8 * b + 16 - 8 * i)
                nc.vector.tensor_scalar(mask[:], mask8[:, i, :], -1.0, 1e30, ALU.add, ALU.mult).then_inc(mask_ready, 1)
                dve.wait_ge(slat_ready, b + 1)
                link(nc.vector.tensor_reduce(lmin[:], slat[:], AX.X, ALU.min))
                wait(dve, mask_ready, b + 1)
                maxima(b, 0)
                for p in range(PAIRS + 1):
                    if p + 1 < PAIRS and p != PG + 2:
                        maxima(b, p + 1)
                    if p < PAIRS and p != PG + 2:
                        normalize(b, p)
                    if p == PG + 1:
                        maxima(b, p + 2)
                        normalize(b, p + 1)
                        take_latents(b, i, 0)
                        take_y(b, 0)
                    if p >= 1:
                        dve.wait_ge(turned_b, PAIRS * b + p)
                        nc.vector.tensor_copy(probsT[:, 4:8, (p - 1) % PG, :],
                                              ps[:, T_BANK + 1, :].rearrange("p (c q) -> p c q", c=4))\
                            .then_inc(probsT_b, 1)
                    if not last:
                        if p == 1:
                            wait(dve, ctx_in[1 - i], 8 * b + 16 + 8 * i)
                            rows_stats(1 - i)
                        if p == 2:
                            dve.wait_ge(rstd_ready, b + 3)
                        if 2 <= p < 6:
                            centre(1 - i, 2 * (p - 2))
                            centre(1 - i, 2 * (p - 2) + 1)
                take_latents(b, i, 1)
                take_y(b, 1)

            def take_outputs(b):
                nc.vector.tensor_copy(oT[:, :, bass.ds(b * SEQ, SEQ)],
                                      ps[:, O_BANK, :].rearrange("p (j l) -> p j l", j=PAIRS)).then_inc(o_ready, 1)

            for t in range(TT):
                link(nc.vector.bn_stats(stats[:, t, :], env.h[:, t, :]))
            for t in range(TT):
                link(nc.vector.bn_aggr(mv[:, t, :], stats[:, t, :]))
            nc.vector.tensor_scalar(mv[:, 0:TT, 1], mv[:, 0:TT, 1], LN_EPS, None, ALU.add).then_inc(stats_ready, 1)
            dve.wait_ge(rstd_ready, 1)
            dve.wait_ge(consts_in, 128)
            for t in range(TT):
                link(nc.vector.tensor_scalar(lat[:, t, :], env.h[:, t, :], mv[:, t, 0:1], rstd[:, t:t + 1],
                                             ALU.subtract, ALU.mult))
                link(nc.vector.tensor_tensor(lat[:, t, :], lat[:, t, :], lg[:], ALU.mult))
                nc.vector.tensor_tensor(lat[:, t, :], lat[:, t, :], lb[:], ALU.add).then_inc(lat_ready, 1)
            link(nc.vector.tensor_tensor(gains[:, 0:1], gains[:, 0:1], gains[:, 1:2], ALU.mult))
            link(nc.vector.tensor_scalar(gains[:, 0:1], gains[:, 0:1], LD ** -0.5, None, ALU.mult))
            nc.vector.engine_nop().then_inc(lat_normed, 1)
            dve.wait_ge(ctx_in0, 16)
            rows_stats(0)
            dve.wait_ge(rstd_ready, 2)
            for c in range(CC):
                centre(0, c)
            jobs(0, TT, lambda c: nc.vector.tensor_scalar(qT[:, PG:PAIRS, c * P:(c + 1) * P], turned_keys(),
                                                          gains[:, 0:1], None, ALU.mult))
            jobs(TT, TT, lambda c: nc.vector.tensor_copy(kTl[:, PG:PAIRS, c * P:(c + 1) * P], turned_keys()))
            dve.wait_ge(kT_a, 2 * TT)
            dve.wait_ge(kT_b, 2 * TT)
            before = link.n
            samples(dve, sample)
            dve.wait_ge(o_done, 2 * BATCH)
            take_outputs(BATCH - 1)
            add_out(nc, env, dve, out_done, x_added)


def gated_latent_attention(nc, env, ins):
    NH, NOPE, HALF = 16, 32, 32
    QK = NOPE + 2 * HALF
    RANK_Q, RANK_KV, VH = 96, 32, 32
    W = NH * NOPE
    KR, GATE = RANK_Q + RANK_KV, RANK_Q + RANK_KV + 2 * HALF
    MISC = GATE + 3
    K1, KS, KW, Q = range(4)
    RING, LAG = 4, 3
    T_BANK, O_BANK = 2, 7
    score_bank = lambda h: (0, 1, 4, 5)[h % RING]
    turn_order = [(a, g) for a in (KS, KW, Q, K1) for g in range(4)]
    with ExitStack() as mem, layer_stage(
            nc, env, mem, "consts_in", "misc_in", "sel_in", "win_in", "lat_in", "zeroed", "hTt_ready", "misc_done", "misc_taken", "squared", "means_ready",
            "rs_ready", "normed", "nT_done", "nT_ready", "gate_sum", "gate_max", "gate_exp", "a_done", "act_took",
            "mults", "roped", "kr_ready", "kr_spread", "heads_turned", "turned_a", "turned_d", "scores_done",
            "max_ready", "exp_done", "factor_ready", "scaled", "turned", "probsT_ready", "pv_done", "o_ready",
            "out_done", "x_added", "vstep") as (
            block, consts_in, misc_in, sel_in, win_in, lat_in, zeroed, hTt_ready, misc_done, misc_taken, squared, means_ready,
            rs_ready, normed, nT_done, nT_ready, gate_sum, gate_max, gate_exp, a_done, act_took,
            mults, roped, kr_ready, kr_spread, heads_turned, turned_a, turned_d, scores_done,
            max_ready, exp_done, factor_ready, scaled, turned, probsT_ready, pv_done, o_ready,
            out_done, x_added, vstep):
        sb = allocator(nc, mem)
        ps = env.ps
        w_misc = sb("w_misc", [P, KD, MISC])
        w_sel, w_win = sb("w_sel", [P, KD, 4 * W]), sb("w_win", [P, KD, 4 * W])
        w_lat = sb("w_lat", [P, 5 * W])
        w_proj = sb("w_proj", [P, 4, D])
        gain, mean64 = sb("gain", [P, 1]), sb("mean64", [P, P])
        masks = sb("masks", [P, 2, P])
        cos, sin = sb("cos", [P, HALF]), sb("sin", [P, HALF])
        hTt = sb("hTt", [P, KD, P])
        misc, squares = sb("misc", [P, MISC]), sb("squares", [P, KR])
        ms, half_less = sb("ms", [P, 2]), sb("half_less", [P, 1])
        nr, nT = sb("nr", [P, P]), sb("nT", [P, P])
        gate, gtop, gtotal = sb("gate", [P, 3]), sb("gtop", [P, 1]), sb("gtotal", [P, 1])
        kt, kr, part = sb("kt", [P, 4, HALF]), sb("kr", [P, 2 * HALF]), sb("part", [P, NH])
        tmp = sb("rope_tmp", [P, 2, 4, W])
        tok, turn = sb("tok", [P, 4, NH, P]), sb("turn", [P, 4, NH, P])
        v = sb("v", [P, 3, W])
        neg, probs = sb("neg", [P, RING, 3, P]), sb("probs", [P, RING, 3, P])
        top, total, factor = sb("top", [P, RING, 3]), sb("total", [P, RING, 3]), sb("factor", [P, RING, 3])
        probsT = sb("probsT", [P, 2, 3, P])
        oT = sb("oT", [P, 4, T])
        step = sb("step", [P, 2])
        by_head = lambda ap: ap.rearrange("p (h d) -> p h d", h=NH)

        def tiles(eng, body):
            body(0)
            with eng.Fori(1, TT) as t:
                body(t)

        @block.sync
        def _(sp):
            env.norm.sync(sp)
            sp.dma_start(w_misc[:], ins["L3_attn_misc"].rearrange("(k p) n -> p k n", p=P)).then_inc(misc_in, 16)
            sp.dma_start(w_sel[:], ins["L3_attn_sel"].rearrange("(k p) n -> p k n", p=P)).then_inc(sel_in, 16)
            for dst, src in ((gain, ins["L3_attn_gain"].unsqueeze(1)), (mean64, env.consts["mean64"]),
                             (masks, env.consts["masks"]), (cos, env.consts["cos64"]), (sin, env.consts["sin64"])):
                sp.dma_start(dst[:], src).then_inc(consts_in, 16)
            sp.dma_start(w_win[:], ins["L3_attn_win"].rearrange("(k p) n -> p k n", p=P)).then_inc(win_in, 16)
            sp.dma_start(w_lat[:], ins["L3_attn_lat"]).then_inc(lat_in, 16)
            sp.dma_start(w_proj[:], ins["L3_attn_w_proj"].rearrange("(k p) n -> p k n", p=P)).then_inc(lat_in, 16)

        @block.tensor
        def _(pe):
            env.norm.tensor(pe)
            def wide(bank, weight, part):
                project(nc, ps[:, bank, :], lambda k: hTt[:, k, :], KD,
                        lambda k: weight[:, k, part * W:(part + 1) * W]).then_inc(a_done, 1)

            def low(bank, part):
                nc.tensor.matmul(ps[:, bank, :], nT[:], w_lat[:, part * W:(part + 1) * W], start=True, stop=True)\
                    .then_inc(a_done, 1)

            def tile(t):
                wait(pe, o_ready, t)
                pe.wait_ge(hTt_ready, t + 1)
                project(nc, ps[:, 0, 0:MISC], lambda k: hTt[:, k, :], KD, lambda k: w_misc[:, k, :]).then_inc(misc_done, 1)
                if isinstance(t, int):
                    pe.wait_ge(sel_in, 16)
                for part in range(4):
                    wide(1 + part, w_sel, part)
                pe.wait_ge(misc_taken, t + 1)
                if isinstance(t, int):
                    pe.wait_ge(consts_in, 80)
                nc.tensor.matmul(ps[:, 0, 0:3], mean64[:], misc[:, GATE:MISC], start=True, stop=True).then_inc(gate_sum, 1)
                if isinstance(t, int):
                    pe.wait_ge(win_in, 16)
                for part in range(3):
                    wide(5 + part, w_win, part)
                pe.wait_ge(act_took, 7 * t + 1)
                wide(1, w_win, 3)
                pe.wait_ge(normed, 2 * t + 2)
                pe.wait_ge(gate_max, t + 1)
                nc.tensor.transpose(ps[:, 0, 0:P], nr[:], env.ident[:]).then_inc(nT_done, 1)
                pe.wait_ge(nT_ready, t + 1)
                pe.wait_ge(act_took, 7 * t + 2)
                if isinstance(t, int):
                    pe.wait_ge(lat_in, 32)
                low(4, 0)
                pe.wait_ge(mults, 12 * t + 4)
                low(2, 1)
                low(3, 2)
                pe.wait_ge(act_took, 7 * t + 4)
                low(5, 3)
                low(1, 4)
                pe.wait_ge(mults, 12 * t + 8)
                for m, (a, g) in enumerate(turn_order):
                    if g == 0:
                        pe.wait_ge(*((kr_spread, t + 1) if a == K1 else
                                     (roped, 6 * t + 2 * {KS: 1, KW: 2, Q: 3}[a])))
                        pe.wait_ge(act_took, 7 * t + 7)
                    if m >= 4:
                        done = turned_d if m % 2 else turned_a
                        pe.wait_ge(done, 8 * t + m // 2 - 1)
                    for j in range(4):
                        last = nc.tensor.transpose(ps[:, (6, 7, 0, 1)[m % 4], j * P:(j + 1) * P], tok[:, a, 4 * g + j, :],
                                                   env.ident[:])
                    last.then_inc(heads_turned, 1)
                pe.wait_ge(turned_a, 8 * t + 8)
                pe.wait_ge(turned_d, 8 * t + 8)
                pe.wait_ge(mults, 12 * t + 12)
                for m in range(NH + LAG + 1):
                    n = NH * t + m
                    if m < NH:
                        if m >= RING:
                            wait(pe, max_ready, 3 * (n - RING + 1))
                        for a in range(3):
                            last = nc.tensor.matmul(ps[:, score_bank(m), a * P:(a + 1) * P], turn[:, Q, m, :],
                                                    turn[:, a, m, :], start=True, stop=True)
                        last.then_inc(scores_done, 1)
                    if LAG <= m < NH + LAG:
                        h = m - LAG
                        wait(pe, scaled, n - LAG + 1)
                        wait(pe, probsT_ready, n - LAG - 1)
                        for a in range(3):
                            last = nc.tensor.transpose(ps[:, T_BANK + h % 2, a * P:(a + 1) * P], probs[:, h % RING, a, :],
                                                       env.ident[:])
                        last.then_inc(turned, 1)
                    if m > LAG:
                        h = m - LAG - 1
                        wait(pe, probsT_ready, n - LAG)
                        for a in range(3):
                            last = nc.tensor.matmul(ps[32 * (h % 4):32 * (h % 4) + 32, O_BANK, (h // 4) * P:(h // 4 + 1) * P],
                                                    v[:, a, h * VH:(h + 1) * VH], probsT[:, h % 2, a, :],
                                                    start=(a == 0), stop=(a == 2))
                        last.then_inc(pv_done, 1)

            pe.wait_ge(misc_in, 16)
            tiles(pe, tile)
            pe.wait_ge(o_ready, TT)
            project_out(nc, env, pe, oT, w_proj, 4, out_done)

        @block.scalar
        def _(act):
            env.norm.scalar(act)
            def tile(t):
                act.wait_ge(misc_taken, t + 1)
                nc.scalar.activation(squares[:, 0:RANK_Q], misc[:, 0:RANK_Q], ACT.Square, accum_out=ms[:, 0:1])\
                    .then_inc(squared, 1)
                nc.scalar.activation(squares[:, RANK_Q:KR], misc[:, RANK_Q:KR], ACT.Square, accum_out=ms[:, 1:2])\
                    .then_inc(squared, 1)

                def take(unit, bank, dst):
                    act.wait_ge(a_done, 13 * t + unit)
                    nc.scalar.copy(dst, by_head(ps[:, bank, :])).then_inc(act_took, 1)

                nope = lambda a: tok[:, a, :, 0:NOPE]
                value = lambda a: by_head(v[:, a, :])
                take(1, 1, nope(KS))
                take(4, 4, value(KS))
                act.wait_ge(gate_max, t + 1)
                nc.scalar.activation(gate[:], gate[:], ACT.Exp, bias=gtop[:], accum_out=gtotal[:]).then_inc(gate_exp, 1)
                take(5, 5, nope(KW))
                take(8, 1, value(KW))
                act.wait_ge(nT_done, t + 1)
                nc.scalar.activation(nT[:], ps[:, 0, 0:P], ACT.Copy, scale=gain[:]).then_inc(nT_ready, 1)
                take(9, 4, nope(Q))
                take(12, 5, nope(K1))
                take(13, 1, value(K1))
                for m, (a, g) in enumerate(turn_order):
                    if m % 2 == 0:
                        act.wait_ge(heads_turned, 16 * t + m + 1)
                        nc.scalar.copy(turn[:, a, 4 * g:4 * g + 4, :].rearrange("p h n -> p (h n)"),
                                       ps[:, (6, 7, 0, 1)[m % 4], :]).then_inc(turned_a, 1)
                for m in range(NH + LAG):
                    n = NH * t + m
                    if m < NH:
                        wait(act, turned, n - RING + 1)
                        for a in range(3):
                            act.wait_ge(max_ready, 3 * n + a + 1)
                            nc.scalar.activation(probs[:, m % RING, a, :], neg[:, m % RING, a, :], ACT.Exp,
                                                 bias=top[:, m % RING, a:a + 1], scale=-1.0,
                                                 accum_out=total[:, m % RING, a:a + 1]).then_inc(exp_done, 1)
                    if m >= LAG:
                        h = m - LAG
                        wait(act, turned, n - LAG + 1)
                        wait(act, pv_done, n - LAG - 1)
                        nc.scalar.copy(probsT[:, h % 2].rearrange("p a n -> p (a n)"), ps[:, T_BANK + h % 2, 0:3 * P])\
                            .then_inc(probsT_ready, 1)

            act.wait_ge(zeroed, 3)
            tiles(act, tile)

        @block.gpsimd
        def _(pool):
            env.norm.gpsimd(pool)
            nc.gpsimd.memset(half_less[:], -0.5).then_inc(zeroed, 1)
            nc.gpsimd.memset(part[:], 1.0 / NH).then_inc(zeroed, 1)

            def rope(t, i, a):
                pool.wait_ge(mults, 12 * t + 4 * (i + 1))
                nc.gpsimd.tensor_tensor(tok[:, a, :, NOPE:NOPE + HALF], by_head(tmp[:, i % 2, 0]),
                                        by_head(tmp[:, i % 2, 1]), ALU.subtract).then_inc(roped, 1)
                nc.gpsimd.tensor_tensor(tok[:, a, :, NOPE + HALF:QK], by_head(tmp[:, i % 2, 2]),
                                        by_head(tmp[:, i % 2, 3]), ALU.add).then_inc(roped, 1)

            def tile(t):
                pool.wait_ge(means_ready, 2 * t + 2)
                nc.gpsimd.tensor_tensor(ms[:], ms[:], half_less[:].broadcast_to([P, 2]), ALU.pow).then_inc(rs_ready, 1)
                rope(t, 0, KS)
                pool.wait_ge(kr_ready, t + 1)
                nc.gpsimd.tensor_tensor(tok[:, K1, :, NOPE:QK], kr[:].unsqueeze(1).broadcast_to([P, NH, 2 * HALF]),
                                        part[:].unsqueeze(2).broadcast_to([P, NH, 2 * HALF]), ALU.mult)\
                    .then_inc(kr_spread, 1)
                rope(t, 1, KW)
                rope(t, 2, Q)
                for m in range(NH):
                    n = NH * t + m
                    pool.wait_ge(factor_ready, n + 1)
                    nc.gpsimd.tensor_tensor(probs[:, m % RING], probs[:, m % RING],
                                            factor[:, m % RING, :].unsqueeze(2).broadcast_to([P, 3, P]), ALU.mult)\
                        .then_inc(scaled, 1)

            pool.wait_ge(zeroed, 3)
            tiles(pool, tile)

        @block.vector
        def _(dve):
            env.norm.vector(dve)
            link = Chain(dve, vstep)
            PER_TILE = 6 + 2 + NH * 2 + 1

            def carry(i):
                nc.vector.memset(step[:, i:i + 1], 0.0).then_inc(vstep, 1)
                link.n += 1

            def rope(t, i, unit, b1, b2):
                dve.wait_ge(a_done, 13 * t + unit)
                if i == 2:
                    dve.wait_ge(roped, 6 * t + 2)
                for n, (bank, table) in enumerate(((b1, cos), (b2, sin), (b1, sin), (b2, cos))):
                    nc.vector.tensor_tensor(by_head(tmp[:, i % 2, n]), by_head(ps[:, bank, :]),
                                            table[:].unsqueeze(1).broadcast_to([P, NH, HALF]), ALU.mult)\
                        .then_inc(mults, 1)

            def tile(t):
                link.restart(before + PER_TILE * t)
                nc.vector.tensor_copy(hTt[:], env.hT[:, :, bass.ds(t * P, P)]).then_inc(hTt_ready, 1)
                dve.wait_ge(misc_done, t + 1)
                nc.vector.tensor_copy(misc[:], ps[:, 0, 0:MISC]).then_inc(misc_taken, 1)
                for i, rank in ((0, RANK_Q), (1, RANK_KV)):
                    dve.wait_ge(squared, 2 * t + i + 1)
                    nc.vector.tensor_scalar(ms[:, i:i + 1], ms[:, i:i + 1], 1.0 / rank, 1e-6, ALU.mult, ALU.add)\
                        .then_inc(means_ready, 1)
                rope(t, 0, 3, 2, 3)
                dve.wait_ge(rs_ready, t + 1)
                for i, cols in ((0, slice(0, RANK_Q)), (1, slice(RANK_Q, KR))):
                    nc.vector.tensor_scalar(nr[:, cols], misc[:, cols], ms[:, i:i + 1], None, ALU.mult)\
                        .then_inc(normed, 1)
                dve.wait_ge(gate_sum, t + 1)
                link(nc.vector.tensor_copy(gate[:], ps[:, 0, 0:3]))
                nc.vector.tensor_reduce(gtop[:], gate[:], AX.X, ALU.max, negate=True).then_inc(gate_max, 1)
                for n, (x, table) in enumerate(((0, cos), (1, sin), (0, sin), (1, cos))):
                    nc.vector.tensor_tensor(kt[:, n], misc[:, KR + x * HALF:KR + (x + 1) * HALF], table[:], ALU.mult)\
                        .then_inc(vstep, 1)
                    link.n += 1
                dve.wait_ge(vstep, link.base + link.n)
                nc.vector.tensor_tensor(kr[:, 0:HALF], kt[:, 0], kt[:, 1], ALU.subtract).then_inc(vstep, 1)
                link.n += 1
                nc.vector.tensor_tensor(kr[:, HALF:], kt[:, 2], kt[:, 3], ALU.add).then_inc(kr_ready, 1)
                dve.wait_ge(gate_exp, t + 1)
                link(nc.vector.reciprocal(gtotal[:], gtotal[:]))
                link(nc.vector.tensor_scalar(gate[:], gate[:], gtotal[:], None, ALU.mult))
                rope(t, 1, 7, 6, 7)
                rope(t, 2, 11, 2, 3)
                for m, (a, g) in enumerate(turn_order):
                    if m % 2 == 1:
                        dve.wait_ge(heads_turned, 16 * t + m + 1)
                        nc.vector.tensor_copy(turn[:, a, 4 * g:4 * g + 4, :].rearrange("p h n -> p (h n)"),
                                              ps[:, (6, 7, 0, 1)[m % 4], :]).then_inc(turned_d, 1)
                for m in range(NH + 1):
                    n = NH * t + m
                    if m < NH:
                        dve.wait_ge(scores_done, n + 1)
                        wait(dve, exp_done, 3 * (n - RING + 1))
                        carry(m % 2)
                        for a in range(3):
                            nc.vector.tensor_tensor_reduce(
                                out=neg[:, m % RING, a, :], in0=ps[:, score_bank(m), a * P:(a + 1) * P],
                                in1=masks[:, a % 2, :], scale=-1.0, scalar=3e38, op0=ALU.add, op1=ALU.min,
                                accum_out=top[:, m % RING, a:a + 1]).then_inc(max_ready, 1)
                    if m >= 1:
                        i = (m - 1) % RING
                        dve.wait_ge(exp_done, 3 * n)
                        link(nc.vector.reciprocal(total[:, i], total[:, i]))
                        nc.vector.tensor_tensor(factor[:, i], total[:, i], gate[:], ALU.mult).then_inc(factor_ready, 1)
                dve.wait_ge(pv_done, NH * (t + 1))
                carry(0)
                nc.vector.tensor_copy(oT[:, :, bass.ds(t * P, P)], ps[:, O_BANK, :].rearrange("p (g n) -> p g n", g=4))\
                    .then_inc(o_ready, 1)

            dve.wait_ge(consts_in, 80)
            link(nc.vector.tensor_scalar(gain[0:RANK_Q], gain[0:RANK_Q], QK ** -0.5, None, ALU.mult))
            nc.vector.memset(tok[:].rearrange("p a h n -> p (a h) n")[:, :, QK:], 0.0).then_inc(zeroed, 1)
            before = link.n
            tiles(dve, tile)
            add_out(nc, env, dve, out_done, x_added)


def build(nc, ins, consts, out):
    env = Env()
    nc.stage_sem_base = min(nc.free_semaphores)
    with ExitStack() as mem:
        sb = lambda name, shape: mem.enter_context(nc.sbuf_tensor(name, shape, F32))
        env.ps = mem.enter_context(nc.psum_tensor("psum", [P, 8, BANK], F32))
        env.x, env.h, env.hT = sb("x", [P, TT, D]), sb("h", [P, TT, D]), sb("hT", [P, KD, T])
        env.ident, env.head_mask = sb("ident", [P, P]), sb("head_mask", [P, HG])
        env.pair_mask, env.same_sample = sb("pair_mask", [P, 2]), sb("same_sample", [P, P])
        env.half_mask = sb("half_mask", [P, 2])
        env.consts = consts
        env.eps, env.ones, env.half_less = sb("eps", [P, 4]), sb("ones", [P, BANK]), sb("half_less", [P, 1])

        with stage(nc, "loaded", "filled") as (block, loaded, filled):
            @block.sync
            def _(sp):
                sp.dma_start(env.x[:], ins["x"].rearrange("(t p) d -> p t d", p=P)).then_inc(loaded, 16)
                sp.dma_start(env.ident[:], consts["ident"]).then_inc(loaded, 16)
                sp.dma_start(env.head_mask[:], consts["head_mask"]).then_inc(loaded, 16)
                sp.dma_start(env.pair_mask[:], consts["pair_mask"]).then_inc(loaded, 16)
                sp.dma_start(env.same_sample[:], consts["same_sample"]).then_inc(loaded, 16)
                sp.dma_start(env.half_mask[:], consts["half_mask"]).then_inc(loaded, 16)
                sp.wait_ge(loaded, 96)

            @block.vector
            def _(dve):
                for i, e in enumerate((1e-5, 1e-6, 1.0, 0.0)):
                    nc.vector.memset(env.eps[:, i:i + 1], e).then_inc(filled, 1)
                nc.vector.memset(env.ones[:], 1.0).then_inc(filled, 1)
                nc.vector.memset(env.half_less[:], -0.5).then_inc(filled, 1)
                dve.wait_ge(filled, 6)

        for n in ONLY:
            env.positions = ins["L1_attn_pe"] if n == 4 else None
            LAYERS[n](nc, env, ins)

        with stage(nc, "stored") as (block, stored):
            @block.sync
            def _(sp):
                sp.dma_start(out.rearrange("(t p) d -> p t d", p=P), env.x[:]).then_inc(stored, 16)
                sp.wait_ge(stored, 16)


LAYERS = {
    0: lambda nc, env, ins: sigmoid_cross_attention(
        nc, env, {n: ins["L0_xattn_" + n] for n in ("WqT", "WkT", "WvT", "WoT")}, ins["ctxT"]),
    1: selective_scan,
    2: moe_top2,
    3: latent_cross_attention,
    4: self_attention,
    6: context_fusion,
    7: rotary_attention,
    9: softmax_cross_attention,
    5: ternary_mlp,
    8: binary_mlp,
    10: gated_latent_attention,
    11: grouped_moe,
}


def constants():
    p = np.arange(P)
    same = p[:, None] // SEQ == p[None, :] // SEQ
    theta = np.power(np.float32(10000.0), np.float32(-2.0) * (np.arange(D // 2, dtype=np.float32) - 1) / D)
    angle = (theta[:, None] * np.arange(SEQ, dtype=np.float32)[None, :]).astype(np.float32)
    freq = (1.0 / np.float32(10000.0) ** (np.arange(0, 64, 2, dtype=np.float32) / np.float32(64))).astype(np.float32)
    angle64 = np.outer((p % SEQ).astype(np.float32), freq).astype(np.float32)
    causal = same & (p[None, :] <= p[:, None])
    return {
        "cos64": np.cos(angle64), "sin64": np.sin(angle64), "mean64": same.astype(np.float32) / SEQ,
        "masks": np.where(np.stack([causal, same], axis=1), 0, -1e30).astype(np.float32),
        "pair_mask": (p[:, None] % 32 // HD == np.arange(2)[None, :]).astype(np.float32),
        "half_mask": (p[:, None] // SEQ == np.arange(2)[None, :]).astype(np.float32),
        "same": same.astype(np.float32),
        "same_sample": np.where(same, 0, -1e30).astype(np.float32),
        "cos256": np.cos(angle), "sin256": np.sin(angle),
        "pick": np.eye(P, dtype=np.float32)[:, 16:48],
        "ident": np.eye(P, dtype=np.float32),
        "head_mask": (p[:, None] // HD == np.arange(HG)[None, :]).astype(np.float32),
    }


def layout(inputs):
    a = {k: np.asarray(v) for k, v in inputs.items()}
    ctx = a["ctx_1024"]
    out = {"x": a["x"].reshape(T, D), "ctx": ctx, "ctxT": ctx.transpose(0, 2, 1)}
    for n in ("Wq", "Wk", "Wv", "Wo"):
        out[f"L0_xattn_{n}T"] = a[f"L0_xattn_{n}"].T
    for n in ("wq", "wk", "wv", "wo"):
        out[f"L3_xattn_{n}"] = a[f"L3_xattn_{n}"]
    out["mask"] = a["mask_1x1xSxS2_ff0"][0, 0]
    w_kv = a["L1_xattn_Wkv"]
    out["L1_xattn_Wk"], out["L1_xattn_Wv"] = w_kv[:, :D * 4], w_kv[:, D * 4:]
    for n in ("Wq", "Wout", "bout", "ln_x_g", "ln_x_b", "ln_l_g", "ln_l_b"):
        out[f"L1_xattn_{n}"] = a[f"L1_xattn_{n}"]
    out["L1_xattn_gains"] = np.stack([np.tile(a[f"L1_xattn_{n}"], 2) for n in ("qn_g", "kn_g")], axis=1)
    out["mask_ctx"] = a["mask_BxS2_bf1"].view(np.uint8)
    out["L1_attn_pe"] = a["L1_attn_pe"][0, :SEQ]
    for n in ("wq", "wk", "wv", "wo", "bv", "bo", "gamma", "beta"):
        out[f"L1_attn_{n}"] = a[f"L1_attn_{n}"]
    for n in ("bq", "bk"):
        out[f"L1_attn_{n}"] = a[f"L1_attn_{n}"].reshape(KD, P).T
    for n in ("W_in", "W_x", "W_dt", "W_out"):
        out[f"L0_attn_{n}T"] = a[f"L0_attn_{n}"].T
    for n in ("b_x", "b_out", "A_log"):
        out[f"L0_attn_{n}"] = a[f"L0_attn_{n}"]
    for n in ("b_in", "b_dt", "D"):
        out[f"L0_attn_{n}"] = a[f"L0_attn_{n}"].reshape(-1, P).T
    w_sim = a["L2_xattn_w_sim"].reshape(3, D)
    out["L2_xattn_w1"] = w_sim[0]
    out["L2_xattn_w23"] = w_sim[1:].reshape(2, KD, P).transpose(2, 0, 1)
    for n in ("b_sim", "W_qv", "b_qv"):
        out[f"L2_xattn_{n}"] = a[f"L2_xattn_{n}"]
    for n in ("wq", "wk"):
        out[f"L2_attn_{n}T"] = a[f"L2_attn_{n}"].reshape(D // 2, 2, D).transpose(2, 1, 0).reshape(D, D)
    out["L2_attn_wvT"] = a["L2_attn_wv"].T
    columns = lambda v: v.reshape(v.shape[:-1] + (-1, P))
    for n in ("W1", "W2", "b2", "gate_W", "shared_W", "shared_b", "gamma", "beta"):
        out[f"L0_ffn_{n}"] = a[f"L0_ffn_{n}"]
    out["L0_ffn_b1"] = columns(a["L0_ffn_b1"]).transpose(2, 0, 1)
    blocks = lambda w: w.reshape(w.shape[0] // P, P, -1, P).transpose(0, 3, 2, 1)
    for n in ("w1", "w2", "h1", "h2"):
        out[f"L1_ffn_{n}"] = blocks(a[f"L1_ffn_{n}_w"])
    out["L1_ffn_w3T"] = a["L1_ffn_w3_w"].T
    out["L1_ffn_w3_s"] = a["L1_ffn_w3_s"]
    out["L1_ffn_scales"] = np.stack([columns(a[f"L1_ffn_{n}_s"]) for n in ("w1", "w2", "h1", "h2")]).transpose(2, 0, 1)
    for n in ("w1", "w2", "b2"):
        out[f"L2_ffn_{n}"] = a[f"L2_ffn_{n}"]
    out["L2_ffn_b1"] = columns(a["L2_ffn_b1"]).T
    out["L3_ffn_gate_wT"] = a["L3_ffn_gate_w"].T
    out["L3_ffn_gate_bias"] = a["L3_ffn_gate_bias"]
    with_shared = [np.concatenate([a[f"L3_ffn_expert_{n}"], a[f"L3_ffn_shared_{n}"].reshape(2, P, D)])
                   for n in ("gate", "up")]
    out["L3_ffn_gate_up"] = np.stack(with_shared, axis=1).reshape(34, 2, P, KD, P).transpose(0, 4, 3, 1, 2)\
        .reshape(34, P, 2 * D)
    shared = a["L3_ffn_shared_down"].T.reshape(2, P, D)
    out["L3_ffn_downT"] = np.concatenate([a["L3_ffn_expert_down"].transpose(0, 2, 1), shared])
    g = lambda n: a["L3_attn_" + n]
    out["L3_attn_misc"] = np.concatenate([g("w_cq"), g("w_ckv"), g("w_krope"), g("w_gate")], axis=1)
    out["L3_attn_gain"] = np.concatenate([g("g_qnorm"), g("g_kvnorm")])
    parts = lambda w: w.reshape(w.shape[0], 16, 3, 32).transpose(0, 2, 1, 3).reshape(w.shape[0], -1)
    out["L3_attn_sel"] = np.concatenate([parts(g("w_selk")), g("w_selv")], axis=1)
    out["L3_attn_win"] = np.concatenate([parts(g("w_wink")), g("w_winv")], axis=1)
    halves = g("w_dq_rope").reshape(96, 16, 2, 32).transpose(0, 2, 1, 3).reshape(96, -1)
    lat = np.zeros((P, 5 * 512), np.float32)
    lat[:96, :1536] = np.concatenate([g("w_dq_nope"), halves], axis=1)
    lat[96:, 1536:] = np.concatenate([g("w_dk_nope"), g("w_dv")], axis=1)
    out["L3_attn_lat"] = lat
    out["L3_attn_w_proj"] = g("w_proj")
    return {k: np.ascontiguousarray(v) for k, v in out.items()}


def kernel(**inputs):
    import concourse.bacc as bacc
    from concourse.bass_utils import run_bass_kernel_spmd

    nc = bacc.Bacc("TRN2", target_bir_lowering=False, num_devices=1)
    arrays, aps = {}, ({}, {})
    for which, group in enumerate((layout(inputs), constants())):
        for name, a in group.items():
            full = f"in_{name}_dram"
            arrays[full] = a
            aps[which][name] = nc.dram_tensor(full, a.shape, mybir.dt.from_np(a.dtype), kind="ExternalInput").ap()
    out = nc.dram_tensor("out_0_dram", (T, D), F32, kind="ExternalOutput").ap()
    build(nc, aps[0], aps[1], out)
    r = run_bass_kernel_spmd(nc, [arrays], core_ids=[0])
    return r.results[0]["out_0_dram"].reshape(BATCH, SEQ, D)
```
